# Optimizing a Trainium2 kernel written in Bass

```python
import numpy as np
import jax
import jax.numpy as jnp

def _softmax(x, axis=-1):
    return jax.nn.softmax(x, axis=axis)

def _gelu(x):
    return jax.nn.gelu(x, approximate=True)

def _silu(x):
    return jax.nn.silu(x)

def _sigmoid(x):
    return jax.nn.sigmoid(x)

def _layernorm(x, axis=-1, eps=1e-05):
    m = jnp.mean(x, axis=axis, keepdims=True)
    v = jnp.var(x, axis=axis, keepdims=True)
    return (x - m) / jnp.sqrt(v + eps)

def _scatter_add(tgt, idx, src, axis=0):
    return tgt.at[idx].add(src)

def _segment_sum(src, seg, n):
    return jax.ops.segment_sum(src, seg, n)
kernel_name = 'mk_cond_resid_d2_seqx_r8_d8186f'

def setup_inputs(seed: int=0):
    np.random.seed(seed)
    _w = jnp.asarray

    def _rec_inputs():
        import jax
        import jax.numpy as jnp
        _rk = jax.random.key(seed)
        x = -0.000125 + 0.9999 * jax.random.normal(jax.random.fold_in(_rk, 1), (32, 128, 128), jnp.float32)
        _lenS = 128 - jax.random.randint(jax.random.fold_in(_rk, 7), (32,), 0, max(1, 128 // 4) + 1, jnp.int32)
        _lenS2 = 128 - jax.random.randint(jax.random.fold_in(_rk, 8), (32,), 0, max(1, 128 // 4) + 1, jnp.int32)
        cond_1024 = -0.00493535 + 1.00056 * jax.random.normal(jax.random.fold_in(_rk, 11), (32, 128), jnp.float32)
        return (x, cond_1024)
    x, cond_1024 = _rec_inputs()

    def _L0_cond_setup():
        import jax, jax.numpy as jnp
        import numpy as np
        import math
        N, T, D, H = (64, 64, 128, 128)
        key = jax.random.key(seed)
        k1, k2, k3, k4 = jax.random.split(key, 4)
        x = jax.random.normal(k1, (N, T, D), dtype=jnp.float32)
        h0 = jax.random.normal(k2, (N, H), dtype=jnp.float32)
        Wx = jax.random.normal(k3, (D, H), dtype=jnp.float32) / math.sqrt(D)
        Wh = jax.random.normal(k4, (H, H), dtype=jnp.float32) / math.sqrt(H)
        b = jnp.zeros((H,), dtype=jnp.float32)
        return {'x': x, 'h0': h0, 'Wx': Wx, 'Wh': Wh, 'b': b}
    _L0_cond_all = _L0_cond_setup()
    _L0_cond_in = {k: v for k, v in _L0_cond_all.items() if k in ('Wx', 'Wh', 'b')}
    del _L0_cond_all

    def _L1_cond_setup():
        import math
        import jax, jax.numpy as jnp
        import numpy as np
        EPS = 1e-07
        MAX_TANH_ARG = 1.0 - 1e-05

        def _norm(x):
            return jnp.sqrt(jnp.sum(x * x, axis=-1, keepdims=True)).clip(EPS)

        def logmap0(x):
            n = _norm(x)
            return jnp.arctanh(jnp.clip(n, EPS, MAX_TANH_ARG)) * x / n

        def expmap0(v):
            n = _norm(v)
            return jnp.tanh(n) * v / n

        def mobius_add(x, y):
            x2 = jnp.sum(x * x, -1, keepdims=True)
            y2 = jnp.sum(y * y, -1, keepdims=True)
            xy = jnp.sum(x * y, -1, keepdims=True)
            num = (1 + 2 * xy + y2) * x + (1 - x2) * y
            den = (1 + 2 * xy + x2 * y2).clip(EPS)
            return num / den

        def plin(x, w, b):
            return expmap0(logmap0(x) @ w + b)

        def layer_norm(x, eps=1e-06):
            m = x.mean(-1, keepdims=True)
            v = ((x - m) ** 2).mean(-1, keepdims=True)
            return (x - m) / jnp.sqrt(v + eps)

        def _beta(a, b):
            return math.exp(math.lgamma(a) + math.lgamma(b) - math.lgamma(a + b))
        D, H, FF = (128, 16, 512)
        HD = D // H
        BETA_N = _beta(D / 2, 0.5)
        BETA_H = _beta(HD / 2, 0.5)

        def _to_heads(p):
            B, S, _ = p.shape
            t = logmap0(p).reshape(B, S, H, HD) * (BETA_H / BETA_N)
            return expmap0(jnp.transpose(t, (0, 2, 1, 3)))

        def _from_heads(ph):
            B, _, S, _ = ph.shape
            t = logmap0(ph) * (BETA_N / BETA_H)
            t = jnp.transpose(t, (0, 2, 1, 3)).reshape(B, S, D)
            return expmap0(t)
        key = jax.random.key(seed)
        ks = jax.random.split(key, 20)
        B, S = (4, 128)
        x = expmap0(0.02 * jax.random.normal(ks[0], (B, S, D), jnp.float32))
        t_emb = jax.random.normal(ks[1], (B, 1, D), jnp.float32)
        g = lambda k, sh: 0.02 * jax.random.normal(k, sh, jnp.float32)
        return {'x': x, 't_emb': t_emb, 'w_q': g(ks[2], (D, D)), 'b_q': jnp.zeros((D,), jnp.float32), 'w_k': g(ks[3], (D, D)), 'b_k': jnp.zeros((D,), jnp.float32), 'w_v': g(ks[4], (D, D)), 'b_v': jnp.zeros((D,), jnp.float32), 'w_o': g(ks[5], (D, D)), 'b_o': jnp.zeros((D,), jnp.float32), 'w_f1': g(ks[6], (D, FF)), 'b_f1': jnp.zeros((FF,), jnp.float32), 'w_f2': g(ks[7], (FF, D)), 'b_f2': jnp.zeros((D,), jnp.float32), 'w_ada': g(ks[8], (D, 6 * D)), 'b_ada': jnp.zeros((6 * D,), jnp.float32)}
    _L1_cond_all = _L1_cond_setup()
    _L1_cond_in = {k: v for k, v in _L1_cond_all.items() if k in ('w_q', 'b_q', 'w_k', 'b_k', 'w_v', 'b_v', 'w_o', 'b_o', 'w_f1', 'b_f1', 'w_f2', 'b_f2', 'w_ada', 'b_ada')}
    del _L1_cond_all
    return {'x': x, 'cond_1024': cond_1024, 'L0_cond_Wx': _L0_cond_in['Wx'], 'L0_cond_Wh': _L0_cond_in['Wh'], 'L0_cond_b': _L0_cond_in['b'], 'L1_cond_w_q': _L1_cond_in['w_q'], 'L1_cond_b_q': _L1_cond_in['b_q'], 'L1_cond_w_k': _L1_cond_in['w_k'], 'L1_cond_b_k': _L1_cond_in['b_k'], 'L1_cond_w_v': _L1_cond_in['w_v'], 'L1_cond_b_v': _L1_cond_in['b_v'], 'L1_cond_w_o': _L1_cond_in['w_o'], 'L1_cond_b_o': _L1_cond_in['b_o'], 'L1_cond_w_f1': _L1_cond_in['w_f1'], 'L1_cond_b_f1': _L1_cond_in['b_f1'], 'L1_cond_w_f2': _L1_cond_in['w_f2'], 'L1_cond_b_f2': _L1_cond_in['b_f2'], 'L1_cond_w_ada': _L1_cond_in['w_ada'], 'L1_cond_b_ada': _L1_cond_in['b_ada']}

def reference(x, cond_1024, L0_cond_Wx, L0_cond_Wh, L0_cond_b, L1_cond_w_q, L1_cond_b_q, L1_cond_w_k, L1_cond_b_k, L1_cond_w_v, L1_cond_b_v, L1_cond_w_o, L1_cond_b_o, L1_cond_w_f1, L1_cond_b_f1, L1_cond_w_f2, L1_cond_b_f2, L1_cond_w_ada, L1_cond_b_ada):
    import jax
    import jax.numpy as jnp

    def _L0_cond_ref(x, h0, Wx, Wh, b):
        import jax, jax.numpy as jnp
        import numpy as np
        import math
        N, T, D, H = (64, 64, 128, 128)
        xW = jnp.einsum('ntd,dh->nth', x, Wx) + b

        def step(prev_h, xw_t):
            next_h = jnp.tanh(prev_h @ Wh + xw_t)
            return (next_h, next_h)
        _, hs = jax.lax.scan(step, h0, jnp.swapaxes(xW, 0, 1))
        return jnp.swapaxes(hs, 0, 1)

    def _L1_cond_ref(x, t_emb, w_q, b_q, w_k, b_k, w_v, b_v, w_o, b_o, w_f1, b_f1, w_f2, b_f2, w_ada, b_ada):
        import math
        import jax, jax.numpy as jnp
        import numpy as np
        EPS = 1e-07
        MAX_TANH_ARG = 1.0 - 1e-05

        def _norm(x):
            return jnp.sqrt(jnp.sum(x * x, axis=-1, keepdims=True)).clip(EPS)

        def logmap0(x):
            n = _norm(x)
            return jnp.arctanh(jnp.clip(n, EPS, MAX_TANH_ARG)) * x / n

        def expmap0(v):
            n = _norm(v)
            return jnp.tanh(n) * v / n

        def mobius_add(x, y):
            x2 = jnp.sum(x * x, -1, keepdims=True)
            y2 = jnp.sum(y * y, -1, keepdims=True)
            xy = jnp.sum(x * y, -1, keepdims=True)
            num = (1 + 2 * xy + y2) * x + (1 - x2) * y
            den = (1 + 2 * xy + x2 * y2).clip(EPS)
            return num / den

        def plin(x, w, b):
            return expmap0(logmap0(x) @ w + b)

        def layer_norm(x, eps=1e-06):
            m = x.mean(-1, keepdims=True)
            v = ((x - m) ** 2).mean(-1, keepdims=True)
            return (x - m) / jnp.sqrt(v + eps)

        def _beta(a, b):
            return math.exp(math.lgamma(a) + math.lgamma(b) - math.lgamma(a + b))
        D, H, FF = (128, 16, 512)
        HD = D // H
        BETA_N = _beta(D / 2, 0.5)
        BETA_H = _beta(HD / 2, 0.5)

        def _to_heads(p):
            B, S, _ = p.shape
            t = logmap0(p).reshape(B, S, H, HD) * (BETA_H / BETA_N)
            return expmap0(jnp.transpose(t, (0, 2, 1, 3)))

        def _from_heads(ph):
            B, _, S, _ = ph.shape
            t = logmap0(ph) * (BETA_N / BETA_H)
            t = jnp.transpose(t, (0, 2, 1, 3)).reshape(B, S, D)
            return expmap0(t)
        ada = t_emb @ w_ada + b_ada
        sh_msa, sc_msa, g_msa, sh_mlp, sc_mlp, g_mlp = jnp.split(ada, 6, axis=-1)
        residual = x
        xn = layer_norm(logmap0(x))
        xm = expmap0(xn * (1 + sc_msa) + sh_msa)
        q = _to_heads(plin(xm, w_q, b_q))
        k = _to_heads(plin(xm, w_k, b_k))
        v = _to_heads(plin(xm, w_v, b_v))
        qt, kt, vt = (logmap0(q), logmap0(k), logmap0(v))
        scores = jnp.einsum('bhqd,bhkd->bhqk', qt, kt) / math.sqrt(HD)
        attn = jax.nn.softmax(scores, axis=-1)
        out_h = expmap0(jnp.einsum('bhqk,bhkd->bhqd', attn, vt))
        attn_out = plin(_from_heads(out_h), w_o, b_o)
        attn_t = g_msa * logmap0(attn_out)
        x = mobius_add(residual, expmap0(attn_t))
        residual = x
        xn = layer_norm(logmap0(x))
        xm = expmap0(xn * (1 + sc_mlp) + sh_mlp)
        ff = plin(plin(xm, w_f1, b_f1), w_f2, b_f2)
        ff_t = g_mlp * logmap0(ff)
        return mobius_add(residual, expmap0(ff_t))
    x = x + _L0_cond_ref(x, cond_1024, L0_cond_Wx, L0_cond_Wh, L0_cond_b)
    x = x + _L1_cond_ref(x, cond_1024[:, None, :], L1_cond_w_q, L1_cond_b_q, L1_cond_w_k, L1_cond_b_k, L1_cond_w_v, L1_cond_b_v, L1_cond_w_o, L1_cond_b_o, L1_cond_w_f1, L1_cond_b_f1, L1_cond_w_f2, L1_cond_b_f2, L1_cond_w_ada, L1_cond_b_ada)
    return x

_drawn_inputs = setup_inputs


def setup_inputs(seed=0):
    import zlib

    import numpy as np

    out = dict(_drawn_inputs(seed))
    spreads = {'L0_cond_b': (0.0, 0.1),
     'L1_cond_b_q': (0.0, 0.8),
     'L1_cond_b_k': (0.0, 0.8),
     'L1_cond_b_v': (0.0, 0.1),
     'L1_cond_b_o': (0.0, 0.1),
     'L1_cond_b_f1': (0.0, 0.1),
     'L1_cond_b_f2': (0.0, 0.1),
     'L1_cond_b_ada': (0.0, 0.1)}
    factors = {'L1_cond_w_q': 8.0, 'L1_cond_w_k': 8.0, 'L1_cond_w_v': 5.603}
    for name, (base, spread) in spreads.items():
        noise = np.random.default_rng([zlib.crc32(name.encode()), seed]).standard_normal(out[name].shape)
        drawn = base * np.exp(spread * noise) if base else spread * noise
        out[name] = jnp.asarray(drawn.astype(out[name].dtype))
    for name, factor in factors.items():
        out[name] = (out[name] * factor).astype(out[name].dtype)
    return out
```

```python
import math

import numpy as np

import concourse.bass as bass
from concourse import mybir
from contextlib import ExitStack

F32 = mybir.dt.float32
F16 = mybir.dt.float16
I32 = mybir.dt.int32
ALU = mybir.AluOpType
ACT = mybir.ActivationFunctionType
AX = mybir.AxisListType

N, T, D = 32, 128, 128
H, HD = 16, 8
FF = 512
P = 128
TS = P // N
TILES = 4
STEPS = TS * TILES
GROUPS = T // STEPS
GW = TILES * D
NH3 = 3 * H
VW = HD + 1
ROWG = 4

EPS = 1e-7
EPS2 = EPS * EPS
MAXT = float(np.float32(1.0 - 1e-5))
CLIP = math.atanh(MAXT)
LN_EPS = 1e-6


def _beta(a, b):
    return math.exp(math.lgamma(a) + math.lgamma(b) - math.lgamma(a + b))


BETA_UP = _beta(HD / 2, 0.5) / _beta(D / 2, 0.5)
SCALE = 1.0 / math.sqrt(HD)


def nn(value):
    return max(value, 0) if isinstance(value, int) else value


class Chain:

    def __init__(self, eng, sem):
        self.eng, self.sem, self.base, self.n = eng, sem, 0, 0

    def start(self, base):
        self.base, self.n = base, 0

    def add(self, ins):
        self.n += 1
        ins.then_inc(self.sem, 1)

    def sync(self):
        self.eng.wait_ge(self.sem, self.base + self.n)

    def link(self, ins):
        self.add(ins)
        self.sync()


def build(nc, x, cond, Wx, Wh, b, w_q, b_q, w_k, b_k, w_v, b_v, w_o, b_o, w_f1, b_f1, w_f2, b_f2, w_ada, b_ada, out):
    v_dram = nc.dram_tensor("v_scratch", (N, T, H * VW), F32, kind="Internal").ap()
    o_dram = nc.dram_tensor("o_scratch", (N, T, D), F32, kind="Internal").ap()
    ctx = ExitStack()
    with ctx:
        def sb(name, shape, dt=F32):
            return ctx.enter_context(nc.sbuf_tensor(name, shape, dt))

        def sem(name):
            return ctx.enter_context(nc.semaphore(name))

        def tiles(ap):
            return ap.rearrange("p (k d) -> p k d", k=TILES)

        wx_sb, wh_sb, wo_sb = sb("wx_sb", [P, D]), sb("wh_sb", [P, D]), sb("wo_sb", [P, D])
        wqkv_sb = sb("wqkv_sb", [P, 3 * D])
        wada_sb = sb("wada_sb", [P, 6 * D])
        w1_sb = sb("w1_sb", [P, FF])
        w2_sb = sb("w2_sb", [P, FF // P, D])
        b_row = sb("b_row", [1, D])
        bias_row = sb("bias_row", [1, 6 * D + 3 * D + D + FF + D])
        cond_sb = sb("cond_sb", [N, D])
        h0T = sb("h0T", [P, N])
        cond4 = sb("cond4", [P, TS, N])
        ident = sb("ident", [P, P])
        ident16 = sb("ident16", [P, P], F16)
        ones_row = sb("ones_row", [1, GW])
        half = sb("half", [P, 256])
        mhalf = sb("mhalf", [P, 256])
        ada = sb("ada", [P, 6 * D])
        bqkv = sb("bqkv", [P, 3 * D])
        bo = sb("bo", [P, D])
        b1 = sb("b1", [P, FF])
        b2 = sb("b2", [P, D])

        X1 = sb("X1", [P, GROUPS * GW])
        X2 = sb("X2", [P, GROUPS * GW])
        X1N = sb("X1N", [P, GROUPS * TILES])
        X2N = sb("X2N", [P, GROUPS * TILES])
        QK = sb("QK", [P, N, 8, T], F16)

        x_st = [sb(f"x_st{i}", [P, TILES, D]) for i in range(2)]
        xT_sb = sb("xT_sb", [P, GW])
        hsT = sb("hsT", [P, STEPS * N])
        st = sb("st", [P, TILES, 6])
        mv = sb("mv", [P, TILES, 2])
        S = sb("S", [P, 24, TILES])
        carry = sb("carry", [P, 2])
        carry_pool = sb("carry_pool", [P, 1])
        SI = sb("SI", [P, 2, TILES], I32)
        U = sb("U", [P, TILES, D])
        SQU = sb("SQU", [P, TILES, D])
        uT = sb("uT", [P, GW])
        Tq = sb("Tq", [P, 3, TILES, D])
        SQT = sb("SQT", [P, 3, TILES, D])
        HS = sb("HS", [P, TILES * NH3 + TILES * 3])
        HR = sb("HR", [P, TILES * NH3 + TILES * 3])
        QK12 = [sb(f"QK12{i}", [P, TILES * H, 4, HD], F16) for i in range(2)]
        Vaug = sb("Vaug", [P, TILES, H, VW])

        QKb = [sb(f"QKb{i}", [P, 8, T], F16) for i in range(2)]
        Vb = [sb(f"Vb{i}", [P, H * VW + 32]) for i in range(2)]
        Pb = [sb(f"Pb{i}", [P, ROWG, 4, T]) for i in range(2)]
        OTs = [sb(f"OTs{i}", [P, 4, T]) for i in range(2)]
        rec = [sb(f"rec{i}", [P, H]) for i in range(2)]
        ob = [sb(f"ob{i}", [P, D]) for i in range(2)]

        free = QK[:, :, :, :].rearrange("p n g t -> p (n g t)").bitcast(F32)
        taken = [0]

        def place(width):
            taken[0] += width
            return free[:, taken[0] - width:taken[0]]

        o_ld = tiles(place(GW))
        oT = place(GW)
        PA = tiles(place(GW))
        GA = [tiles(place(GW)) for _ in range(2)]
        SQ3 = [place(3 * GW).rearrange("p (a k d) -> p a k d", a=3, k=TILES) for _ in range(2)]
        TMP = tiles(place(GW))
        vb = [place(FF) for _ in range(2)]
        vsq = [place(FF) for _ in range(2)]
        vT = [place(FF) for _ in range(2)]
        YO = tiles(place(GW))
        R3 = sb("R3", [P, 3, TILES])
        ssv = sb("ssv", [P, TILES])
        RU = sb("RU", [P, TILES])

        ps = ctx.enter_context(nc.psum_tensor("ps", [P, 8, 512], F32))

        rnn_w = sem("rnn_weights_in"); all_w = sem("other_weights_in"); x_in = sem("x_in")
        pool_const = sem("pool_const"); pool_chain = sem("pool_chain"); dve_chain = sem("dve_chain")
        condT_ps = sem("condT_ps"); cond_ready = sem("cond_ready")
        ada_ps = sem("ada_ps"); ada_used = sem("ada_used"); setup_done = sem("setup_done")
        xT_ps = sem("xT_ps"); xT_copied = sem("xT_copied"); xw_ready = sem("xw_ready")
        h_ready = sem("h_ready"); rnn_mm = sem("rnn_mm"); hT_ready = sem("hT_ready")
        x1_added = sem("x1_added")
        pow_req = sem("pow_req"); pow_done = sem("pow_done")
        u0_ready = sem("u0_ready"); u_ready = sem("u_ready"); squ_ready = sem("squ_ready")
        uT_ps = sem("uT_ps"); uT_copied = sem("uT_copied")
        qkv_ps = sem("qkv_ps"); t_done = sem("t_done"); sqt_ready = sem("sqt_ready")
        f_ready = sem("f_ready"); q1_ready = sem("q1_ready"); q2_ready = sem("q2_ready")
        v_ready = sem("v_ready"); v_out = sem("v_out")
        d_ps = sem("d_ps"); d_copied = sem("d_copied")
        qk_in = [sem("qk_in0"), sem("qk_in1")]; v_in = [sem("v_in0"), sem("v_in1")]
        s_ps = sem("s_ps"); p_ready = sem("p_ready"); pv_ps = sem("pv_ps"); ot_copied = sem("ot_copied")
        o4_ps = sem("o4_ps"); o_norm = sem("o_norm"); o_out = [sem("o_out0"), sem("o_out1")]; rec_done = sem("rec_done")
        o_in = sem("o_in"); oT_ps = sem("oT_ps"); oT_copied = sem("oT_copied"); wo_ps = sem("wo_ps")
        p_done = sem("p_done"); ga_ready = sem("ga_ready"); sqp_ready = sem("sqp_ready"); sqg_ready = sem("sqg_ready")
        xg_ready = sem("xg_ready"); na_ready = sem("na_ready"); th_ready = sem("th_ready")
        f1_ps = sem("f1_ps"); v_done = sem("v_done"); vsq_done = sem("vsq_done")
        vT_ps = sem("vT_ps"); vT_copied = sem("vT_copied"); f2_ps = sem("f2_ps")
        x2_done = sem("x2_done"); y_done = sem("y_done"); y_out = sem("y_out")
        u0_ready3 = sem("u0_ready3"); u_ready3 = sem("u_ready3"); squ_ready3 = sem("squ_ready3")
        uT_ps3 = sem("uT_ps3"); uT_copied3 = sem("uT_copied3")
        pow_req3 = sem("pow_req3"); pow_done3 = sem("pow_done3"); dve_chain3 = sem("dve_chain3")
        pool_chain3 = sem("pool_chain3")

        SETUP_LINKS = 8
        PREP_LINKS = [None]
        block = ctx.enter_context(nc.Block())

        dram_tile = lambda ap, j, s: ap.rearrange("n (g k s) d -> s n g k d", g=GROUPS, s=TS)[s, :, bass.ds(j, 1), :, :].rearrange("n o k d -> n (o k) d")

        def rows4(ap, width=D):
            return ap.unsqueeze(1).broadcast_to([P, TILES, width])

        def cols(store, j, width):
            return store[:, bass.ds(j * width, width)]

        def heads(i):
            return Tq[:, i, :, :].rearrange("p k (h d) -> p (k h) d", d=HD)

        def twice(i):
            return heads(i).unsqueeze(2).broadcast_to([P, TILES * H, 2, HD])

        def parts(i, part):
            if i == 0:
                return QK12[0][:, :, :, :].rearrange("p h (b s) d -> p h b s d", s=2)[:, :, :, part, :]
            return QK12[1][:, :, 2 * part:2 * part + 2, :]

        @block.sync
        def _(sp):
            def load_x(j, par):
                for s in range(TS):
                    sp.dma_start(x_st[par][s * N:(s + 1) * N, :, :], dram_tile(x, j, s)).then_inc(x_in, 16)

            load_x(0, 0)
            sp.dma_start(wx_sb[:, :], Wx).then_inc(rnn_w, 16)
            sp.dma_start(wh_sb[:, :], Wh).then_inc(rnn_w, 16)
            sp.dma_start(b_row[:, :], b.unsqueeze(0)).then_inc(rnn_w, 16)
            sp.dma_start(cond_sb[:, :], cond).then_inc(rnn_w, 16)
            sp.dma_start(wada_sb[:, :], w_ada).then_inc(all_w, 16)
            for n, w in enumerate((w_q, w_k, w_v)):
                sp.dma_start(wqkv_sb[:, n * D:(n + 1) * D], w).then_inc(all_w, 16)
            at = 0
            for row in (b_ada, b_q, b_k, b_v, b_o, b_f1, b_f2):
                width = row.shape[0]
                sp.dma_start(bias_row[:, at:at + width], row.unsqueeze(0)).then_inc(all_w, 16)
                at += width
            sp.dma_start(wo_sb[:, :], w_o).then_inc(all_w, 16)
            sp.dma_start(w1_sb[:, :], w_f1).then_inc(all_w, 16)
            sp.dma_start(w2_sb[:, :, :], w_f2.rearrange("(c p) d -> p c d", p=P)).then_inc(all_w, 16)
            sp.wait_ge(x_in, 64)
            load_x(1, 1)

            def move(j, par, last=False):
                if not last:
                    sp.wait_ge(x1_added, nn(j))
                    sp.wait_ge(x_in, 64 * (j + 1))
                    load_x(j + 1, 1 - par)

            def store_v(j):
                sp.wait_ge(v_ready, j + 1)
                for s in range(TS):
                    sp.dma_start(dram_tile(v_dram, j, s),
                                 Vaug[s * N:(s + 1) * N, :, :, :].rearrange("n k h c -> n k (h c)")).then_inc(v_out, 16)

            move(1, 1)
            store_v(0)
            move(2, 0)
            store_v(1)
            with sp.Fori(1, GROUPS // 2 - 1) as i:
                for u in range(2):
                    move(2 * i + 1 + u, 1 - u)
                    store_v(2 * i + u)
            store_v(GROUPS - 2)
            store_v(GROUPS - 1)

            sp.wait_ge(v_out, 64 * GROUPS)
            sp.wait_ge(d_copied, 2 * TILES * GROUPS)

            def load_batch(n, par):
                sp.dma_start(QKb[par][:, :, :].rearrange("p g t -> p (g t)"),
                             QK[:, bass.ds(n, 1), :, :].rearrange("p o g t -> p (o g t)")).then_inc(qk_in[par], 16)
                sp.dma_start(Vb[par][:, 0:H * VW], v_dram[bass.ds(n, 1), :, :].rearrange("o t c -> (o t) c")).then_inc(v_in[par], 16)

            def store_o(n, par):
                sp.wait_ge(o_norm, n + 1)
                sp.dma_start(o_dram[bass.ds(n, 1), :, :].rearrange("o t d -> (o t) d"), ob[par][:, :]).then_inc(o_out[par], 16)

            load_batch(0, 0)
            load_batch(1, 1)
            sp.wait_ge(s_ps, 2)
            sp.wait_ge(pv_ps, 1)
            load_batch(2, 0)
            sp.wait_ge(pv_ps, 2)
            load_batch(3, 1)
            with sp.Fori(0, (N - 4) // 2) as i:
                for u in range(2):
                    store_o(2 * i + u, u)
                    sp.wait_ge(pv_ps, 2 * i + u + 3)
                    load_batch(2 * i + u + 4, u)
            for n in range(N - 4, N):
                store_o(n, n % 2)

            for par in range(2):
                sp.wait_ge(o_out[par], 16 * (N // 2))

            def load_o(j):
                for s in range(TS):
                    sp.dma_start(o_ld[s * N:(s + 1) * N, :, :], dram_tile(o_dram, j, s)).then_inc(o_in, 16)

            def store_y(j):
                sp.wait_ge(y_done, j + 1)
                for s in range(TS):
                    sp.dma_start(dram_tile(out, j, s), YO[s * N:(s + 1) * N, :, :]).then_inc(y_out, 16)

            load_o(0)
            sp.wait_ge(oT_ps, 1)
            load_o(1)
            with sp.Fori(0, GROUPS - 2) as i:
                sp.wait_ge(oT_ps, i + 2)
                load_o(i + 2)
                store_y(i)
            store_y(GROUPS - 2)
            store_y(GROUPS - 1)
            sp.wait_ge(y_out, 64 * GROUPS)

        @block.gpsimd
        def _(pool):
            nc.gpsimd.memset(ident[:, :], 0.0).then_inc(pool_chain, 1)
            nc.gpsimd.memset(half[:, :], 0.5).then_inc(pool_const, 1)
            nc.gpsimd.memset(mhalf[:, :], -0.5).then_inc(pool_const, 1)
            nc.gpsimd.memset(ones_row[:, :], 1.0).then_inc(pool_const, 1)
            nc.gpsimd.memset(Vaug[:, :, :, :], 1.0).then_inc(pool_const, 1)
            for i in range(2):
                nc.gpsimd.memset(Vb[i][:, :], 0.0).then_inc(pool_const, 1)
            pool.wait_ge(pool_chain, 1)
            nc.gpsimd.affine_select(out=ident[:, :], in_=ident[:, :], compare_op=ALU.not_equal, fill=1.0, base=0,
                                    pattern=[[-1, P]], channel_multiplier=1).then_inc(pool_chain, 1)
            pool.wait_ge(pool_chain, 2)
            nc.gpsimd.tensor_copy(ident16[:, :], ident[:, :]).then_inc(pool_const, 1)
            pool.wait_ge(pool_const, 7)
            pool.wait_ge(setup_done, 1)

            def power(dst, src, exponent, req, done, n):
                pool.wait_ge(req, nn(n))
                nc.gpsimd.tensor_tensor(dst, src, exponent, ALU.pow).then_inc(done, 1)

            def modulate(j, c0, u0_r, u_r, squ_r, chain, base, free=None):
                pool.wait_ge(u0_r, j + 1)
                nc.gpsimd.tensor_tensor(U[:, :, :], U[:, :, :], rows4(ada[:, c0 + D:c0 + 2 * D]), ALU.mult).then_inc(chain, 1)
                pool.wait_ge(chain, base + 1)
                nc.gpsimd.tensor_tensor(U[:, :, :], U[:, :, :], rows4(ada[:, c0:c0 + D]), ALU.add).then_inc(u_r, 1)
                pool.wait_ge(u_r, j + 1)
                nc.gpsimd.tensor_tensor(SQU[:, :, :], U[:, :, :], U[:, :, :], ALU.mult).then_inc(squ_r, 1)

            def prep(j):
                power(S[:, 1, :], S[:, 0, :], half[:, 0:TILES], pow_req, pow_done, 4 * j + 1)
                power(S[:, 15, :], S[:, 14, :], mhalf[:, 0:TILES], pow_req, pow_done, 4 * j + 2)
                modulate(j, 0, u0_ready, u_ready, squ_ready, pool_chain, j + 2)
                power(S[:, 18, :], S[:, 17, :], mhalf[:, 0:TILES], pow_req, pow_done, 4 * j + 3)
                pool.wait_ge(t_done, TILES * j + TILES)
                nc.gpsimd.tensor_tensor(SQT[:, :, :, :], Tq[:, :, :, :], Tq[:, :, :, :], ALU.mult).then_inc(sqt_ready, 1)
                power(HR[:, :], HS[:, :], mhalf[:, 0:TILES * NH3 + TILES * 3], pow_req, pow_done, 4 * j + 4)
                pool.wait_ge(f_ready, j + 1)
                pool.wait_ge(d_ps, nn(2 * TILES * j))
                nc.gpsimd.tensor_tensor(carry_pool[:, :], half[:, 0:1], half[:, 0:1], ALU.add)
                for i in range(2):
                    ins = nc.gpsimd.tensor_copy(parts(i, 0), twice(i))
                ins.then_inc(q1_ready, 1)

            prep(0)
            with pool.Fori(1, GROUPS) as j:
                prep(j)

            def products(j, n, half_no):
                c0 = (2 if half_no == 0 else 5) * D
                pool.wait_ge(p_done, n + 1)
                nc.gpsimd.tensor_tensor(GA[half_no][:, :, :], PA[:, :, :], rows4(ada[:, c0:c0 + D]), ALU.mult).then_inc(ga_ready, 1)
                pool.wait_ge(ga_ready, n + 1)
                src = X1 if half_no == 0 else X2
                nc.gpsimd.tensor_tensor(SQ3[half_no][:, 2, :, :], GA[half_no][:, :, :], tiles(cols(src, j, GW)), ALU.mult).then_inc(xg_ready, 1)

            def mobius_powers(n, b0):
                power(S[:, 18, :], S[:, 17, :], mhalf[:, 0:TILES], pow_req3, pow_done3, b0 + 1)
                power(S[:, 3, :], S[:, 2, :], half[:, 0:TILES], pow_req3, pow_done3, b0 + 2)

            def a_part(j, n, b0):
                products(j, n, 0)
                mobius_powers(n, b0)
                power(S[:, 1, :], S[:, 0, :], half[:, 0:TILES], pow_req3, pow_done3, b0 + 3)
                power(S[:, 15, :], S[:, 14, :], mhalf[:, 0:TILES], pow_req3, pow_done3, b0 + 4)
                modulate(j, 3 * D, u0_ready3, u_ready3, squ_ready3, pool_chain3, j)
                power(S[:, 18, :], S[:, 17, :], mhalf[:, 0:TILES], pow_req3, pow_done3, b0 + 5)

            def b_part(j, n, b0):
                power(S[:, 18, :], S[:, 17, :], mhalf[:, 0:TILES], pow_req3, pow_done3, b0 + 1)
                products(j, n, 1)
                mobius_powers(n, b0 + 1)

            a_part(0, 0, 0)
            with pool.Fori(1, GROUPS) as i:
                a_part(i, 2 * i - 1, 8 * i - 3)
                b_part(i - 1, 2 * i, 8 * i + 2)
            b_part(GROUPS - 1, 2 * GROUPS - 1, 8 * GROUPS - 3)

        @block.scalar
        def _(act):
            def rnn_step(i, s, par):
                act.wait_ge(rnn_mm, STEPS * i + s + 1)
                nc.scalar.activation(hsT[:, s * N:(s + 1) * N], ps[:, par, s * N:(s + 1) * N], ACT.Tanh).then_inc(h_ready, 1)

            def copy_xT(j):
                act.wait_ge(xT_ps, j + 1)
                act.wait_ge(xw_ready, nn(j))
                nc.scalar.activation(xT_sb[:, :], ps[:, 4, :], ACT.Copy).then_inc(xT_copied, 1)

            def copy_uT(j):
                act.wait_ge(uT_ps, j + 1)
                act.wait_ge(qkv_ps, nn(TILES * j))
                nc.scalar.activation(uT[:, :], ps[:, 4, :], ACT.Copy).then_inc(uT_copied, 1)

            def copy_d(j, k, qk):
                act.wait_ge(d_ps, 2 * TILES * j + 2 * k + qk + 1)
                src = ps[:, 3 + 4 * qk, :].bitcast(F16)[:, 0:512].rearrange("p (g s n) -> p g s n", g=4, s=TS)
                dst = QK[:, :, 4 * qk:4 * qk + 4, bass.ds(STEPS * j + TS * k, TS)].rearrange("p n g s -> p g s n")
                nc.scalar.activation(dst, src, ACT.Copy).then_inc(d_copied, 1)

            def group(i, par, first=False, second=False, last=False):
                for s in range(STEPS):
                    rnn_step(i, s, par)
                    if s == 2 and not last:
                        copy_xT(i + 1)
                    if not first and s == 11:
                        copy_uT(i - 1)
                    if not first and not second and s in (1, 3, 5, 7):
                        copy_d(i - 2, (s - 1) // 2, 0)
                    if not first and not second and s in (2, 4, 6, 8):
                        copy_d(i - 2, (s - 2) // 2, 1)

            copy_xT(0)
            group(0, 0, first=True)
            group(1, 1, second=True)
            group(2, 0)
            with act.Fori(1, GROUPS // 2 - 1) as i:
                for u in range(2):
                    group(2 * i + 1 + u, 1 - u)
            group(GROUPS - 1, 1, last=True)
            for j in (GROUPS - 2, GROUPS - 1):
                if j == GROUPS - 1:
                    copy_uT(j)
                for k in range(TILES):
                    for qk in range(2):
                        copy_d(j, k, qk)

            def exps(n, par):
                for hf in range(2):
                    act.wait_ge(s_ps, 2 * n + hf + 1)
                    act.wait_ge(pv_ps, nn(n - 1))
                    nc.scalar.activation(Pb[par][:, 2 * hf:2 * hf + 2, :, :].rearrange("p g j q -> p (g j q)"),
                                         ps[:, 2 * hf:2 * hf + 2, :].rearrange("p g c -> p (g c)"),
                                         ACT.Exp, scale=SCALE).then_inc(p_ready, 1)

            exps(0, 0)
            exps(1, 1)
            with act.Fori(1, N // 2) as i:
                for u in range(2):
                    exps(2 * i + u, u)

            def a_front(i):
                act.wait_ge(oT_ps, i + 1)
                nc.scalar.activation(oT[:, :], ps[:, 0, :], ACT.Copy).then_inc(oT_copied, 1)

            def square_p(n, hn):
                act.wait_ge(p_done, n + 1)
                nc.scalar.activation(SQ3[hn][:, 0, :, :], PA[:, :, :], ACT.Square).then_inc(sqp_ready, 1)

            def square_g(n, hn):
                act.wait_ge(ga_ready, n + 1)
                nc.scalar.activation(SQ3[hn][:, 1, :, :], GA[hn][:, :, :], ACT.Square).then_inc(sqg_ready, 1)

            def tanh(n):
                act.wait_ge(na_ready, n + 1)
                nc.scalar.activation(S[:, 5, :], S[:, 4, :], ACT.Tanh).then_inc(th_ready, 1)

            def square_v(j, k):
                act.wait_ge(v_done, TILES * j + k + 1)
                nc.scalar.activation(vsq[k % 2][:, :], vb[k % 2][:, :], ACT.Square, accum_out=ssv[:, k:k + 1]).then_inc(vsq_done, 1)

            def copy_vT(j, k):
                act.wait_ge(vT_ps, TILES * j + k + 1)
                act.wait_ge(f2_ps, nn(TILES * j + k - 1))
                nc.scalar.activation(vT[k % 2][:, :], ps[:, 5 + k % 2, :], ACT.Copy).then_inc(vT_copied, 1)

            def copy_uT3(j):
                act.wait_ge(uT_ps3, j + 1)
                act.wait_ge(f1_ps, nn(TILES * j))
                nc.scalar.activation(uT[:, :], ps[:, 2, :], ACT.Copy).then_inc(uT_copied3, 1)

            def a_only(j, n):
                a_front(j)
                square_p(n, 0)
                square_g(n, 0)
                tanh(n)
                copy_uT3(j)

            def b_rest(j, n):
                square_p(n, 1)
                square_g(n, 1)
                tanh(n)

            a_only(0, 0)

            def both(i):
                j = i - 1
                a_front(i)
                square_v(j, 0)
                square_p(2 * i - 1, 0)
                copy_vT(j, 0)
                square_v(j, 1)
                square_g(2 * i - 1, 0)
                copy_vT(j, 1)
                square_v(j, 2)
                copy_vT(j, 2)
                tanh(2 * i - 1)
                square_v(j, 3)
                copy_vT(j, 3)
                copy_uT3(i)
                b_rest(j, 2 * i)

            both(1)
            with act.Fori(2, GROUPS) as i:
                both(i)
            for k in range(TILES):
                square_v(GROUPS - 1, k)
                copy_vT(GROUPS - 1, k)
            b_rest(GROUPS - 1, 2 * GROUPS - 1)

        @block.vector
        def _(dve):
            chain = Chain(dve, dve_chain)
            chain.start(0)
            V = nc.vector

            dve.wait_ge(condT_ps, 1)
            V.tensor_copy(h0T[:, :], ps[:, 2, 0:N]).then_inc(h_ready, 1)
            V.tensor_copy(cond4[:, :, :], ps[:, 2, 0:N].unsqueeze(1).broadcast_to([P, TS, N])).then_inc(cond_ready, 1)
            dve.wait_ge(ada_ps, 1)
            V.tensor_copy(ada[:, 0:3 * D], ps[:, 5, 0:3 * D]).then_inc(ada_used, 1)
            dve.wait_ge(ada_ps, 2)
            V.tensor_copy(ada[:, 3 * D:6 * D], ps[:, 6, 0:3 * D]).then_inc(ada_used, 1)
            dve.wait_ge(ada_used, 2)
            for c in (D, 4 * D):
                V.tensor_scalar_add(ada[:, c:c + D], ada[:, c:c + D], 1.0).then_inc(ada_used, 1)
            dve.wait_ge(ada_ps, 3)
            V.tensor_copy(bqkv[:, :], ps[:, 7, 0:3 * D]).then_inc(ada_used, 1)
            dve.wait_ge(ada_ps, 4)
            V.tensor_copy(b1[:, :], ps[:, 3, :]).then_inc(ada_used, 1)
            dve.wait_ge(ada_ps, 5)
            V.tensor_copy(bo[:, :], ps[:, 5, 0:D]).then_inc(ada_used, 1)
            V.tensor_copy(b2[:, :], ps[:, 5, D:2 * D]).then_inc(ada_used, 1)
            dve.wait_ge(ada_used, 8)
            V.memset(S[:, 23, :], 0.0).then_inc(setup_done, 1)
            dve.wait_ge(setup_done, 1)

            def request(ins, req, done, n):
                ins.then_inc(req, 1)
                dve.wait_ge(done, n)

            def ln_coefficients(store, j, req, done, n):
                mean, var = mv[:, :, 0], mv[:, :, 1]
                chain.link(V.tensor_tensor(S[:, 6, :], mean, mean, ALU.mult))
                chain.link(V.tensor_tensor(S[:, 7, :], S[:, 6, :], var, ALU.add))
                chain.add(V.tensor_scalar(cols(store, j, TILES), S[:, 7, :], float(D), None, ALU.mult))
                request(V.tensor_scalar(S[:, 0, :], S[:, 7, :], float(D), None, ALU.mult), req, done, n)
                chain.link(V.tensor_scalar(S[:, 8, :], S[:, 1, :], EPS, MAXT, ALU.max, ALU.min))
                z = S[:, 8, :]
                chain.add(V.tensor_scalar(S[:, 9, :], S[:, 1, :], EPS, None, ALU.max))
                chain.link(V.tensor_scalar(S[:, 7, :], z, -1.0, 1.0, ALU.mult, ALU.add))
                chain.link(V.reciprocal(S[:, 10, :], S[:, 7, :]))
                chain.link(V.scalar_tensor_tensor(S[:, 11, :], z, 1.0, S[:, 10, :], ALU.add, ALU.mult))
                y, yi = S[:, 11, :], S[:, 11, :].bitcast(I32)
                chain.add(V.tensor_scalar(SI[:, 0, :], yi, 23, None, ALU.logical_shift_right))
                chain.add(V.tensor_scalar(SI[:, 1, :], yi, 0x7FFFFF, 0x3F800000, ALU.bitwise_and, ALU.bitwise_or))
                chain.add(V.tensor_scalar(S[:, 12, :], y, 2.0, None, ALU.is_ge))
                chain.link(V.reciprocal(S[:, 19, :], S[:, 9, :]))
                m = SI[:, 1, :].bitcast(F32)
                chain.add(V.tensor_scalar(S[:, 13, :], SI[:, 0, :], -127.0, None, ALU.add))
                chain.link(V.tensor_scalar(S[:, 6, :], m, 1.0, None, ALU.add))
                chain.link(V.reciprocal(S[:, 7, :], S[:, 6, :]))
                chain.link(V.scalar_tensor_tensor(S[:, 6, :], m, -1.0, S[:, 7, :], ALU.add, ALU.mult))
                chain.link(V.tensor_tensor(S[:, 7, :], S[:, 6, :], z, ALU.subtract))
                chain.link(V.tensor_tensor(S[:, 6, :], S[:, 7, :], S[:, 12, :], ALU.mult))
                chain.link(V.tensor_tensor(S[:, 10, :], S[:, 6, :], z, ALU.add))
                w = S[:, 10, :]
                chain.link(V.tensor_tensor(S[:, 11, :], w, w, ALU.mult))
                w2 = S[:, 11, :]
                chain.link(V.tensor_scalar(S[:, 6, :], w2, 1.0 / 15, None, ALU.mult))
                at, to = 6, 7
                for k in (13, 11, 9, 7, 5, 3):
                    chain.link(V.scalar_tensor_tensor(S[:, to, :], S[:, at, :], 1.0 / k, w2, ALU.add, ALU.mult))
                    at, to = to, at
                chain.link(V.scalar_tensor_tensor(S[:, to, :], S[:, at, :], 1.0, w, ALU.add, ALU.mult))
                at, to = to, at
                chain.link(V.scalar_tensor_tensor(S[:, to, :], S[:, 13, :], 0.5 * math.log(2.0), S[:, at, :], ALU.mult, ALU.add))
                chain.link(V.tensor_tensor(S[:, 12, :], S[:, to, :], S[:, 19, :], ALU.mult))
                chain.link(V.tensor_tensor(S[:, 6, :], S[:, 12, :], S[:, 12, :], ALU.mult))
                chain.link(V.tensor_tensor(S[:, 7, :], S[:, 6, :], var, ALU.mult))
                request(V.tensor_scalar(S[:, 14, :], S[:, 7, :], LN_EPS, None, ALU.add), req, done, n + 1)
                chain.link(V.tensor_tensor(S[:, 16, :], S[:, 12, :], S[:, 15, :], ALU.mult))
                chain.link(V.tensor_tensor(S[:, 19, :], S[:, 16, :], mean, ALU.mult))

            def normalise(src, store, j, req, done, n, u0_sem, u_free, free_n):
                V.memset(carry[:, 0:1], 0.0)
                for k in range(TILES):
                    chain.add(V.bn_stats(st[:, k, :], src(k)))
                chain.sync()
                V.memset(carry[:, 1:2], 0.0)
                for k in range(TILES):
                    chain.add(V.bn_aggr(mv[:, k, :], st[:, k, :]))
                chain.sync()
                ln_coefficients(store, j, req, done, n)
                dve.wait_ge(u_free, nn(free_n))
                for k in range(TILES):
                    ins = V.tensor_scalar(U[:, k, :], src(k), S[:, 16, k:k + 1], S[:, 19, k:k + 1], ALU.mult, ALU.subtract)
                ins.then_inc(u0_sem, 1)

            def clip_factor(dst, req, done, n):
                chain.link(V.tensor_scalar(dst, S[:, 18, :], CLIP, 1.0, ALU.mult, ALU.min))

            def prep(j, par, links):
                chain.start(links * j)
                dve.wait_ge(hT_ready, j + 1)
                V.tensor_tensor(tiles(cols(X1, j, GW)), x_st[par][:, :, :], tiles(ps[:, 2, :]), ALU.add).then_inc(x1_added, 1)
                dve.wait_ge(x1_added, j + 1)
                normalise(lambda k: X1[:, bass.ds(j * GW + k * D, D)], X1N, j, pow_req, pow_done, 4 * j + 1, u0_ready, uT_ps, j)
                dve.wait_ge(squ_ready, j + 1)
                chain.link(V.reduce_sum(S[:, 6, :], SQU[:, :, :], AX.X))
                request(V.tensor_scalar(S[:, 17, :], S[:, 6, :], EPS2, None, ALU.max), pow_req, pow_done, 4 * j + 3)
                clip_factor(S[:, 20, :], pow_req, pow_done, 0)
                for k in range(TILES):
                    dve.wait_ge(qkv_ps, TILES * j + k + 1)
                    V.scalar_tensor_tensor(Tq[:, :, k, :], ps[:, 5 + k % 2, 0:3 * D].rearrange("p (a d) -> p a d", a=3),
                                           S[:, 20, k:k + 1], bqkv[:, :].rearrange("p (a d) -> p a d", a=3),
                                           ALU.mult, ALU.add).then_inc(t_done, 1)
                dve.wait_ge(sqt_ready, j + 1)
                hs = HS[:, 0:TILES * NH3]
                chain.link(V.reduce_sum(hs, SQT[:, :, :, :].rearrange("p a k (h d) -> p (a k h) d", d=HD), AX.X))
                tot = HS[:, TILES * NH3:]
                chain.link(V.reduce_sum(tot, hs.rearrange("p (a h) -> p a h", h=H), AX.X))
                request(V.tensor_scalar(HS[:, :], HS[:, :], EPS2, None, ALU.max), pow_req, pow_done, 4 * j + 4)
                chain.link(V.tensor_scalar(HS[:, :], HR[:, :], CLIP, None, ALU.mult))
                chain.link(V.tensor_scalar(HR[:, TILES * NH3:], tot, 1.0, BETA_UP, ALU.min, ALU.mult))
                rt = HR[:, TILES * NH3:].unsqueeze(2).broadcast_to([P, 3 * TILES, H])
                chain.link(V.tensor_tensor(HR[:, 0:TILES * NH3].rearrange("p (a h) -> p a h", h=H),
                                           hs.rearrange("p (a h) -> p a h", h=H), rt, ALU.min))
                f = HR[:, 0:TILES * NH3].rearrange("p (a h) -> p a h", a=3).unsqueeze(3).broadcast_to([P, 3, TILES * H, HD])
                t = Tq[:, :, :, :].rearrange("p a k (h d) -> p a (k h) d", d=HD)
                V.tensor_tensor(t[:, 0:2, :, :], t[:, 0:2, :, :], f[:, 0:2, :, :], ALU.mult).then_inc(f_ready, 1)
                dve.wait_ge(v_out, nn(64 * j))
                V.tensor_tensor(Vaug[:, :, :, 0:HD].rearrange("p k h d -> p (k h) d"), t[:, 2, :, :], f[:, 2, :, :],
                                ALU.mult).then_inc(v_ready, 1)
                dve.wait_ge(f_ready, j + 1)
                dve.wait_ge(q1_ready, j + 1)
                for i in range(2):
                    ins = V.tensor_tensor(parts(i, 1), twice(i), parts(i, 0), ALU.subtract)
                ins.then_inc(q2_ready, 1)
                return chain.n

            links = prep(0, 0, 0)
            assert prep(1, 1, links) == links
            with dve.Fori(1, GROUPS // 2) as i:
                for u in range(2):
                    prep(2 * i + u, u, links)

            def evacuate(n, par):
                dve.wait_ge(pv_ps, n + 1)
                V.tensor_copy(OTs[par][:, :, :], ps[:, 4, :].rearrange("p (j q) -> p j q", j=4)).then_inc(ot_copied, 1)

            def normal(n, par):
                dve.wait_ge(o4_ps, n + 1)
                o4 = ps[:, 5 + par, :].rearrange("p (h c) -> p h c", c=32)
                V.reciprocal(rec[par][:, :], o4[:, :, HD]).then_inc(rec_done, 1)
                dve.wait_ge(rec_done, n + 1)
                if isinstance(n, int):
                    dve.wait_ge(o_out[par], nn(16 * (n // 2)))
                else:
                    dve.wait_ge(o_out[par], nn(8 * n - 8 * par))
                V.scalar_tensor_tensor(ob[par][:, :].rearrange("p (h d) -> p h d", d=HD), o4[:, :, 0:HD], 1.0 / BETA_UP,
                                       rec[par][:, :].unsqueeze(2).broadcast_to([P, H, HD]), ALU.mult, ALU.mult).then_inc(o_norm, 1)

            evacuate(0, 0)
            for u in range(2):
                evacuate(u + 1, 1 - u)
                normal(u, u)
            with dve.Fori(1, (N - 2) // 2) as i:
                for u in range(2):
                    evacuate(2 * i + u + 1, 1 - u)
                    normal(2 * i + u, u)
            evacuate(N - 1, 1)
            normal(N - 2, 0)
            normal(N - 1, 1)

            chain.sem = dve_chain3

            def mobius(xn, n, pn, hn):
                dve.wait_ge(sqp_ready, n + 1)
                dve.wait_ge(sqg_ready, n + 1)
                dve.wait_ge(xg_ready, n + 1)
                chain.link(V.reduce_sum(R3[:, :, :], SQ3[hn][:, :, :, :], AX.X))
                request(V.tensor_scalar(S[:, 17, :], R3[:, 0, :], EPS2, None, ALU.max), pow_req3, pow_done3, pn)
                chain.link(V.tensor_scalar(S[:, 6, :], S[:, 18, :], CLIP, 1.0, ALU.mult, ALU.min))
                rp = S[:, 6, :]
                chain.link(V.tensor_tensor(S[:, 7, :], rp, rp, ALU.mult))
                request(V.tensor_tensor(S[:, 2, :], S[:, 7, :], R3[:, 1, :], ALU.mult), pow_req3, pow_done3, pn + 1)
                sa = S[:, 2, :]
                V.tensor_scalar(S[:, 4, :], S[:, 3, :], EPS, None, ALU.max).then_inc(na_ready, 1)
                dve.wait_ge(na_ready, n + 1)
                chain.link(V.reciprocal(S[:, 7, :], S[:, 4, :]))
                dve.wait_ge(th_ready, n + 1)
                chain.link(V.tensor_tensor(S[:, 8, :], S[:, 5, :], S[:, 7, :], ALU.mult))
                tau = S[:, 8, :]
                chain.add(V.tensor_tensor(S[:, 9, :], tau, tau, ALU.mult))
                chain.link(V.tensor_tensor(S[:, 10, :], tau, rp, ALU.mult))
                tr = S[:, 10, :]
                chain.add(V.tensor_tensor(S[:, 11, :], S[:, 9, :], sa, ALU.mult))
                chain.link(V.tensor_tensor(S[:, 12, :], tr, R3[:, 2, :], ALU.mult))
                y2 = S[:, 11, :]
                chain.add(V.tensor_scalar(S[:, 13, :], S[:, 12, :], 2.0, 1.0, ALU.mult, ALU.add))
                chain.link(V.tensor_tensor(S[:, 7, :], xn, y2, ALU.mult))
                chain.link(V.tensor_tensor(S[:, 9, :], S[:, 7, :], S[:, 13, :], ALU.add))
                chain.link(V.tensor_scalar(S[:, 7, :], S[:, 9, :], EPS, None, ALU.max))
                chain.add(V.reciprocal(S[:, 9, :], S[:, 7, :]))
                chain.add(V.tensor_tensor(S[:, 12, :], S[:, 13, :], y2, ALU.add))
                chain.link(V.tensor_scalar(S[:, 14, :], xn, -1.0, 1.0, ALU.mult, ALU.add))
                chain.add(V.tensor_tensor(S[:, 21, :], S[:, 12, :], S[:, 9, :], ALU.mult))
                chain.link(V.tensor_tensor(S[:, 7, :], S[:, 14, :], S[:, 9, :], ALU.mult))
                chain.link(V.tensor_tensor(S[:, 22, :], S[:, 7, :], tr, ALU.mult))

            def v_tile(j, k, par_u):
                dve.wait_ge(f1_ps, TILES * j + k + 1)
                dve.wait_ge(vsq_done, nn(TILES * j + k - 1))
                dve.wait_ge(vT_ps, nn(TILES * j + k - 1))
                V.scalar_tensor_tensor(vb[k % 2][:, :], ps[:, 3 + k % 2, :], RU[:, k:k + 1], b1[:, :],
                                       ALU.mult, ALU.add).then_inc(v_done, 1)

            def a_project(j, n):
                dve.wait_ge(wo_ps, j + 1)
                V.tensor_tensor(PA[:, :, :], tiles(ps[:, 1, :]), rows4(bo[:, :]), ALU.add).then_inc(p_done, 1)

            def a_update(j, n, pn):
                mobius(cols(X1N, j, TILES), n, pn, 0)
                for k in range(TILES):
                    chain.add(V.tensor_scalar(TMP[:, k, :], GA[0][:, k, :], S[:, 22, k:k + 1], None, ALU.mult))
                chain.sync()
                for k in range(TILES):
                    ins = V.scalar_tensor_tensor(X2[:, bass.ds(j * GW + k * D, D)], X1[:, bass.ds(j * GW + k * D, D)],
                                                 S[:, 21, k:k + 1], TMP[:, k, :], ALU.mult, ALU.add)
                ins.then_inc(x2_done, 1)
                dve.wait_ge(x2_done, j + 1)

            def a_norm(j, pn):
                normalise(lambda k: X2[:, bass.ds(j * GW + k * D, D)], X2N, j, pow_req3, pow_done3, pn + 2,
                          u0_ready3, uT_ps3, j)

            def a_norm_u(j, pn):
                dve.wait_ge(squ_ready3, j + 1)
                chain.link(V.reduce_sum(S[:, 6, :], SQU[:, :, :], AX.X))
                request(V.tensor_scalar(S[:, 17, :], S[:, 6, :], EPS2, None, ALU.max), pow_req3, pow_done3, pn + 4)
                clip_factor(RU[:, :], None, None, 0)

            def b_final(j, n, pn):
                dve.wait_ge(vsq_done, TILES * (j + 1))
                request(V.tensor_scalar(S[:, 17, :], ssv[:, :], EPS2, None, ALU.max), pow_req3, pow_done3, pn)
                clip_factor(S[:, 20, :], None, None, 0)
                dve.wait_ge(f2_ps, TILES * (j + 1))
                for k in range(TILES):
                    ins = V.scalar_tensor_tensor(PA[:, k, :], ps[:, 7, k * D:(k + 1) * D], S[:, 20, k:k + 1], b2[:, :],
                                                 ALU.mult, ALU.add)
                ins.then_inc(p_done, 1)
                mobius(cols(X2N, j, TILES), n, pn + 1, 1)
                for k in range(TILES):
                    chain.add(V.scalar_tensor_tensor(TMP[:, k, :], GA[1][:, k, :], S[:, 22, k:k + 1],
                                                     X1[:, bass.ds(j * GW + k * D, D)], ALU.mult, ALU.add))
                chain.sync()
                dve.wait_ge(y_out, nn(64 * j))
                for k in range(TILES):
                    ins = V.scalar_tensor_tensor(YO[:, k, :], X2[:, bass.ds(j * GW + k * D, D)], S[:, 21, k:k + 1],
                                                 TMP[:, k, :], ALU.mult, ALU.add)
                ins.then_inc(y_done, 1)

            chain.start(0)
            a_project(0, 0)
            a_update(0, 0, 1)
            a_norm(0, 1)
            a_norm_u(0, 1)
            a_links = chain.n

            def both(i, links):
                j, pn = i - 1, 8 * i - 2
                chain.start(a_links + links * j)
                v_tile(j, 0, 0)
                a_project(i, 2 * i - 1)
                v_tile(j, 1, 0)
                v_tile(j, 2, 0)
                a_update(i, 2 * i - 1, pn)
                v_tile(j, 3, 0)
                a_norm(i, pn)
                a_norm_u(i, pn)
                b_final(j, 2 * i, pn + 5)
                return chain.n

            links3 = both(1, 0)
            with dve.Fori(2, GROUPS) as i:
                both(i, links3)
            j = GROUPS - 1
            chain.start(a_links + links3 * j)
            for k in range(TILES):
                v_tile(j, k, 0)
            b_final(j, 2 * j + 1, 8 * GROUPS - 2)

        @block.tensor
        def _(pe):
            mm = nc.tensor.matmul

            def x_transposes(j, par):
                pe.wait_ge(x_in, 64 * (j + 1))
                pe.wait_ge(uT_copied, nn(j - 2))
                for k in range(TILES):
                    ins = nc.tensor.transpose(ps[:, 4, k * P:(k + 1) * P], x_st[par][:, k, :], ident[:, :])
                ins.then_inc(xT_ps, 1)

            def x_products(j, par):
                pe.wait_ge(xT_copied, j + 1)
                mm(ps[:, par, :], wx_sb[:, :], xT_sb[:, :], start=True, stop=False, skip_group_check=True)
                mm(ps[:, par, :], b_row[:, :], ones_row[:, :], start=False, stop=False, skip_group_check=True).then_inc(xw_ready, 1)

            def rnn_step(i, s, par):
                pe.wait_ge(h_ready, STEPS * i + s + 1)
                rhs = hsT[:, (s - 1) * N:s * N] if s else (hsT[:, (STEPS - 1) * N:] if not (isinstance(i, int) and i == 0) else h0T[:, :])
                mm(ps[:, par, s * N:(s + 1) * N], wh_sb[:, :], rhs, start=False, stop=s == STEPS - 1,
                   skip_group_check=True).then_inc(rnn_mm, 1)

            def h_transpose(i, k):
                if k == 0:
                    pe.wait_ge(x1_added, nn(i))
                ins = nc.tensor.transpose(ps[:, 2, k * P:(k + 1) * P], hsT[:, k * P:(k + 1) * P], ident[:, :])
                if k == TILES - 1:
                    ins.then_inc(hT_ready, 1)

            def u_transposes(j, bank, ready, copied, copies, done):
                pe.wait_ge(ready, j + 1)
                pe.wait_ge(copied, nn(copies))
                for k in range(TILES):
                    ins = nc.tensor.transpose(ps[:, bank, k * P:(k + 1) * P], U[:, k, :], ident[:, :])
                ins.then_inc(done, 1)

            def qkv(j, k):
                pe.wait_ge(uT_copied, j + 1)
                pe.wait_ge(t_done, nn(TILES * j + k - 1))
                mm(ps[:, 5 + k % 2, 0:3 * D], uT[:, k * P:(k + 1) * P], wqkv_sb[:, :], start=True, stop=True).then_inc(qkv_ps, 1)

            def split_transposes(j, k, qk):
                pe.wait_ge(q2_ready, j + 1)
                pe.wait_ge(d_copied, nn(2 * TILES * j + 2 * k + qk - 1 if qk or k else 2 * TILES * j))
                dst = ps[:, 3 + 4 * qk, :].bitcast(F16)
                for g in range(4):
                    h0 = H * k + 4 * g
                    src = QK12[qk][:, h0:h0 + 4, :, :].rearrange("p h b d -> p (h b d)")
                    c = g * P
                    ins = nc.tensor.transpose(dst[:, c:c + P], src, ident16[:, :])
                ins.then_inc(d_ps, 1)

            pe.wait_ge(pool_const, 7)
            pe.wait_ge(pool_chain, 2)
            pe.wait_ge(rnn_w, 64)
            nc.tensor.transpose(ps[:, 2, 0:N], cond_sb[:, :], ident[0:N, 0:N]).then_inc(condT_ps, 1)
            x_transposes(0, 0)
            x_products(0, 0)

            def group(i, par, first=False, second=False, last=False):
                for s in range(STEPS):
                    rnn_step(i, s, par)
                    if s == 0 and not first:
                        h_transpose(i - 1, TILES - 1)
                    if s % TS == 0 and s:
                        h_transpose(i, s // TS - 1)
                    if not first and not second and s in (1, 3, 5, 7):
                        split_transposes(i - 2, (s - 1) // 2, 0)
                    if not first and not second and s in (2, 4, 6, 8):
                        split_transposes(i - 2, (s - 2) // 2, 1)
                    if s == 1 and not last:
                        x_transposes(i + 1, 1 - par)
                    if s == 9 and not last:
                        x_products(i + 1, 1 - par)
                    if s == 10 and not first:
                        u_transposes(i - 1, 4, u_ready, xT_copied, min(i + 2, GROUPS) if isinstance(i, int) else i + 2, uT_ps)
                    if s in (12, 13, 14, 15) and not first:
                        qkv(i - 1, s - 12)
                    if first and s in (2, 3, 4, 5, 6):
                        setup(s - 2)

            def setup(part):
                rows = {"qkv": 6 * D, "o": 9 * D, "f1": 10 * D, "f2": 10 * D + FF}

                def spread(bank, c0, at, width):
                    return mm(ps[:, bank, c0:c0 + width], ones_row[:, 0:P], bias_row[:, at:at + width], start=True, stop=True)

                if part == 0:
                    pe.wait_ge(all_w, 14 * 16)
                    pe.wait_ge(cond_ready, 1)
                if part < 2:
                    c = part * 3 * D
                    mm(ps[:, 5 + part, 0:3 * D], cond4[:, :, :].rearrange("p s n -> p (s n)"), wada_sb[:, c:c + 3 * D], start=True, stop=False)
                    mm(ps[:, 5 + part, 0:3 * D], ones_row[:, 0:P], bias_row[:, c:c + 3 * D], start=False, stop=True).then_inc(ada_ps, 1)
                if part == 2:
                    spread(7, 0, rows["qkv"], 3 * D).then_inc(ada_ps, 1)
                if part == 3:
                    spread(3, 0, rows["f1"], FF).then_inc(ada_ps, 1)
                if part == 4:
                    pe.wait_ge(ada_used, 1)
                    spread(5, 0, rows["o"], D)
                    spread(5, D, rows["f2"], D).then_inc(ada_ps, 1)

            group(0, 0, first=True)
            pe.wait_ge(ada_used, 8)
            group(1, 1, second=True)
            group(2, 0)
            with pe.Fori(1, GROUPS // 2 - 1) as i:
                for u in range(2):
                    group(2 * i + 1 + u, 1 - u)
            group(GROUPS - 1, 1, last=True)
            pe.wait_ge(h_ready, STEPS * GROUPS + 1)
            h_transpose(GROUPS - 1, TILES - 1)
            for j in (GROUPS - 2, GROUPS - 1):
                if j == GROUPS - 1:
                    u_transposes(j, 4, u_ready, uT_copied, j, uT_ps)
                    for k in range(TILES):
                        qkv(j, k)
                for k in range(TILES):
                    for qk in range(2):
                        split_transposes(j, k, qk)
            pe.wait_ge(d_copied, 2 * TILES * GROUPS)

            def scores(n, par, loads, hf):
                pe.wait_ge(qk_in[par], 16 * loads)
                pe.wait_ge(p_ready, nn(2 * n + hf - 1))
                for j in range(4):
                    for g in (2 * hf, 2 * hf + 1):
                        r = slice(32 * g, 32 * g + 32)
                        ins = mm(ps[:, g, j * T:(j + 1) * T], QKb[par][r, 4 + j, :], QKb[par][r, j, :], start=True, stop=True)
                ins.then_inc(s_ps, 1)

            def weighted(n, par, loads):
                pe.wait_ge(v_in[par], 16 * loads)
                pe.wait_ge(p_ready, 2 * n + 2)
                pe.wait_ge(ot_copied, nn(n))
                for j in range(4):
                    for g in range(ROWG):
                        h = 4 * j + g
                        ins = mm(ps[32 * g:32 * g + 32, 4, j * T:(j + 1) * T], Vb[par][:, VW * h:VW * h + 32],
                                 Pb[par][:, g, j, :], start=True, stop=True)
                ins.then_inc(pv_ps, 1)

            def back(n, par):
                pe.wait_ge(ot_copied, n + 1)
                pe.wait_ge(o_norm, nn(n - 1))
                for j in range(4):
                    ins = nc.tensor.transpose(ps[:, 5 + par, j * P:(j + 1) * P], OTs[par][:, j, :], ident[:, :])
                ins.then_inc(o4_ps, 1)

            def step(n, par, half_n, has_s=True, has_w=True, has_b=True):
                if has_s:
                    scores(n, par, half_n + 1, 0)
                if has_b:
                    back(n - 2, par)
                if has_s:
                    scores(n, par, half_n + 1, 1)
                if has_w:
                    weighted(n - 1, 1 - par, half_n + par)

            step(0, 0, 0, has_w=False, has_b=False)
            step(1, 1, 0, has_b=False)
            step(2, 0, 1)
            step(3, 1, 1)
            with pe.Fori(2, N // 2) as i:
                for u in range(2):
                    step(2 * i + u, u, i)
            step(N, 0, N // 2, has_s=False)
            step(N + 1, 1, N // 2, has_s=False, has_w=False)

            def o_transposes(i):
                pe.wait_ge(o_in, 64 * (i + 1))
                pe.wait_ge(oT_copied, nn(i))
                for k in range(TILES):
                    ins = nc.tensor.transpose(ps[:, 0, k * P:(k + 1) * P], o_ld[:, k, :], ident[:, :])
                ins.then_inc(oT_ps, 1)

            def project(i, p_count):
                pe.wait_ge(oT_copied, i + 1)
                pe.wait_ge(p_done, nn(p_count))
                for k in range(TILES):
                    ins = mm(ps[:, 1, k * D:(k + 1) * D], oT[:, k * P:(k + 1) * P], wo_sb[:, :], start=True, stop=True)
                ins.then_inc(wo_ps, 1)

            def f1(j, k):
                pe.wait_ge(uT_copied3, j + 1)
                pe.wait_ge(v_done, nn(TILES * j + k - 1))
                mm(ps[:, 3 + k % 2, :], uT[:, k * P:(k + 1) * P], w1_sb[:, :], start=True, stop=True).then_inc(f1_ps, 1)

            def v_transposes(j, k):
                pe.wait_ge(v_done, TILES * j + k + 1)
                pe.wait_ge(vT_copied, nn(TILES * j + k - 1))
                for c in range(FF // P):
                    ins = nc.tensor.transpose(ps[:, 5 + k % 2, c * P:(c + 1) * P], vb[k % 2][:, c * P:(c + 1) * P], ident[:, :])
                ins.then_inc(vT_ps, 1)

            def f2(j, k, p_count):
                pe.wait_ge(vT_copied, TILES * j + k + 1)
                if k == 0:
                    pe.wait_ge(p_done, nn(p_count))
                for c in range(FF // P):
                    ins = mm(ps[:, 7, k * D:(k + 1) * D], vT[k % 2][:, c * P:(c + 1) * P], w2_sb[:, c, :], start=c == 0, stop=c == 3)
                ins.then_inc(f2_ps, 1)

            def hidden(j, mid, p_count):
                f1(j, 0)
                mid()
                f1(j, 1)
                v_transposes(j, 0)
                f1(j, 2)
                v_transposes(j, 1)
                f2(j, 0, p_count)
                f1(j, 3)
                v_transposes(j, 2)
                f2(j, 1, p_count)
                v_transposes(j, 3)
                f2(j, 2, p_count)
                f2(j, 3, p_count)

            o_transposes(0)
            project(0, 0)
            u_transposes(0, 2, u_ready3, uT_copied3, 0, uT_ps3)

            def both(i):
                o_transposes(i)
                hidden(i - 1, lambda: project(i, 2 * i - 1), 2 * i - 1)
                u_transposes(i, 2, u_ready3, uT_copied3, i, uT_ps3)

            both(1)
            with pe.Fori(2, GROUPS) as i:
                both(i)
            hidden(GROUPS - 1, lambda: None, 2 * GROUPS - 1)


_INS = ['x', 'cond_1024', 'L0_cond_Wx', 'L0_cond_Wh', 'L0_cond_b', 'L1_cond_w_q', 'L1_cond_b_q', 'L1_cond_w_k',
        'L1_cond_b_k', 'L1_cond_w_v', 'L1_cond_b_v', 'L1_cond_w_o', 'L1_cond_b_o', 'L1_cond_w_f1', 'L1_cond_b_f1',
        'L1_cond_w_f2', 'L1_cond_b_f2', 'L1_cond_w_ada', 'L1_cond_b_ada']


def kernel(**inputs):
    import numpy as _np
    import concourse.bacc as _bacc
    from concourse import mybir as _mybir
    from concourse.bass_utils import run_bass_kernel_spmd as _run

    nc = _bacc.Bacc("TRN2", target_bir_lowering=False, num_devices=1)
    arrays, args = {}, []
    for name in _INS:
        a = _np.ascontiguousarray(inputs[name])
        arrays[f"in_{name}_dram"] = a
        args.append(nc.dram_tensor(f"in_{name}_dram", a.shape, _mybir.dt.from_np(a.dtype), kind="ExternalInput").ap())
    args.append(nc.dram_tensor("out_0_dram", (N, T, D), F32, kind="ExternalOutput").ap())
    build(nc, *args)
    r = _run(nc, [arrays], core_ids=[0])
    return r.results[0]["out_0_dram"]
```

```python
import math

import numpy as np

import concourse.bass as bass
from concourse import mybir
from contextlib import ExitStack

F32 = mybir.dt.float32
F16 = mybir.dt.float16
I32 = mybir.dt.int32
ALU = mybir.AluOpType
ACT = mybir.ActivationFunctionType
AX = mybir.AxisListType

N, T, D = 32, 128, 128
H, HD = 16, 8
FF = 512
P = 128
TS = P // N
TILES = 4
STEPS = TS * TILES
GROUPS = T // STEPS
GW = TILES * D
NT = GROUPS * TILES
NH3 = 3 * H
VW = HD + 1
ROWG = 4

EPS = 1e-7
EPS2 = EPS * EPS
MAXT = float(np.float32(1.0 - 1e-5))
CLIP = math.atanh(MAXT)
LN_EPS = 1e-6


def _beta(a, b):
    return math.exp(math.lgamma(a) + math.lgamma(b) - math.lgamma(a + b))


BETA_UP = _beta(HD / 2, 0.5) / _beta(D / 2, 0.5)
SCALE = 1.0 / math.sqrt(HD)


def nn(value):
    return max(value, 0) if isinstance(value, int) else value


class Chain:

    def __init__(self, eng, sem):
        self.eng, self.sem, self.base, self.n, self.per = eng, sem, 0, 0, None

    def start(self, step):
        if isinstance(step, int) and step == 0:
            return
        if self.per is None:
            self.per = self.n
        self.base, self.n = self.per * step, 0

    def add(self, ins):
        self.n += 1
        ins.then_inc(self.sem, 1)

    def sync(self):
        self.eng.wait_ge(self.sem, self.base + self.n)

    def link(self, ins):
        self.add(ins)
        self.sync()


def by_pairs(eng, step):
    for u in range(2):
        step(u, u)
    with eng.Fori(1, GROUPS // 2) as i:
        for u in range(2):
            step(2 * i + u, u)


def build(nc, x, cond, Wx, Wh, b, w_q, b_q, w_k, b_k, w_v, b_v, w_o, b_o, w_f1, b_f1, w_f2, b_f2, w_ada, b_ada, out):
    v_dram = nc.dram_tensor("v_scratch", (N, T, H * VW), F32, kind="Internal").ap()
    o_dram = nc.dram_tensor("o_scratch", (N, T, D), F32, kind="Internal").ap()
    ctx = ExitStack()
    with ctx:
        def sb(name, shape, dt=F32):
            return ctx.enter_context(nc.sbuf_tensor(name, shape, dt))

        def sem(name):
            return ctx.enter_context(nc.semaphore(name))

        def tiles(ap):
            return ap.rearrange("p (k d) -> p k d", k=TILES)

        wx_sb, wh_sb, wo_sb = sb("wx_sb", [P, D]), sb("wh_sb", [P, D]), sb("wo_sb", [P, D])
        wqkv_sb = sb("wqkv_sb", [P, 3 * D])
        wada_sb = sb("wada_sb", [P, 6 * D])
        w1_sb = sb("w1_sb", [P, FF])
        w2_sb = sb("w2_sb", [P, FF // P, D])
        b_row = sb("b_row", [1, D])
        bias_row = sb("bias_row", [1, 6 * D + 3 * D + D + FF + D])
        cond_sb = sb("cond_sb", [N, D])
        h0T = sb("h0T", [P, N])
        cond4 = sb("cond4", [P, TS, N])
        ident = sb("ident", [P, P])
        ident16 = sb("ident16", [P, P], F16)
        ones_row = sb("ones_row", [1, GW])
        mask = sb("mask", [P, ROWG])
        ada = sb("ada", [P, 6 * D])
        bqkv = sb("bqkv", [P, 3 * D])
        bo = sb("bo", [P, D])
        b1 = sb("b1", [P, FF])
        b2 = sb("b2", [P, D])

        X1 = sb("X1", [P, GROUPS * GW])
        X2 = sb("X2", [P, GROUPS * GW])
        XN = [sb(f"XN{i}", [P, NT]) for i in range(2)]
        QK = sb("QK", [P, N, 8, T], F16)
        U1 = X2

        S = sb("S", [P, 20, NT])
        SI = sb("SI", [P, 2, NT], I32)
        MV = sb("MV", [P, NT, 2])
        LA, LB = sb("LA", [P, NT]), sb("LB", [P, NT])
        USS, RU = sb("USS", [P, NT]), sb("RU", [P, NT])
        R3 = sb("R3", [P, 3, NT])
        AL, BE = sb("AL", [P, NT]), sb("BE", [P, NT])

        x_st = [sb(f"x_st{i}", [P, TILES, D]) for i in range(2)]
        xT_sb = sb("xT_sb", [P, GW])
        hsT = sb("hsT", [P, STEPS * N])
        st = sb("st", [P, TILES, 6])
        mv = sb("mv", [P, TILES, 2])
        carry = sb("carry", [P, 2])
        U0 = [sb(f"U0{i}", [P, TILES, D]) for i in range(2)]
        SQU = [sb(f"SQU{i}", [P, TILES, D]) for i in range(2)]
        UP = [sb(f"UP{i}", [P, TILES, D]) for i in range(2)]
        uT = [sb(f"uT{i}", [P, GW]) for i in range(2)]
        Tq = [sb(f"Tq{i}", [P, 3, TILES, D]) for i in range(2)]
        SQT = sb("SQT", [P, 3, TILES, D])
        NH = TILES * NH3
        HS = sb("HS", [P, NH + TILES * 3])
        HR = sb("HR", [P, NH + TILES * 3])
        QK12 = [sb(f"QK12{i}", [P, TILES * H, 4, HD], F16) for i in range(2)]
        Vaug = sb("Vaug", [P, TILES, H, VW])

        QKb = [sb(f"QKb{i}", [P, 8, T], F16) for i in range(2)]
        QD = [Tq[i][:, :, :, :].rearrange("p a k d -> p (a k d)").bitcast(F16)[:, 0:4 * ROWG * T]
              .rearrange("p (j g t) -> p j g t", j=4, g=ROWG) for i in range(2)]
        Vb = [sb(f"Vb{i}", [P, H * VW + 32]) for i in range(2)]
        Pb = [sb(f"Pb{i}", [P, 4, ROWG, T]) for i in range(2)]
        OTs = x_st
        rec = [sb(f"rec{i}", [P, H]) for i in range(2)]
        ob = [sb(f"ob{i}", [P, D]) for i in range(2)]

        free = QK[:, :, :, :].rearrange("p n g t -> p (n g t)").bitcast(F32)
        taken = [0]

        def place(width):
            taken[0] += width
            return free[:, taken[0] - width:taken[0]]

        GA = place(GROUPS * GW)
        U3 = place(GROUPS * GW)
        o_ld = [tiles(place(GW)) for _ in range(2)]
        oT = place(GW)
        PA = [tiles(place(GW)) for _ in range(2)]
        SQ3 = [place(3 * GW).rearrange("p (a k d) -> p a k d", a=3, k=TILES) for _ in range(2)]
        TMP = [tiles(place(GW)) for _ in range(2)]
        spare = [Pb[i][:, :, :, :].rearrange("p j g q -> p (j g q)") for i in range(2)]
        vb, vsq, vT = ([spare[i][:, n * FF:(n + 1) * FF] for i in range(2)] for n in range(3))
        YO = [tiles(spare[i][:, 3 * FF:3 * FF + GW]) for i in range(2)]
        ssv = sb("ssv", [P, 2, TILES])
        RV = sb("RV", [P, 6, TILES])

        ps = ctx.enter_context(nc.psum_tensor("ps", [P, 8, 512], F32))

        rnn_w = sem("rnn_w")
        all_w = sem("all_w")
        x_in = sem("x_in")
        pool_const = sem("pool_const")
        pool_chain = sem("pool_chain")
        condT_ps = sem("condT_ps")
        cond_ready = sem("cond_ready")
        ada_ps = sem("ada_ps")
        ada_used = sem("ada_used")
        setup_done = sem("setup_done")
        xT_ps = sem("xT_ps")
        xT_copied = sem("xT_copied")
        xw_ready = sem("xw_ready")
        h_ready = sem("h_ready")
        rnn_mm = sem("rnn_mm")
        hT_ready = sem("hT_ready")
        x1_added = sem("x1_added")
        u0_done = sem("u0_done")
        u_stored = sem("u_stored")
        squ_done = sem("squ_done")
        uss_done = sem("uss_done")
        up_ready = sem("up_ready")
        uT_ps = sem("uT_ps")
        uT_copied = sem("uT_copied")
        qkv_ps = sem("qkv_ps")
        t_done = sem("t_done")
        sqt_done = sem("sqt_done")
        hs_ready = sem("hs_ready")
        hr_ready = sem("hr_ready")
        f_ready = sem("f_ready")
        q1_done = sem("q1_done")
        q2_done = sem("q2_done")
        v_ready = sem("v_ready")
        v_out = sem("v_out")
        d_ps = sem("d_ps")
        d_copied = sem("d_copied")
        s_ps = sem("s_ps")
        p_ready = sem("p_ready")
        pv_ps = sem("pv_ps")
        ot_copied = sem("ot_copied")
        qd_ready = sem("qd_ready")
        o4_ps = sem("o4_ps")
        o_norm = sem("o_norm")
        rec_done = sem("rec_done")
        oT_ps = sem("oT_ps")
        oT_copied = sem("oT_copied")
        wo_ps = sem("wo_ps")
        p_done = sem("p_done")
        ga_ready = sem("ga_ready")
        sqp_ready = sem("sqp_ready")
        sqg_ready = sem("sqg_ready")
        xg_ready = sem("xg_ready")
        r3_done = sem("r3_done")
        na_ready = sem("na_ready")
        th_ready = sem("th_ready")
        ab_ready = sem("ab_ready")
        tmp_ready = sem("tmp_ready")
        x2_done = sem("x2_done")
        u0_done3 = sem("u0_done3")
        u_stored3 = sem("u_stored3")
        squ_done3 = sem("squ_done3")
        uss_done3 = sem("uss_done3")
        up_ready3 = sem("up_ready3")
        uT_ps3 = sem("uT_ps3")
        uT_copied3 = sem("uT_copied3")
        f1_ps = sem("f1_ps")
        v_done = sem("v_done")
        vsq_done = sem("vsq_done")
        vT_ps = sem("vT_ps")
        vT_copied = sem("vT_copied")
        f2_ps = sem("f2_ps")
        p2_done = sem("p2_done")
        ga2_ready = sem("ga2_ready")
        sqp2_ready = sem("sqp2_ready")
        sqg2_ready = sem("sqg2_ready")
        xg2_ready = sem("xg2_ready")
        r32_done = sem("r32_done")
        ab2_ready = sem("ab2_ready")
        tmp2_ready = sem("tmp2_ready")
        y_done = sem("y_done")
        chain_bn = sem("chain_bn")
        chain_small = sem("chain_small")
        chain_front = sem("chain_front")
        chain_heads = sem("chain_heads")
        chain_pool = sem("chain_pool")
        chain_bn3 = sem("chain_bn3")
        chain_small3 = sem("chain_small3")
        chain_front3 = sem("chain_front3")
        chain_rv = sem("chain_rv")
        chain_final = sem("chain_final")
        chain_x2 = sem("chain_x2")
        chain_pool3 = sem("chain_pool3")
        qk_in, v_in, o_out = ([sem(f"{n}{i}") for i in range(2)] for n in ("qk_in", "v_in", "o_out"))
        o_in, y_out = ([sem(f"{n}{i}") for i in range(2)] for n in ("o_in", "y_out"))
        hr_sqrt, low_done = sem("hr_sqrt"), sem("low_done")

        block = ctx.enter_context(nc.Block())

        dram_tile = lambda ap, j, s: ap.rearrange("n (g k s) d -> s n g k d", g=GROUPS, s=TS)[s, :, bass.ds(j, 1), :, :].rearrange("n o k d -> n (o k) d")

        def rows4(ap, width=D):
            return ap.unsqueeze(1).broadcast_to([P, TILES, width])

        def cols(store, j, width):
            return store[:, bass.ds(j * width, width)]

        def per_tile(numbers, j):
            return cols(numbers, j, TILES).unsqueeze(2).broadcast_to([P, TILES, D])

        def heads(par, i):
            return Tq[par][:, i, :, :].rearrange("p k (h d) -> p (k h) d", d=HD)

        @block.sync
        def _(sp):
            def load_x(j, par):
                for s in range(TS):
                    sp.dma_start(x_st[par][s * N:(s + 1) * N, :, :], dram_tile(x, j, s)).then_inc(x_in, 16)

            load_x(0, 0)
            sp.dma_start(wx_sb[:, :], Wx).then_inc(rnn_w, 16)
            sp.dma_start(wh_sb[:, :], Wh).then_inc(rnn_w, 16)
            sp.dma_start(b_row[:, :], b.unsqueeze(0)).then_inc(rnn_w, 16)
            sp.dma_start(cond_sb[:, :], cond).then_inc(rnn_w, 16)
            sp.dma_start(wada_sb[:, :], w_ada).then_inc(all_w, 16)
            for n, w in enumerate((w_q, w_k, w_v)):
                sp.dma_start(wqkv_sb[:, n * D:(n + 1) * D], w).then_inc(all_w, 16)
            at = 0
            for row in (b_ada, b_q, b_k, b_v, b_o, b_f1, b_f2):
                width = row.shape[0]
                sp.dma_start(bias_row[:, at:at + width], row.unsqueeze(0)).then_inc(all_w, 16)
                at += width
            sp.dma_start(wo_sb[:, :], w_o).then_inc(all_w, 16)
            sp.dma_start(w1_sb[:, :], w_f1).then_inc(all_w, 16)
            sp.dma_start(w2_sb[:, :, :], w_f2.rearrange("(c p) d -> p c d", p=P)).then_inc(all_w, 16)
            sp.wait_ge(x_in, 64)
            load_x(1, 1)

            def next_x(j, par):
                sp.wait_ge(x1_added, j)
                sp.wait_ge(x_in, 64 * (j + 1))
                load_x(j + 1, 1 - par)

            next_x(1, 1)
            with sp.Fori(1, GROUPS // 2 - 1) as i:
                for u in range(2):
                    next_x(2 * i + u, u)
            next_x(GROUPS - 2, 0)

            def store_v(j, par):
                sp.wait_ge(v_ready, j + 1)
                for s in range(TS):
                    sp.dma_start(dram_tile(v_dram, j, s),
                                 Vaug[s * N:(s + 1) * N, :, :, :].rearrange("n k h c -> n k (h c)")).then_inc(v_out, 16)

            by_pairs(sp, store_v)

            sp.wait_ge(v_out, 64 * GROUPS)
            sp.wait_ge(d_copied, NT)

            def load_qk(n, par):
                sp.dma_start(QKb[par][:, :, :].rearrange("p g t -> p (g t)"),
                             QK[:, bass.ds(n, 1), :, :].rearrange("p o g t -> p (o g t)")).then_inc(qk_in[par], 16)

            def load_v(n, par):
                sp.dma_start(Vb[par][:, 0:H * VW], v_dram[bass.ds(n, 1), :, :].rearrange("o t c -> (o t) c")).then_inc(v_in[par], 16)

            def store_o(n, par):
                sp.wait_ge(o_norm, n + 1)
                sp.dma_start(o_dram[bass.ds(n, 1), :, :].rearrange("o t d -> (o t) d"), ob[par][:, :]).then_inc(o_out[par], 16)

            for n in range(2):
                load_qk(n, n)
                load_v(n, n)

            def batch(n, par):
                sp.wait_ge(s_ps, 2 * n + 2)
                load_qk(n + 2, par)
                if not (isinstance(n, int) and n == 0):
                    sp.wait_ge(pv_ps, n)
                    load_v(n + 1, 1 - par)
                if not (isinstance(n, int) and n < 2):
                    store_o(n - 2, par)

            batch(0, 0)
            batch(1, 1)
            with sp.Fori(1, N // 2 - 1) as i:
                for u in range(2):
                    batch(2 * i + u, u)
            sp.wait_ge(pv_ps, N - 2)
            load_v(N - 1, 1)
            for n in range(N - 4, N):
                store_o(n, n % 2)

            for par in range(2):
                sp.wait_ge(o_out[par], 16 * (N // 2))

            def load_o(j, par):
                sp.wait_ge(oT_ps, nn(j - 1))
                for s in range(TS):
                    sp.dma_start(o_ld[par][s * N:(s + 1) * N, :, :], dram_tile(o_dram, j, s)).then_inc(o_in[par], 16)

            by_pairs(sp, load_o)

            def store_y(j, par):
                sp.wait_ge(y_done, j + 1)
                for s in range(TS):
                    sp.dma_start(dram_tile(out, j, s), YO[par][s * N:(s + 1) * N, :, :]).then_inc(y_out[par], 16)

            by_pairs(sp, store_y)
            for par in range(2):
                sp.wait_ge(y_out[par], 64 * (GROUPS // 2))

        @block.gpsimd
        def _(pool):
            G = nc.gpsimd
            G.memset(ident[:, :], 0.0).then_inc(pool_chain, 1)
            G.memset(ones_row[:, :], 1.0).then_inc(pool_const, 1)
            G.memset(Vaug[:, :, :, :], 1.0).then_inc(pool_const, 1)
            for i in range(2):
                G.memset(Vb[i][:, :], 0.0).then_inc(pool_const, 1)
            pool.wait_ge(pool_chain, 1)
            G.affine_select(out=ident[:, :], in_=ident[:, :], compare_op=ALU.not_equal, fill=1.0, base=0,
                            pattern=[[-1, P]], channel_multiplier=1).then_inc(pool_chain, 1)
            pool.wait_ge(pool_chain, 2)
            G.tensor_copy(ident16[:, :], ident[:, :]).then_inc(pool_const, 1)
            pool.wait_ge(setup_done, 1)

            def modulate(j, par, store, c0, from_ln, chain, stored, squared):
                pool.wait_ge(from_ln, j + 1)
                chain.start(j)
                chain.link(G.tensor_tensor(U0[par][:, :, :], U0[par][:, :, :], rows4(ada[:, c0 + D:c0 + 2 * D]), ALU.mult))
                G.tensor_tensor(tiles(cols(store, j, GW)), U0[par][:, :, :], rows4(ada[:, c0:c0 + D]), ALU.add).then_inc(stored, 1)

            chain1 = Chain(pool, chain_pool)
            by_pairs(pool, lambda j, par: modulate(j, par, U1, 0, u0_done, chain1, u_stored, squ_done))

            def scale_v(j, par):
                pool.wait_ge(hr_ready, j + 1)
                pool.wait_ge(v_out, 64 * j)
                f = HS[:, 2 * TILES * H:NH].unsqueeze(2).broadcast_to([P, TILES * H, HD])
                G.tensor_tensor(Vaug[:, :, :, 0:HD].rearrange("p k h d -> p (k h) d"), heads(par, 2), f, ALU.mult).then_inc(v_ready, 1)

            by_pairs(pool, scale_v)

            def gated(j, par):
                pool.wait_ge(p_done, j + 1)
                G.tensor_tensor(tiles(cols(GA, j, GW)), PA[par][:, :, :], rows4(ada[:, 2 * D:3 * D]), ALU.mult).then_inc(ga_ready, 1)
                pool.wait_ge(ga_ready, j + 1)
                pool.wait_ge(r3_done, nn(j - 1))
                G.tensor_tensor(SQ3[par][:, 2, :, :], tiles(cols(GA, j, GW)), tiles(cols(X1, j, GW)), ALU.mult).then_inc(xg_ready, 1)

            by_pairs(pool, gated)

            pool.wait_ge(ab_ready, 1)

            def update(j, par):
                pool.wait_ge(x2_done, nn(j - 1))
                G.tensor_tensor(TMP[par][:, :, :], tiles(cols(GA, j, GW)), per_tile(BE, j), ALU.mult).then_inc(tmp_ready, 1)

            by_pairs(pool, update)
            chain3 = Chain(pool, chain_pool3)
            by_pairs(pool, lambda j, par: modulate(j, par, U3, 3 * D, u0_done3, chain3, u_stored3, squ_done3))

            def gated2(j, par):
                pool.wait_ge(p2_done, j + 1)
                G.tensor_tensor(tiles(cols(GA, j, GW)), PA[par][:, :, :], rows4(ada[:, 5 * D:6 * D]), ALU.mult).then_inc(ga2_ready, 1)
                pool.wait_ge(ga2_ready, j + 1)
                pool.wait_ge(r32_done, nn(j - 1))
                G.tensor_tensor(SQ3[par][:, 2, :, :], tiles(cols(GA, j, GW)), tiles(cols(X2, j, GW)), ALU.mult).then_inc(xg2_ready, 1)

            by_pairs(pool, gated2)

            pool.wait_ge(ab2_ready, 1)

            def update2(j, par):
                pool.wait_ge(y_done, nn(j - 1))
                G.tensor_tensor(TMP[par][:, :, :], tiles(cols(GA, j, GW)), per_tile(BE, j), ALU.mult).then_inc(tmp2_ready, 1)

            by_pairs(pool, update2)

        @block.scalar
        def _(act):
            A = nc.scalar

            def copy_xT(j):
                act.wait_ge(xT_ps, j + 1)
                act.wait_ge(xw_ready, j)
                A.activation(xT_sb[:, :], ps[:, 4, :], ACT.Copy).then_inc(xT_copied, 1)

            def group(i, par, last=False):
                for s in range(STEPS):
                    act.wait_ge(rnn_mm, STEPS * i + s + 1)
                    A.activation(hsT[:, s * N:(s + 1) * N], ps[:, par, s * N:(s + 1) * N], ACT.Tanh).then_inc(h_ready, 1)
                    if s == 2 and not last:
                        copy_xT(i + 1)

            copy_xT(0)
            group(0, 0)
            group(1, 1)
            with act.Fori(1, GROUPS // 2 - 1) as i:
                for u in range(2):
                    group(2 * i + u, u)
            group(GROUPS - 2, 0)
            group(GROUPS - 1, 1, last=True)

            def square_u(j, par, store, stored, summed, squared):
                act.wait_ge(stored, j + 1)
                act.wait_ge(summed, nn(j - 1))
                A.activation(SQU[par][:, :, :], tiles(cols(store, j, GW)), ACT.Square).then_inc(squared, 1)

            by_pairs(act, lambda j, par: square_u(j, par, U1, u_stored, uss_done, squ_done))

            def copy_uT(j, par, bank, done, readers, count, copied):
                act.wait_ge(done, j + 1)
                act.wait_ge(readers, nn(count))
                A.activation(uT[par][:, :], ps[:, bank, :], ACT.Copy).then_inc(copied, 1)

            def copy_d(j, k):
                act.wait_ge(d_ps, TILES * j + k + 1)
                src = ps[:, 6 + k % 2, :].bitcast(F16).rearrange("p (g s n) -> p g s n", g=8, s=TS)
                dst = QK[:, :, :, bass.ds(STEPS * j + TS * k, TS)].rearrange("p n g s -> p g s n")
                A.activation(dst, src, ACT.Copy).then_inc(d_copied, 1)

            def project(j, par):
                copy_uT(j, par, par, uT_ps, qkv_ps, TILES * (j - 1), uT_copied)
                for k in range(TILES):
                    act.wait_ge(t_done, TILES * j + k + 1)
                    if k == 0:
                        act.wait_ge(hs_ready, j)
                    A.activation(SQT[:, :, k, :], Tq[par][:, :, k, :], ACT.Square).then_inc(sqt_done, 1)
                lag = not (isinstance(j, int) and j == 0)
                if lag:
                    copy_d(j - 1, 0)
                    copy_d(j - 1, 1)
                act.wait_ge(hs_ready, j + 1)
                A.activation(HR[:, :], HS[:, :], ACT.Sqrt).then_inc(hr_sqrt, 1)
                if lag:
                    copy_d(j - 1, 2)
                    copy_d(j - 1, 3)
                act.wait_ge(f_ready, j + 1)
                act.wait_ge(d_ps, TILES * j)
                for i in range(2):
                    A.activation(QK12[i][:, :, 0, :], heads(par, i), ACT.Copy).then_inc(q1_done, 1)

            by_pairs(act, project)
            for k in range(TILES):
                copy_d(GROUPS - 1, k)

            def exps(n, par):
                for hf in range(2):
                    act.wait_ge(s_ps, 2 * n + hf + 1)
                    act.wait_ge(pv_ps, nn(n - 1))
                    A.activation(Pb[par][:, 2 * hf:2 * hf + 2, :, :].rearrange("p j g q -> p (j g q)"),
                                 ps[:, 2 * hf:2 * hf + 2, :].rearrange("p j c -> p (j c)"),
                                 ACT.Exp, scale=SCALE).then_inc(p_ready, 1)

            exps(0, 0)
            exps(1, 1)
            with act.Fori(1, N // 2) as i:
                for u in range(2):
                    exps(2 * i + u, u)

            def squares(j, par, p_sem, sqp, ga_sem, sqg, summed):
                act.wait_ge(p_sem, j + 1)
                act.wait_ge(summed, nn(j - 1))
                A.activation(SQ3[par][:, 0, :, :], PA[par][:, :, :], ACT.Square).then_inc(sqp, 1)
                act.wait_ge(ga_sem, j + 1)
                A.activation(SQ3[par][:, 1, :, :], tiles(cols(GA, j, GW)), ACT.Square).then_inc(sqg, 1)

            def after_attention(j, par):
                act.wait_ge(oT_ps, j + 1)
                act.wait_ge(wo_ps, j)
                A.activation(oT[:, :], ps[:, 0, :], ACT.Copy).then_inc(oT_copied, 1)
                if not (isinstance(j, int) and j == 0):
                    squares(j - 1, 1 - par, p_done, sqp_ready, ga_ready, sqg_ready, r3_done)

            by_pairs(act, after_attention)
            squares(GROUPS - 1, 1, p_done, sqp_ready, ga_ready, sqg_ready, r3_done)

            def tanh(n):
                act.wait_ge(na_ready, n)
                A.activation(S[:, 5, :], S[:, 4, :], ACT.Tanh).then_inc(th_ready, 1)

            tanh(1)
            by_pairs(act, lambda j, par: square_u(j, par, U3, u_stored3, uss_done3, squ_done3))

            def square_v(j, par, k):
                act.wait_ge(v_done, TILES * j + k + 1)
                A.activation(vsq[k % 2], vb[k % 2], ACT.Square, accum_out=ssv[:, par, k:k + 1]).then_inc(vsq_done, 1)

            def copy_vT(j, k):
                act.wait_ge(vT_ps, TILES * j + k + 1)
                act.wait_ge(f2_ps, nn(TILES * j + k - 1))
                A.activation(vT[k % 2], ps[:, 5 + k % 2, :], ACT.Copy).then_inc(vT_copied, 1)

            def hidden(j, par):
                lag = not (isinstance(j, int) and j == 0)
                if lag:
                    copy_vT(j - 1, 3)
                copy_uT(j, par, 0, uT_ps3, f1_ps, TILES * (j - 1), uT_copied3)
                square_v(j, par, 0)
                square_v(j, par, 1)
                copy_vT(j, 0)
                copy_vT(j, 1)
                square_v(j, par, 2)
                copy_vT(j, 2)
                square_v(j, par, 3)
                if lag:
                    squares(j - 1, 1 - par, p2_done, sqp2_ready, ga2_ready, sqg2_ready, r32_done)

            by_pairs(act, hidden)
            copy_vT(GROUPS - 1, 3)
            squares(GROUPS - 1, 1, p2_done, sqp2_ready, ga2_ready, sqg2_ready, r32_done)
            tanh(2)

        @block.vector
        def _(dve):
            V = nc.vector
            small = Chain(dve, chain_small)

            small.link(V.memset(mask[:, :], 0.0))
            for g in range(ROWG):
                small.link(V.memset(mask[32 * g:32 * g + 32, g:g + 1], 1.0))
            dve.wait_ge(condT_ps, 1)
            V.tensor_copy(h0T[:, :], ps[:, 2, 0:N]).then_inc(h_ready, 1)
            V.tensor_copy(cond4[:, :, :], ps[:, 2, 0:N].unsqueeze(1).broadcast_to([P, TS, N])).then_inc(cond_ready, 1)
            dve.wait_ge(ada_ps, 1)
            V.tensor_copy(ada[:, 0:3 * D], ps[:, 5, 0:3 * D]).then_inc(ada_used, 1)
            dve.wait_ge(ada_ps, 2)
            V.tensor_copy(ada[:, 3 * D:6 * D], ps[:, 6, 0:3 * D]).then_inc(ada_used, 1)
            dve.wait_ge(ada_used, 2)
            for c in (D, 4 * D):
                V.tensor_scalar_add(ada[:, c:c + D], ada[:, c:c + D], 1.0).then_inc(ada_used, 1)
            dve.wait_ge(ada_ps, 3)
            V.tensor_copy(bqkv[:, :], ps[:, 7, 0:3 * D]).then_inc(ada_used, 1)
            dve.wait_ge(ada_ps, 4)
            V.tensor_copy(b1[:, :], ps[:, 3, :]).then_inc(ada_used, 1)
            dve.wait_ge(ada_ps, 5)
            V.tensor_copy(bo[:, :], ps[:, 5, 0:D]).then_inc(ada_used, 1)
            V.tensor_copy(b2[:, :], ps[:, 5, D:2 * D]).then_inc(ada_used, 1)
            dve.wait_ge(ada_used, 8)
            V.memset(carry[:, :], 0.0).then_inc(setup_done, 1)
            dve.wait_ge(setup_done, 1)

            def statistics(store, j, chain):
                for k in range(TILES):
                    chain.add(V.bn_stats(st[:, k, :], store[:, bass.ds(j * GW + k * D, D)]))
                chain.sync()
                V.memset(carry[:, 1:2], 0.0)
                for k in range(TILES):
                    chain.add(V.bn_aggr(mv[:, k, :], st[:, k, :]))
                chain.sync()
                chain.link(V.tensor_copy(MV[:, bass.ds(TILES * j, TILES), :], mv[:, :, :]))

            def states(j, par):
                bn.start(j)
                dve.wait_ge(hT_ready, j + 1)
                V.tensor_tensor(tiles(cols(X1, j, GW)), x_st[par][:, :, :], tiles(ps[:, 2, :]), ALU.add).then_inc(x1_added, 1)
                dve.wait_ge(x1_added, j + 1)
                V.memset(carry[:, 0:1], 0.0)
                statistics(X1, j, bn)

            bn = Chain(dve, chain_bn)
            by_pairs(dve, states)

            def rsqrt(dst, src, xh, w, chain):
                chain.add(V.tensor_scalar(xh, src, -0.5, None, ALU.mult))
                chain.link(V.tensor_scalar(dst.bitcast(I32), src.bitcast(I32), -0.5, 1597463007.0, ALU.mult, ALU.add))
                for _ in range(3):
                    chain.link(V.tensor_tensor(w, dst, dst, ALU.mult))
                    chain.link(V.tensor_tensor(w, w, xh, ALU.mult))
                    chain.link(V.scalar_tensor_tensor(dst, w, 1.5, dst, ALU.add, ALU.mult))

            def row(i):
                return S[:, i, :]

            def ln_coefficients(xn, link, add):
                mean, var = MV[:, :, 0], MV[:, :, 1]
                link(V.tensor_tensor(row(6), mean, mean, ALU.mult))
                link(V.tensor_tensor(row(7), row(6), var, ALU.add))
                add(V.tensor_scalar(xn[:, :], row(7), float(D), None, ALU.mult))
                link(V.tensor_scalar(row(0), row(7), float(D), EPS2, ALU.mult, ALU.max))
                rsqrt(row(9), row(0), row(6), row(7), small)
                link(V.tensor_tensor(row(1), row(0), row(9), ALU.mult))
                link(V.tensor_scalar(row(8), row(1), EPS, MAXT, ALU.max, ALU.min))
                z = row(8)
                link(V.tensor_scalar(row(7), z, -1.0, 1.0, ALU.mult, ALU.add))
                link(V.reciprocal(row(10), row(7)))
                link(V.scalar_tensor_tensor(row(11), z, 1.0, row(10), ALU.add, ALU.mult))
                y, yi = row(11), row(11).bitcast(I32)
                add(V.tensor_scalar(SI[:, 0, :], yi, 23, None, ALU.logical_shift_right))
                add(V.tensor_scalar(row(12), y, 2.0, None, ALU.is_ge))
                link(V.tensor_scalar(SI[:, 1, :], yi, 0x7FFFFF, 0x3F800000, ALU.bitwise_and, ALU.bitwise_or))
                m = SI[:, 1, :].bitcast(F32)
                add(V.tensor_scalar(row(13), SI[:, 0, :], -127.0, None, ALU.add))
                link(V.tensor_scalar(row(6), m, 1.0, None, ALU.add))
                link(V.reciprocal(row(7), row(6)))
                link(V.scalar_tensor_tensor(row(6), m, -1.0, row(7), ALU.add, ALU.mult))
                link(V.tensor_tensor(row(7), row(6), z, ALU.subtract))
                link(V.tensor_tensor(row(6), row(7), row(12), ALU.mult))
                link(V.tensor_tensor(row(10), row(6), z, ALU.add))
                w = row(10)
                link(V.tensor_tensor(row(11), w, w, ALU.mult))
                w2 = row(11)
                link(V.tensor_scalar(row(6), w2, 1.0 / 15, None, ALU.mult))
                at, to = 6, 7
                for k in (13, 11, 9, 7, 5, 3):
                    link(V.scalar_tensor_tensor(row(to), row(at), 1.0 / k, w2, ALU.add, ALU.mult))
                    at, to = to, at
                link(V.scalar_tensor_tensor(row(to), row(at), 1.0, w, ALU.add, ALU.mult))
                at, to = to, at
                link(V.scalar_tensor_tensor(row(to), row(13), 0.5 * math.log(2.0), row(at), ALU.mult, ALU.add))
                link(V.tensor_tensor(row(12), row(to), row(9), ALU.mult))
                link(V.tensor_tensor(row(6), row(12), row(12), ALU.mult))
                link(V.tensor_tensor(row(7), row(6), var, ALU.mult))
                link(V.tensor_scalar(row(14), row(7), LN_EPS, None, ALU.add))
                rsqrt(row(15), row(14), row(6), row(7), small)
                link(V.tensor_tensor(LA[:, :], row(12), row(15), ALU.mult))
                link(V.tensor_tensor(LB[:, :], LA[:, :], mean, ALU.mult))

            def normalise(j, par, src, chain, stored, squared, out_sem, summed):
                def front(j, par):
                    chain.start(j)
                    dve.wait_ge(stored, nn(j - 1))
                    chain.link(V.tensor_tensor(U0[par][:, :, :], tiles(cols(src, j, GW)), per_tile(LA, j), ALU.mult))
                    V.tensor_tensor(U0[par][:, :, :], U0[par][:, :, :], per_tile(LB, j), ALU.subtract).then_inc(out_sem, 1)

                front(j, par)
                if not (isinstance(j, int) and j == 0):
                    sum_u(j - 1, 1 - par, squared, summed)

            def sum_u(j, par, squared, summed):
                dve.wait_ge(squared, j + 1)
                V.reduce_sum(cols(USS, j, TILES), SQU[par][:, :, :], AX.X).then_inc(summed, 1)

            def clip_factors(dst, ss):
                small.link(V.tensor_scalar(row(0), ss, EPS2, None, ALU.max))
                rsqrt(row(1), row(0), row(6), row(7), small)
                small.link(V.tensor_scalar(dst, row(1), CLIP, 1.0, ALU.mult, ALU.min))

            ln_coefficients(XN[0], small.link, small.add)
            front1 = Chain(dve, chain_front)
            by_pairs(dve, lambda j, par: normalise(j, par, X1, front1, u_stored, squ_done, u0_done, uss_done))
            sum_u(GROUPS - 1, 1, squ_done, uss_done)
            dve.wait_ge(uss_done, GROUPS)
            clip_factors(RU[:, :], USS[:, :])

            def low_parts(j, par):
                dve.wait_ge(q1_done, 2 * j + 2)
                for i in range(2):
                    low = QK12[i][:, :, 1 + i, :]
                    V.tensor_tensor(low, heads(par, i), QK12[i][:, :, 0, :], ALU.subtract).then_inc(low_done, 1)
                dve.wait_ge(low_done, 2 * j + 2)
                V.tensor_copy(QK12[0][:, :, 2:4, :].rearrange("p h b d -> p h (b d)"),
                              QK12[0][:, :, 0:2, :].rearrange("p h b d -> p h (b d)"))
                V.tensor_copy(QK12[1][:, :, 1, :], QK12[1][:, :, 0, :])
                V.tensor_copy(QK12[1][:, :, 3, :], QK12[1][:, :, 2, :]).then_inc(q2_done, 1)

            hd = Chain(dve, chain_heads)

            def project(j, par):
                hd.start(j)
                dve.wait_ge(uT_ps, nn(j - 1))
                V.tensor_tensor(UP[par][:, :, :], tiles(cols(U1, j, GW)), per_tile(RU, j), ALU.mult).then_inc(up_ready, 1)
                if not (isinstance(j, int) and j == 0):
                    low_parts(j - 1, 1 - par)
                for k in range(TILES):
                    dve.wait_ge(qkv_ps, TILES * j + k + 1)
                    if k == 0:
                        dve.wait_ge(v_ready, nn(j - 1))
                        dve.wait_ge(q2_done, nn(j - 1))
                    V.tensor_tensor(Tq[par][:, :, k, :], ps[:, 2 + k, 0:3 * D].rearrange("p (a d) -> p a d", a=3),
                                    bqkv[:, :].rearrange("p (a d) -> p a d", a=3), ALU.add).then_inc(t_done, 1)
                dve.wait_ge(sqt_done, TILES * (j + 1))
                dve.wait_ge(v_ready, j)
                hs, tot = HS[:, 0:NH], HS[:, NH:]
                hd.link(V.reduce_sum(hs, SQT[:, :, :, :].rearrange("p a k (h d) -> p (a k h) d", d=HD), AX.X))
                hd.link(V.reduce_sum(tot, hs.rearrange("p (a h) -> p a h", h=H), AX.X))
                V.tensor_scalar(HS[:, :], HS[:, :], EPS2, None, ALU.max).then_inc(hs_ready, 1)
                dve.wait_ge(hr_sqrt, j + 1)
                rh, rt = HR[:, 0:NH], HR[:, NH:]
                hd.add(V.tensor_scalar(rh, rh, 1.0 / CLIP, None, ALU.mult))
                hd.link(V.tensor_scalar(rt, rt, 1.0 / CLIP, 1.0, ALU.mult, ALU.max))
                hd.link(V.tensor_scalar(rt, rt, 1.0 / BETA_UP, None, ALU.mult))
                hd.link(V.tensor_tensor(rh.rearrange("p (a h) -> p a h", h=H), rh.rearrange("p (a h) -> p a h", h=H),
                                        rt.unsqueeze(2).broadcast_to([P, 3 * TILES, H]), ALU.max))
                V.reciprocal(hs, rh).then_inc(hr_ready, 1)
                dve.wait_ge(hr_ready, j + 1)
                f = hs[:, 0:2 * TILES * H].unsqueeze(2).broadcast_to([P, 2 * TILES * H, HD])
                t = Tq[par][:, 0:2, :, :].rearrange("p a k (h d) -> p (a k h) d", d=HD)
                V.tensor_tensor(t, t, f, ALU.mult).then_inc(f_ready, 1)

            by_pairs(dve, project)
            low_parts(GROUPS - 1, 1)

            def mask_q(n, par, loads):
                dve.wait_ge(qk_in[par], 16 * loads)
                dve.wait_ge(s_ps, nn(2 * n - 2))
                for g in range(ROWG):
                    ins = V.tensor_scalar(QD[par][:, :, g, :], QKb[par][:, 0:4, :], mask[:, g:g + 1], None, ALU.mult)
                ins.then_inc(qd_ready, 1)

            def evacuate(n, par):
                dve.wait_ge(pv_ps, n + 1)
                V.tensor_copy(OTs[par][:, :, :], ps[:, 4, :].rearrange("p (j q) -> p j q", j=4)).then_inc(ot_copied, 1)

            def normal(n, par, sent):
                dve.wait_ge(o4_ps, n + 1)
                o4 = ps[:, 5 + par, :].rearrange("p (h c) -> p h c", c=32)
                V.reciprocal(rec[par][:, :], o4[:, :, HD]).then_inc(rec_done, 1)
                dve.wait_ge(rec_done, n + 1)
                dve.wait_ge(o_out[par], 16 * sent)
                V.scalar_tensor_tensor(ob[par][:, :].rearrange("p (h d) -> p h d", d=HD), o4[:, :, 0:HD], 1.0 / BETA_UP,
                                       rec[par][:, :].unsqueeze(2).broadcast_to([P, H, HD]), ALU.mult, ALU.mult).then_inc(o_norm, 1)

            mask_q(0, 0, 1)
            mask_q(1, 1, 1)
            evacuate(0, 0)

            def batch(i, u):
                n = 2 * i + u
                mask_q(n + 2, u, i + 2)
                evacuate(n + 1, 1 - u)
                normal(n, u, i)

            batch(0, 0)
            batch(0, 1)
            with dve.Fori(1, N // 2 - 1) as i:
                for u in range(2):
                    batch(i, u)
            evacuate(N - 1, 1)
            normal(N - 2, 0, N // 2 - 1)
            normal(N - 1, 1, N // 2 - 1)

            def sum3(j, par, sqp, sqg, xg, done):
                dve.wait_ge(sqp, j + 1)
                dve.wait_ge(sqg, j + 1)
                dve.wait_ge(xg, j + 1)
                V.reduce_sum(R3[:, :, bass.ds(TILES * j, TILES)], SQ3[par][:, :, :, :], AX.X).then_inc(done, 1)

            def mobius(xn, n, ready):
                link, add = small.link, small.add
                link(V.tensor_scalar(row(0), R3[:, 0, :], EPS2, None, ALU.max))
                rsqrt(row(1), row(0), row(6), row(7), small)
                link(V.tensor_scalar(row(8), row(1), CLIP, 1.0, ALU.mult, ALU.min))
                rp = row(8)
                link(V.tensor_tensor(row(7), rp, rp, ALU.mult))
                link(V.tensor_tensor(row(2), row(7), R3[:, 1, :], ALU.mult))
                sa = row(2)
                link(V.tensor_scalar(row(3), sa, EPS2, None, ALU.max))
                rsqrt(row(9), row(3), row(6), row(7), small)
                V.tensor_tensor(row(4), row(3), row(9), ALU.mult).then_inc(na_ready, 1)
                dve.wait_ge(th_ready, n)
                link(V.tensor_tensor(row(10), row(5), row(9), ALU.mult))
                tau = row(10)
                add(V.tensor_tensor(row(11), tau, tau, ALU.mult))
                link(V.tensor_tensor(row(12), tau, rp, ALU.mult))
                tr = row(12)
                add(V.tensor_tensor(row(13), row(11), sa, ALU.mult))
                link(V.tensor_tensor(row(14), tr, R3[:, 2, :], ALU.mult))
                y2 = row(13)
                add(V.tensor_scalar(row(15), row(14), 2.0, 1.0, ALU.mult, ALU.add))
                link(V.tensor_tensor(row(16), xn, y2, ALU.mult))
                add(V.tensor_scalar(row(17), xn, -1.0, 1.0, ALU.mult, ALU.add))
                link(V.tensor_tensor(row(6), row(16), row(15), ALU.add))
                add(V.tensor_tensor(row(18), row(15), y2, ALU.add))
                link(V.tensor_scalar(row(7), row(6), EPS, None, ALU.max))
                link(V.reciprocal(row(6), row(7)))
                add(V.tensor_tensor(AL[:, :], row(18), row(6), ALU.mult))
                link(V.tensor_tensor(row(7), row(17), row(6), ALU.mult))
                V.tensor_tensor(BE[:, :], row(7), tr, ALU.mult).then_inc(ready, 1)
                dve.wait_ge(ready, 1)

            def after_attention(j, par):
                dve.wait_ge(wo_ps, j + 1)
                V.tensor_tensor(PA[par][:, :, :], tiles(ps[:, 1 + par, :]), rows4(bo[:, :]), ALU.add).then_inc(p_done, 1)
                if not (isinstance(j, int) and j == 0):
                    sum3(j - 1, 1 - par, sqp_ready, sqg_ready, xg_ready, r3_done)

            by_pairs(dve, after_attention)
            sum3(GROUPS - 1, 1, sqp_ready, sqg_ready, xg_ready, r3_done)
            dve.wait_ge(r3_done, GROUPS)
            mobius(XN[0][:, :], 1, ab_ready)

            x2c = Chain(dve, chain_x2)
            bn3 = Chain(dve, chain_bn3)

            def new_x(j, par):
                x2c.start(j)
                bn3.start(j)
                x2c.link(V.tensor_tensor(U0[par][:, :, :], tiles(cols(X1, j, GW)), per_tile(AL, j), ALU.mult))
                dve.wait_ge(tmp_ready, j + 1)
                V.tensor_tensor(tiles(cols(X2, j, GW)), U0[par][:, :, :], TMP[par][:, :, :], ALU.add).then_inc(x2_done, 1)
                dve.wait_ge(x2_done, j + 1)
                V.memset(carry[:, 0:1], 0.0)
                statistics(X2, j, bn3)

            by_pairs(dve, new_x)
            small3 = Chain(dve, chain_small)
            ln_coefficients(XN[1], small.link, small.add)
            front3 = Chain(dve, chain_front3)
            by_pairs(dve, lambda j, par: normalise(j, par, X2, front3, u_stored3, squ_done3, u0_done3, uss_done3))
            sum_u(GROUPS - 1, 1, squ_done3, uss_done3)
            dve.wait_ge(uss_done3, GROUPS)
            clip_factors(RU[:, :], USS[:, :])

            def v_tile(j, k):
                dve.wait_ge(f1_ps, TILES * j + k + 1)
                dve.wait_ge(vsq_done, nn(TILES * j + k - 1))
                dve.wait_ge(vT_ps, nn(TILES * j + k - 1))
                V.tensor_tensor(vb[k % 2], ps[:, 3 + k % 2, :], b1[:, :], ALU.add).then_inc(v_done, 1)

            rvc = Chain(dve, chain_rv)

            def second(j, par):
                rvc.start(j)
                dve.wait_ge(vsq_done, TILES * (j + 1))
                rvc.link(V.tensor_scalar(RV[:, 0, :], ssv[:, par, :], EPS2, None, ALU.max))
                rsqrt(RV[:, 1, :], RV[:, 0, :], RV[:, 2, :], RV[:, 3, :], rvc)
                rvc.link(V.tensor_scalar(RV[:, 4, :], RV[:, 1, :], CLIP, 1.0, ALU.mult, ALU.min))
                dve.wait_ge(f2_ps, TILES * (j + 1))
                for k in range(TILES):
                    ins = V.scalar_tensor_tensor(PA[par][:, k, :], ps[:, 7 - 5 * par, k * D:(k + 1) * D], RV[:, 4, k:k + 1], b2[:, :],
                                                 ALU.mult, ALU.add)
                ins.then_inc(p2_done, 1)

            def hidden(j, par):
                dve.wait_ge(uT_ps3, nn(j - 1))
                V.tensor_tensor(UP[par][:, :, :], tiles(cols(U3, j, GW)), per_tile(RU, j), ALU.mult).then_inc(up_ready3, 1)
                v_tile(j, 0)
                v_tile(j, 1)
                lag = not (isinstance(j, int) and j == 0)
                if lag:
                    second(j - 1, 1 - par)
                v_tile(j, 2)
                v_tile(j, 3)
                if lag:
                    sum3(j - 1, 1 - par, sqp2_ready, sqg2_ready, xg2_ready, r32_done)

            by_pairs(dve, hidden)
            second(GROUPS - 1, 1)
            sum3(GROUPS - 1, 1, sqp2_ready, sqg2_ready, xg2_ready, r32_done)
            dve.wait_ge(r32_done, GROUPS)
            mobius(XN[1][:, :], 2, ab2_ready)

            fin = Chain(dve, chain_final)

            def final(j, par, sent):
                fin.start(j)
                fin.link(V.tensor_tensor(U0[par][:, :, :], tiles(cols(X2, j, GW)), per_tile(AL, j), ALU.mult))
                fin.link(V.tensor_tensor(U0[par][:, :, :], U0[par][:, :, :], tiles(cols(X1, j, GW)), ALU.add))
                dve.wait_ge(tmp2_ready, j + 1)
                dve.wait_ge(y_out[par], 64 * sent)
                V.tensor_tensor(YO[par][:, :, :], U0[par][:, :, :], TMP[par][:, :, :], ALU.add).then_inc(y_done, 1)

            final(0, 0, 0)
            final(1, 1, 0)
            with dve.Fori(1, GROUPS // 2) as i:
                for u in range(2):
                    final(2 * i + u, u, i)

        @block.tensor
        def _(pe):
            mm = nc.tensor.matmul
            turn = nc.tensor.transpose

            def x_transposes(j, par):
                pe.wait_ge(x_in, 64 * (j + 1))
                pe.wait_ge(xT_copied, j)
                for k in range(TILES):
                    ins = turn(ps[:, 4, k * P:(k + 1) * P], x_st[par][:, k, :], ident[:, :])
                ins.then_inc(xT_ps, 1)

            def x_products(j, par):
                pe.wait_ge(xT_copied, j + 1)
                mm(ps[:, par, :], wx_sb[:, :], xT_sb[:, :], start=True, stop=False, skip_group_check=True)
                mm(ps[:, par, :], b_row[:, :], ones_row[:, :], start=False, stop=False, skip_group_check=True).then_inc(xw_ready, 1)

            def rnn_step(i, s, par):
                pe.wait_ge(h_ready, STEPS * i + s + 1)
                rhs = hsT[:, (s - 1) * N:s * N] if s else (hsT[:, (STEPS - 1) * N:] if not (isinstance(i, int) and i == 0) else h0T[:, :])
                mm(ps[:, par, s * N:(s + 1) * N], wh_sb[:, :], rhs, start=False, stop=s == STEPS - 1,
                   skip_group_check=True).then_inc(rnn_mm, 1)

            def h_transpose(i, k):
                if k == 0:
                    pe.wait_ge(x1_added, i)
                ins = turn(ps[:, 2, k * P:(k + 1) * P], hsT[:, k * P:(k + 1) * P], ident[:, :])
                if k == TILES - 1:
                    ins.then_inc(hT_ready, 1)

            pe.wait_ge(pool_const, 5)
            pe.wait_ge(pool_chain, 2)
            pe.wait_ge(rnn_w, 64)
            turn(ps[:, 2, 0:N], cond_sb[:, :], ident[0:N, 0:N]).then_inc(condT_ps, 1)
            x_transposes(0, 0)
            x_products(0, 0)

            def setup(part):
                rows = {"qkv": 6 * D, "o": 9 * D, "f1": 10 * D, "f2": 10 * D + FF}

                def spread(bank, c0, at, width):
                    return mm(ps[:, bank, c0:c0 + width], ones_row[:, 0:P], bias_row[:, at:at + width], start=True, stop=True)

                if part == 0:
                    pe.wait_ge(all_w, 14 * 16)
                    pe.wait_ge(cond_ready, 1)
                if part < 2:
                    c = part * 3 * D
                    mm(ps[:, 5 + part, 0:3 * D], cond4[:, :, :].rearrange("p s n -> p (s n)"), wada_sb[:, c:c + 3 * D], start=True, stop=False)
                    mm(ps[:, 5 + part, 0:3 * D], ones_row[:, 0:P], bias_row[:, c:c + 3 * D], start=False, stop=True).then_inc(ada_ps, 1)
                if part == 2:
                    spread(7, 0, rows["qkv"], 3 * D).then_inc(ada_ps, 1)
                if part == 3:
                    spread(3, 0, rows["f1"], FF).then_inc(ada_ps, 1)
                if part == 4:
                    pe.wait_ge(ada_used, 1)
                    spread(5, 0, rows["o"], D)
                    spread(5, D, rows["f2"], D).then_inc(ada_ps, 1)

            def group(i, par, last=False):
                first = isinstance(i, int) and i == 0
                for s in range(STEPS):
                    rnn_step(i, s, par)
                    if s == 0 and not first:
                        h_transpose(i - 1, TILES - 1)
                    if s % TS == 0 and s:
                        h_transpose(i, s // TS - 1)
                    if s == 1 and not last:
                        x_transposes(i + 1, 1 - par)
                    if s == 9 and not last:
                        x_products(i + 1, 1 - par)
                    if first and s in (2, 3, 5, 6, 7):
                        setup((2, 3, 5, 6, 7).index(s))

            group(0, 0)
            group(1, 1)
            with pe.Fori(1, GROUPS // 2 - 1) as i:
                for u in range(2):
                    group(2 * i + u, u)
            group(GROUPS - 2, 0)
            group(GROUPS - 1, 1, last=True)
            pe.wait_ge(h_ready, STEPS * GROUPS + 1)
            h_transpose(GROUPS - 1, TILES - 1)

            def u_transposes(j, par, bank, ready, copied, copies, done):
                pe.wait_ge(ready, j + 1)
                pe.wait_ge(copied, nn(copies))
                for k in range(TILES):
                    ins = turn(ps[:, bank, k * P:(k + 1) * P], UP[par][:, k, :], ident[:, :])
                ins.then_inc(done, 1)

            def split_transposes(j, k):
                if k == 0:
                    pe.wait_ge(q2_done, j + 1)
                pe.wait_ge(d_copied, nn(TILES * j + k - 1))
                dst = ps[:, 6 + k % 2, :].bitcast(F16)
                for g in range(8):
                    h0 = H * k + 4 * (g % 4)
                    src = QK12[g // 4][:, h0:h0 + 4, :, :].rearrange("p h b d -> p (h b d)")
                    ins = turn(dst[:, g * P:(g + 1) * P], src, ident16[:, :])
                ins.then_inc(d_ps, 1)

            def project(j, par):
                u_transposes(j, par, par, up_ready, uT_copied, j - 1, uT_ps)
                if not (isinstance(j, int) and j == 0):
                    split_transposes(j - 1, 0)
                    split_transposes(j - 1, 1)
                pe.wait_ge(uT_copied, j + 1)
                for k in range(TILES):
                    pe.wait_ge(t_done, nn(TILES * (j - 1) + k + 1))
                    mm(ps[:, 2 + k, 0:3 * D], uT[par][:, k * P:(k + 1) * P], wqkv_sb[:, :], start=True, stop=True).then_inc(qkv_ps, 1)
                if not (isinstance(j, int) and j == 0):
                    split_transposes(j - 1, 2)
                    split_transposes(j - 1, 3)

            by_pairs(pe, project)
            for k in range(TILES):
                split_transposes(GROUPS - 1, k)
            pe.wait_ge(d_copied, NT)
            pe.wait_ge(t_done, NT)

            def scores(n, par, hf):
                if hf == 0:
                    pe.wait_ge(qd_ready, n + 1)
                pe.wait_ge(p_ready, nn(2 * n + hf - 1))
                for j in (2 * hf, 2 * hf + 1):
                    ins = mm(ps[:, j, :], QKb[par][:, 4 + j, :], QD[par][:, j, :, :].rearrange("p g q -> p (g q)"), start=True, stop=True)
                ins.then_inc(s_ps, 1)

            def weighted(n, par, loads):
                pe.wait_ge(v_in[par], 16 * loads)
                pe.wait_ge(p_ready, 2 * n + 2)
                pe.wait_ge(ot_copied, nn(n))
                for j in range(4):
                    for g in range(ROWG):
                        h = 4 * j + g
                        ins = mm(ps[32 * g:32 * g + 32, 4, j * T:(j + 1) * T], Vb[par][:, VW * h:VW * h + 32],
                                 Pb[par][:, j, g, :], start=True, stop=True)
                ins.then_inc(pv_ps, 1)

            def back(n, par):
                pe.wait_ge(ot_copied, n + 1)
                pe.wait_ge(o_norm, nn(n - 1))
                for j in range(4):
                    ins = turn(ps[:, 5 + par, j * P:(j + 1) * P], OTs[par][:, j, :], ident[:, :])
                ins.then_inc(o4_ps, 1)

            def step(n, par, half_n, has_s=True, has_w=True, has_b=True):
                if has_s:
                    scores(n, par, 0)
                if has_b:
                    back(n - 2, par)
                if has_s:
                    scores(n, par, 1)
                if has_w:
                    weighted(n - 1, 1 - par, half_n + par)

            step(0, 0, 0, has_w=False, has_b=False)
            step(1, 1, 0, has_b=False)
            step(2, 0, 1)
            step(3, 1, 1)
            with pe.Fori(2, N // 2) as i:
                for u in range(2):
                    step(2 * i + u, u, i)
            step(N, 0, N // 2, has_s=False)
            step(N + 1, 1, N // 2, has_s=False, has_w=False)

            def o_transposes(j, par, loads):
                pe.wait_ge(o_in[par], 64 * loads)
                pe.wait_ge(oT_copied, nn(j))
                for k in range(TILES):
                    ins = turn(ps[:, 0, k * P:(k + 1) * P], o_ld[par][:, k, :], ident[:, :])
                ins.then_inc(oT_ps, 1)

            def after_attention(j, par, loads):
                o_transposes(j, par, loads)
                pe.wait_ge(oT_copied, j + 1)
                pe.wait_ge(p_done, nn(j - 1))
                for k in range(TILES):
                    ins = mm(ps[:, 1 + par, k * D:(k + 1) * D], oT[:, k * P:(k + 1) * P], wo_sb[:, :], start=True, stop=True)
                ins.then_inc(wo_ps, 1)

            after_attention(0, 0, 1)
            after_attention(1, 1, 1)
            with pe.Fori(1, GROUPS // 2) as i:
                for u in range(2):
                    after_attention(2 * i + u, u, i + 1)
            pe.wait_ge(p_done, GROUPS)

            def f1(j, k, par):
                if k == 0:
                    pe.wait_ge(uT_copied3, j + 1)
                pe.wait_ge(v_done, nn(TILES * j + k - 1))
                mm(ps[:, 3 + k % 2, :], uT[par][:, k * P:(k + 1) * P], w1_sb[:, :], start=True, stop=True).then_inc(f1_ps, 1)

            def v_transposes(j, k):
                pe.wait_ge(v_done, TILES * j + k + 1)
                pe.wait_ge(vT_copied, nn(TILES * j + k - 1))
                for c in range(FF // P):
                    ins = turn(ps[:, 5 + k % 2, c * P:(c + 1) * P], vb[k % 2][:, c * P:(c + 1) * P], ident[:, :])
                ins.then_inc(vT_ps, 1)

            def f2(j, k, par):
                pe.wait_ge(vT_copied, TILES * j + k + 1)
                if k == 0:
                    pe.wait_ge(p2_done, nn(j - 1))
                for c in range(FF // P):
                    ins = mm(ps[:, 7 - 5 * par, k * D:(k + 1) * D], vT[k % 2][:, c * P:(c + 1) * P], w2_sb[:, c, :], start=c == 0, stop=c == 3)
                ins.then_inc(f2_ps, 1)

            def hidden(j, par):
                lag = not (isinstance(j, int) and j == 0)
                if lag:
                    v_transposes(j - 1, 3)
                    f2(j - 1, 2, 1 - par)
                u_transposes(j, par, 0, up_ready3, uT_copied3, j, uT_ps3)
                if lag:
                    f2(j - 1, 3, 1 - par)
                f1(j, 0, par)
                f1(j, 1, par)
                v_transposes(j, 0)
                f1(j, 2, par)
                v_transposes(j, 1)
                f2(j, 0, par)
                f1(j, 3, par)
                v_transposes(j, 2)
                f2(j, 1, par)

            by_pairs(pe, hidden)
            v_transposes(GROUPS - 1, 3)
            f2(GROUPS - 1, 2, 1)
            f2(GROUPS - 1, 3, 1)


_INS = ['x', 'cond_1024', 'L0_cond_Wx', 'L0_cond_Wh', 'L0_cond_b', 'L1_cond_w_q', 'L1_cond_b_q', 'L1_cond_w_k',
        'L1_cond_b_k', 'L1_cond_w_v', 'L1_cond_b_v', 'L1_cond_w_o', 'L1_cond_b_o', 'L1_cond_w_f1', 'L1_cond_b_f1',
        'L1_cond_w_f2', 'L1_cond_b_f2', 'L1_cond_w_ada', 'L1_cond_b_ada']


def kernel(**inputs):
    import numpy as _np
    import concourse.bacc as _bacc
    from concourse import mybir as _mybir
    from concourse.bass_utils import run_bass_kernel_spmd as _run

    nc = _bacc.Bacc("TRN2", target_bir_lowering=False, num_devices=1)
    arrays, args = {}, []
    for name in _INS:
        a = _np.ascontiguousarray(inputs[name])
        arrays[f"in_{name}_dram"] = a
        args.append(nc.dram_tensor(f"in_{name}_dram", a.shape, _mybir.dt.from_np(a.dtype), kind="ExternalInput").ap())
    args.append(nc.dram_tensor("out_0_dram", (N, T, D), F32, kind="ExternalOutput").ap())
    build(nc, *args)
    r = _run(nc, [arrays], core_ids=[0])
    return r.results[0]["out_0_dram"]
```

```python
import math

import numpy as np

import concourse.bass as bass
from concourse import mybir
from contextlib import ExitStack

F32 = mybir.dt.float32
F16 = mybir.dt.float16
I32 = mybir.dt.int32
ALU = mybir.AluOpType
ACT = mybir.ActivationFunctionType
AX = mybir.AxisListType

N, T, D = 32, 128, 128
H, HD = 16, 8
FF = 512
P = 128
TS = P // N
TILES = 4
STEPS = TS * TILES
GROUPS = T // STEPS
GW = TILES * D
PAIRW = 2 * TILES
NT = GROUPS * TILES
NH3 = 3 * H
VW = HD + 1
BATCHES = 4
CHUNKS = FF // P
ROWG = 4

EPS = 1e-7
EPS2 = EPS * EPS
MAXT = float(np.float32(1.0 - 1e-5))
CLIP = math.atanh(MAXT)
LN_EPS = 1e-6

RSQRT_C = 0.375 ** 0.2
RSQRT_A, RSQRT_B = -1.25 / RSQRT_C ** 3, 1.875 / RSQRT_C
RSQRT_BITS = 1594948992.0


def _beta(a, b):
    return math.exp(math.lgamma(a) + math.lgamma(b) - math.lgamma(a + b))


BETA_UP = _beta(HD / 2, 0.5) / _beta(D / 2, 0.5)
SCALE = 1.0 / math.sqrt(HD)


def nn(value):
    return max(value, 0) if isinstance(value, int) else value


class Chain:

    def __init__(self, eng, sem):
        self.eng, self.sem, self.base, self.n, self.per = eng, sem, 0, 0, None

    def start(self, step, per=None, behind=0):
        if per is None and isinstance(step, int) and step == 0:
            return
        if self.per is None:
            self.per = per or self.n
        self.base, self.n = self.per * step, behind

    def add(self, ins):
        self.n += 1
        ins.then_inc(self.sem, 1)

    def sync(self):
        self.eng.wait_ge(self.sem, self.base + self.n)

    def link(self, ins):
        self.add(ins)
        self.sync()


def by_pairs(eng, step):
    for u in range(2):
        step(u, u)
    with eng.Fori(1, GROUPS // 2) as i:
        for u in range(2):
            step(2 * i + u, u)


def by_batches(eng, step, peeled):
    for i in range(peeled):
        for u in range(BATCHES):
            step(i, u)
    with eng.Fori(peeled, N // BATCHES - 1) as i:
        for u in range(BATCHES):
            step(i, u)
    for u in range(BATCHES):
        step(N // BATCHES - 1, u)


def uses(i, u):
    return 2 * i + u // 2 + 1


def build(nc, x, cond, Wx, Wh, b, w_q, b_q, w_k, b_k, w_v, b_v, w_o, b_o, w_f1, b_f1, w_f2, b_f2, w_ada, b_ada, out):
    v_dram = nc.dram_tensor("v_scratch", (N, T, H * VW), F32, kind="Internal").ap()
    o_dram = nc.dram_tensor("o_scratch", (N, T, D), F32, kind="Internal").ap()
    ctx = ExitStack()
    with ctx:
        def sb(name, shape, dt=F32):
            return ctx.enter_context(nc.sbuf_tensor(name, shape, dt))

        def sem(name):
            return ctx.enter_context(nc.semaphore(name))

        def tiles(ap):
            return ap.rearrange("p (k d) -> p k d", k=TILES)

        wx_sb, wh_sb, wo_sb = sb("wx_sb", [P, D]), sb("wh_sb", [P, D]), sb("wo_sb", [P, D])
        wqkv_sb = sb("wqkv_sb", [P, 3 * D])
        wada_sb = sb("wada_sb", [P, 6 * D])
        w1_sb = sb("w1_sb", [P, FF])
        w2_sb = sb("w2_sb", [P, FF // P, D])
        b_row = sb("b_row", [1, D])
        ones_row = sb("ones_row", [1, P])
        cond_sb = sb("cond_sb", [N, D])
        h0T = sb("h0T", [P, N])
        cond4 = sb("cond4", [P, TS, N])
        ident = sb("ident", [P, P])
        ident16 = sb("ident16", [P, P], F16)
        mask = sb("mask", [P, ROWG])
        ada = sb("ada", [P, 6 * D])
        bqkv = sb("bqkv", [P, 3 * D])
        bo = sb("bo", [P, D])
        b1 = sb("b1", [P, CHUNKS])
        b2 = sb("b2", [P, D])

        X1 = sb("X1", [P, GROUPS * GW])
        X2 = sb("X2", [P, GROUPS * GW])
        XN = [sb(f"XN{i}", [P, NT]) for i in range(2)]
        QK = sb("QK", [P, N, 8, T], F16)
        U1 = X2

        S = sb("S", [P, 20, NT])
        SI = sb("SI", [P, 2, NT], I32)
        MV = sb("MV", [P, NT, 2])
        LA, LB = sb("LA", [P, NT]), sb("LB", [P, NT])
        USS, RU = sb("USS", [P, NT]), sb("RU", [P, NT])
        R3 = sb("R3", [P, 3, NT])
        AL, BE = sb("AL", [P, NT]), sb("BE", [P, NT])

        x_st = [sb(f"x_st{i}", [P, TILES, D]) for i in range(2)]
        xT_sb = sb("xT_sb", [P, GW])
        hsT = sb("hsT", [P, STEPS * N])
        st = [sb(f"st{i}", [P, TILES, 6]) for i in range(2)]
        mv = sb("mv", [P, TILES, 2])
        carry = sb("carry", [P, 2])
        ones = sb("ones", [P, 1])
        U0 = [sb(f"U0{i}", [P, TILES, D]) for i in range(2)]
        SQU = [sb(f"SQU{i}", [P, TILES, D]) for i in range(2)]
        UP = [sb(f"UP{i}", [P, TILES, D]) for i in range(2)]
        uT = [sb(f"uT{i}", [P, GW]) for i in range(2)]
        Tq = [sb(f"Tq{i}", [P, 3, TILES, D]) for i in range(2)]
        SQT = sb("SQT", [P, 3, TILES, D])
        NH = TILES * NH3
        HS = sb("HS", [P, NH + TILES * 3])
        HR = sb("HR", [P, NH + TILES * 3])
        QK12 = [[sb(f"QK12{i}", [P, TILES * H, 4, HD], F16)[:, :, :, :] for i in range(2)]]
        Vaug = sb("Vaug", [P, TILES, H, VW])

        QD = [Tq[i][:, :, :, :].rearrange("p a k d -> p (a k d)").bitcast(F16)[:, 0:4 * ROWG * T]
              .rearrange("p (j g t) -> p j g t", j=4, g=ROWG) for i in range(2)]
        Vb = [sb(f"Vb{i}", [P, H * VW + 32]) for i in range(2)]
        Pb = [sb(f"Pb{i}", [P, 4, ROWG, T]) for i in range(2)]
        QK12.append([Pb[0][:, :, :, :].rearrange("p j g t -> p (j g t)").bitcast(F16)
                     [:, i * TILES * H * 4 * HD:(i + 1) * TILES * H * 4 * HD].rearrange("p (m b d) -> p m b d", b=4, d=HD)
                     for i in range(2)])
        OTs = x_st
        rec = [sb(f"rec{i}", [P, H]) for i in range(2)]
        ob = [sb(f"ob{i}", [P, D]) for i in range(2)]

        free = QK[:, :, :, :].rearrange("p n g t -> p (n g t)").bitcast(F32)
        taken = [0]

        def place(width):
            taken[0] += width
            return free[:, taken[0] - width:taken[0]]

        GA = place(GROUPS * GW)
        U3 = place(GROUPS * GW)
        vsq = [place(CHUNKS * GW)]
        o_ld = [vsq[0][:, i * 2 * GW:(i + 1) * 2 * GW] for i in range(2)]
        PA = [tiles(place(GW)) for _ in range(2)]
        SQ3 = [place(3 * GW).rearrange("p (a k d) -> p a k d", a=3, k=TILES) for _ in range(2)]
        vsq.append(place(CHUNKS * GW))
        oT = [vsq[1][:, i * GW:(i + 1) * GW] for i in range(2)]

        def squares3(j, groups):
            half, at = divmod(j * GW, CHUNKS * GW)
            return vsq[half][:, at:at + groups * GW]

        vT = [Pb[i][:, :, :, :].rearrange("p j g q -> p (j g q)") for i in range(2)]
        RV = sb("RV", [P, 6, TILES])

        ps = ctx.enter_context(nc.psum_tensor("ps", [P, 8, 512], F32))

        rnn_w = sem("rnn_w")
        all_w = sem("all_w")
        x_in = [sem(f"x_in{i}") for i in range(2)]
        x_copied = sem("x_copied")
        pool_const = sem("pool_const")
        pool_chain = sem("pool_chain")
        condT_ps = sem("condT_ps")
        cond_ready = sem("cond_ready")
        ada_ps = sem("ada_ps")
        ada_used = sem("ada_used")
        setup_done = sem("setup_done")
        xT_ps = sem("xT_ps")
        xT_copied = sem("xT_copied")
        xw_ready = sem("xw_ready")
        h_ready = sem("h_ready")
        rnn_mm = sem("rnn_mm")
        hT_ready = sem("hT_ready")
        x1_added = sem("x1_added")
        u0_done = sem("u0_done")
        u0_last = sem("u0_last")
        u_stored = sem("u_stored")
        squ_done = sem("squ_done")
        uss_done = sem("uss_done")
        ru_ready = sem("ru_ready")
        ln_ready = sem("ln_ready")
        ru_ready3 = sem("ru_ready3")
        rv_max = sem("rv_max")
        rv_sqrt = sem("rv_sqrt")
        up_ready = sem("up_ready")
        uT_ps = sem("uT_ps")
        uT_copied = sem("uT_copied")
        qkv_ps = sem("qkv_ps")
        t_done = sem("t_done")
        sqt_done = sem("sqt_done")
        hs_ready = sem("hs_ready")
        hr_ready = sem("hr_ready")
        f_ready = sem("f_ready")
        fk_ready = sem("fk_ready")
        q1_done = sem("q1_done")
        q2_done = sem("q2_done")
        v_ready = sem("v_ready")
        v_out = sem("v_out")
        d_ps = sem("d_ps")
        d_copied = sem("d_copied")
        d_last = sem("d_last")
        low_last = sem("low_last")
        s_ps = sem("s_ps")
        p_ready = sem("p_ready")
        pv_ps = sem("pv_ps")
        ot_copied = sem("ot_copied")
        qd_ready = sem("qd_ready")
        o4_ps = sem("o4_ps")
        o_norm = sem("o_norm")
        rec_done = sem("rec_done")
        oT_ps = sem("oT_ps")
        oT_copied = sem("oT_copied")
        wo_ps = sem("wo_ps")
        p_done = sem("p_done")
        ga_ready = sem("ga_ready")
        sqp_ready = sem("sqp_ready")
        sqg_ready = sem("sqg_ready")
        xg_ready = sem("xg_ready")
        r3_done = sem("r3_done")
        na_ready = sem("na_ready")
        th_ready = sem("th_ready")
        ab_ready = sem("ab_ready")
        tmp_ready = sem("tmp_ready")
        x2_done = sem("x2_done")
        ax_ready = sem("ax_ready")
        ax2_ready = sem("ax2_ready")
        u0_done3 = sem("u0_done3")
        xs_done3 = sem("xs_done3")
        um_done3 = sem("um_done3")
        ln_ready3 = sem("ln_ready3")
        u_stored3 = sem("u_stored3")
        squ_done3 = sem("squ_done3")
        uss_done3 = sem("uss_done3")
        up_ready3 = sem("up_ready3")
        uT_ps3 = sem("uT_ps3")
        uT_copied3 = sem("uT_copied3")
        f1_ps = sem("f1_ps")
        sum_half = sem("sum_half")
        sum_done = sem("sum_done")
        ss_ps = sem("ss_ps")
        vsq_done = sem("vsq_done")
        vT_copied = sem("vT_copied")
        f2_ps = sem("f2_ps")
        p2_done = sem("p2_done")
        ga2_ready = sem("ga2_ready")
        sqp2_ready = sem("sqp2_ready")
        sqg2_ready = sem("sqg2_ready")
        xg2_ready = sem("xg2_ready")
        r32_done = sem("r32_done")
        ab2_ready = sem("ab2_ready")
        tmp2_ready = sem("tmp2_ready")
        y_done = sem("y_done")
        chain_bn = sem("chain_bn")
        chain_small = sem("chain_small")
        chain_ln = sem("chain_ln")
        chain_centre = sem("chain_centre")
        chain_clip = sem("chain_clip")
        chain_front = sem("chain_front")
        chain_heads = sem("chain_heads")
        chain_pool = sem("chain_pool")
        chain_bn3 = sem("chain_bn3")
        chain_small3 = sem("chain_small3")
        chain_rv = sem("chain_rv")
        x1x2_done = sem("x1x2_done")
        v_in, o_out = ([sem(f"{n}{i}") for i in range(2)] for n in ("v_in", "o_out"))
        o_in = [sem(f"o_in{i}") for i in range(2)]
        y_out = sem("y_out")
        hr_sqrt, low_done = sem("hr_sqrt"), sem("low_done")

        block = ctx.enter_context(nc.Block())

        def dram_pair(ap, i, s):
            v = ap.rearrange("n (i k s) d -> s n i k d", i=GROUPS // 2, s=TS)
            return v[s, :, bass.ds(i, 1), :, :].rearrange("n o k d -> n (o k) d")

        dram_tile = lambda ap, j, s: ap.rearrange("n (g k s) d -> s n g k d", g=GROUPS, s=TS)[s, :, bass.ds(j, 1), :, :].rearrange("n o k d -> n (o k) d")

        def d_places(j, k):
            src = ps[:, 6 + k % 2, :].bitcast(F16).rearrange("p (g s n) -> p g s n", g=8, s=TS)
            return QK[:, :, :, bass.ds(STEPS * j + TS * k, TS)].rearrange("p n g s -> p g s n"), src

        def rows4(ap, width=D):
            return ap.unsqueeze(1).broadcast_to([P, TILES, width])

        def cols(store, j, width):
            return store[:, bass.ds(j * width, width)]

        def per_tile(numbers, j):
            return cols(numbers, j, TILES).unsqueeze(2).broadcast_to([P, TILES, D])

        def heads(par, i):
            return Tq[par][:, i, :, :].rearrange("p k (h d) -> p (k h) d", d=HD)

        def rsqrt(E, dst, src, xh, w, chain):
            chain.add(E.tensor_scalar(xh, src, -0.5, None, ALU.mult))
            chain.link(E.tensor_scalar(dst.bitcast(I32), src.bitcast(I32), -0.5, RSQRT_BITS, ALU.mult, ALU.add))
            chain.link(E.tensor_tensor(w, dst, dst, ALU.mult))
            chain.link(E.tensor_tensor(w, w, src, ALU.mult))
            chain.link(E.scalar_tensor_tensor(w, w, RSQRT_A, w, ALU.add, ALU.mult))
            chain.link(E.scalar_tensor_tensor(dst, w, RSQRT_B, dst, ALU.add, ALU.mult))
            chain.link(E.tensor_tensor(w, dst, dst, ALU.mult))
            chain.link(E.tensor_tensor(w, w, xh, ALU.mult))
            chain.link(E.scalar_tensor_tensor(dst, w, 1.5, dst, ALU.add, ALU.mult))

        def ln_coefficients(E, at, w, xn, chain, ready):
            link, add = chain.link, chain.add
            mean, var = MV[:, at, 0], MV[:, at, 1]

            def row(i):
                return S[:, i, 0:w]

            link(E.tensor_tensor(row(6), mean, mean, ALU.mult))
            link(E.tensor_tensor(row(7), row(6), var, ALU.add))
            add(E.tensor_scalar(xn[:, at], row(7), float(D), None, ALU.mult))
            link(E.tensor_scalar(row(0), row(7), float(D), EPS2, ALU.mult, ALU.max))
            rsqrt(E, row(9), row(0), row(6), row(7), chain)
            link(E.tensor_tensor(row(1), row(0), row(9), ALU.mult))
            link(E.tensor_scalar(row(8), row(1), EPS, MAXT, ALU.max, ALU.min))
            z = row(8)
            link(E.tensor_scalar(row(7), z, -1.0, 1.0, ALU.mult, ALU.add))
            link(E.reciprocal(row(10), row(7)))
            link(E.scalar_tensor_tensor(row(11), z, 1.0, row(10), ALU.add, ALU.mult))
            y, yi = row(11), row(11).bitcast(I32)
            add(E.tensor_scalar(SI[:, 0, 0:w], yi, 23, None, ALU.logical_shift_right))
            add(E.tensor_scalar(row(12), y, 2.0, None, ALU.is_ge))
            link(E.tensor_scalar(SI[:, 1, 0:w], yi, 0x7FFFFF, 0x3F800000, ALU.bitwise_and, ALU.bitwise_or))
            m = SI[:, 1, 0:w].bitcast(F32)
            add(E.tensor_scalar(row(13), SI[:, 0, 0:w], -127.0, None, ALU.add))
            link(E.tensor_scalar(row(6), m, 1.0, None, ALU.add))
            link(E.reciprocal(row(7), row(6)))
            link(E.scalar_tensor_tensor(row(6), m, -1.0, row(7), ALU.add, ALU.mult))
            link(E.tensor_tensor(row(7), row(6), z, ALU.subtract))
            link(E.tensor_tensor(row(6), row(7), row(12), ALU.mult))
            link(E.tensor_tensor(row(10), row(6), z, ALU.add))
            z_or_m = row(10)
            link(E.tensor_tensor(row(11), z_or_m, z_or_m, ALU.mult))
            w2 = row(11)
            link(E.tensor_scalar(row(6), w2, 1.0 / 15, None, ALU.mult))
            src, to = 6, 7
            for k in (13, 11, 9, 7, 5, 3):
                link(E.scalar_tensor_tensor(row(to), row(src), 1.0 / k, w2, ALU.add, ALU.mult))
                src, to = to, src
            link(E.scalar_tensor_tensor(row(to), row(src), 1.0, z_or_m, ALU.add, ALU.mult))
            src, to = to, src
            link(E.scalar_tensor_tensor(row(to), row(13), 0.5 * math.log(2.0), row(src), ALU.mult, ALU.add))
            link(E.tensor_tensor(row(12), row(to), row(9), ALU.mult))
            link(E.tensor_tensor(row(6), row(12), row(12), ALU.mult))
            link(E.tensor_tensor(row(7), row(6), var, ALU.mult))
            link(E.tensor_scalar(row(14), row(7), LN_EPS, None, ALU.add))
            rsqrt(E, row(15), row(14), row(6), row(7), chain)
            link(E.tensor_tensor(LA[:, at], row(12), row(15), ALU.mult))
            E.tensor_tensor(LB[:, at], LA[:, at], mean, ALU.mult).then_inc(ready, 1)

        @block.sync
        def _(sp):
            def load_x(j, par):
                for s in range(TS):
                    sp.dma_start(tiles(cols(X1, j, GW))[s * N:(s + 1) * N, :, :], dram_tile(x, j, s)).then_inc(x_in[par], 16)

            load_x(0, 0)
            sp.dma_start(wx_sb[:, :], Wx).then_inc(rnn_w, 16)
            sp.dma_start(cond_sb[:, :], cond).then_inc(rnn_w, 16)
            sp.dma_start(wh_sb[:, :], Wh).then_inc(rnn_w, 16)
            sp.dma_start(b_row[:, :], b.unsqueeze(0)).then_inc(rnn_w, 16)
            load_x(1, 1)
            sp.dma_start(wada_sb[:, :], w_ada).then_inc(all_w, 16)
            for dst, bias in ((ada, b_ada), (bo, b_o), (b2, b_f2), (bqkv[:, 0:D], b_q), (bqkv[:, D:2 * D], b_k), (bqkv[:, 2 * D:3 * D], b_v)):
                sp.dma_start(dst[:, :], bias.unsqueeze(0).broadcast_to([P, bias.shape[0]])).then_inc(all_w, 16)
            for c in range(CHUNKS):
                sp.dma_start(b1[:, c:c + 1], b_f1[c * P:(c + 1) * P].unsqueeze(1)).then_inc(all_w, 16)
            for n, w in enumerate((w_q, w_k, w_v)):
                sp.dma_start(wqkv_sb[:, n * D:(n + 1) * D], w).then_inc(all_w, 16)
            sp.dma_start(wo_sb[:, :], w_o).then_inc(all_w, 16)
            sp.dma_start(w1_sb[:, :], w_f1).then_inc(all_w, 16)
            sp.dma_start(w2_sb[:, :, :], w_f2.rearrange("(c p) d -> p c d", p=P)).then_inc(all_w, 16)
            with sp.Fori(1, GROUPS // 2) as i:
                for u in range(2):
                    sp.wait_ge(x_in[u], 64 * i)
                    load_x(2 * i + u, u)

            def store_v(j, par):
                sp.wait_ge(v_ready, j + 1)
                for s in range(TS):
                    sp.dma_start(dram_tile(v_dram, j, s),
                                 Vaug[s * N:(s + 1) * N, :, :, :].rearrange("n k h c -> n k (h c)")).then_inc(v_out, 16)

            by_pairs(sp, store_v)

            sp.wait_ge(v_out, 64 * GROUPS)

            def load_v(n, par):
                sp.dma_start(Vb[par][:, 0:H * VW], v_dram[bass.ds(n, 1), :, :].rearrange("o t c -> (o t) c")).then_inc(v_in[par], 16)

            def store_o(n, par):
                sp.wait_ge(o_norm, n + 1)
                sp.dma_start(o_dram[bass.ds(n, 1), :, :].rearrange("o t d -> (o t) d"), ob[par][:, :]).then_inc(o_out[par], 16)

            for n in range(2):
                load_v(n, n)

            def batch(i, u):
                n, par = BATCHES * i + u, u % 2
                if not (isinstance(n, int) and (n == 0 or n == N - 1)):
                    sp.wait_ge(pv_ps, n)
                    load_v(n + 1, 1 - par)
                if not (isinstance(n, int) and n < 3):
                    store_o(n - 3, 1 - par)

            by_batches(sp, batch, 1)
            for n in range(N - 3, N):
                store_o(n, n % 2)

            for par in range(2):
                sp.wait_ge(o_out[par], 16 * (N // 2))

            def load_o(i, par):
                sp.wait_ge(oT_ps, nn(2 * i - 2))
                for s in range(TS):
                    sp.dma_start(o_ld[par][s * N:(s + 1) * N, :].rearrange("n (k d) -> n k d", d=D), dram_pair(o_dram, i, s)).then_inc(o_in[par], 16)

            for i in range(GROUPS // 2):
                load_o(i, i % 2)

            for first, last in ((0, GROUPS // 2), (GROUPS // 2, GROUPS - 2), (GROUPS - 2, GROUPS)):
                sp.wait_ge(y_done, last)
                for s in range(TS):
                    rows = out.rearrange("n (k s) d -> s n k d", s=TS)[s, :, first * TILES:last * TILES, :]
                    sp.dma_start(rows, X2[s * N:(s + 1) * N, first * GW:last * GW].rearrange("n (k d) -> n k d", d=D)).then_inc(y_out, 16)
            sp.wait_ge(y_out, 16 * TS * 3)

        @block.gpsimd
        def _(pool):
            G = nc.gpsimd
            G.memset(ident[:, :], 0.0).then_inc(pool_chain, 1)
            G.memset(ones_row[:, :], 1.0).then_inc(pool_const, 1)
            G.memset(Vaug[:, :, :, :], 1.0).then_inc(pool_const, 1)
            G.memset(ones[:, :], 1.0).then_inc(pool_chain, 1)
            for i in range(2):
                G.memset(Vb[i][:, :], 0.0).then_inc(pool_const, 1)
            pool.wait_ge(pool_chain, 2)
            G.affine_select(out=ident[:, :], in_=ident[:, :], compare_op=ALU.not_equal, fill=1.0, base=0,
                            pattern=[[-1, P]], channel_multiplier=1).then_inc(pool_chain, 1)
            pool.wait_ge(pool_chain, 3)
            G.tensor_copy(ident16[:, :], ident[:, :]).then_inc(pool_const, 1)

            def copy_x(j, par, loads):
                pool.wait_ge(x_in[par], 64 * loads)
                pool.wait_ge(xT_ps, nn(j - 1))
                G.tensor_tensor(x_st[par][:, :, :], tiles(cols(X1, j, GW)), ones[:, :].unsqueeze(2).broadcast_to([P, TILES, D]),
                                ALU.mult).then_inc(x_copied, 1)

            for j in range(1, 4):
                copy_x(j, j % 2, j // 2 + 1)
            pool.wait_ge(setup_done, 1)

            def modulate(j, par, centred, value):
                pool.wait_ge(centred, value)
                chain1.start(j)
                chain1.link(G.tensor_tensor(U0[par][:, :, :], U0[par][:, :, :], rows4(ada[:, D:2 * D]), ALU.mult))
                G.tensor_tensor(tiles(cols(U1, j, GW)), U0[par][:, :, :], rows4(ada[:, 0:D]), ALU.add).then_inc(u_stored, 1)

            chain1 = Chain(pool, chain_pool)

            def square(j, par):
                pool.wait_ge(u_stored, j + 1)
                pool.wait_ge(uss_done, nn(j - 1))
                G.tensor_tensor(SQU[par][:, :, :], tiles(cols(U1, j, GW)), tiles(cols(U1, j, GW)), ALU.mult).then_inc(squ_done, 1)

            def centre(j, par):
                pool.wait_ge(u_stored, nn(j - 1))
                centre1.start(j)
                centre1.link(G.tensor_tensor(U0[par][:, :, :], tiles(cols(X1, j, GW)), per_tile(LA, j), ALU.mult))
                G.tensor_tensor(U0[par][:, :, :], U0[par][:, :, :], per_tile(LB, j), ALU.subtract).then_inc(u0_done, 1)

            centre1 = Chain(pool, chain_centre)

            def pair(i):
                for u in range(2):
                    copy_x(2 * i + 4 + u, u, i + 3)
                pool.wait_ge(ln_ready, i + 1)
                for u in range(2):
                    centre(2 * i + u, u)
                    modulate(2 * i + u, u, u0_done, 2 * i + u + 1)
                    square(2 * i + u, u)

            pair(0)
            pair(1)
            pool.wait_ge(ln_ready, GROUPS // 2 - 1)
            for u in range(2):
                centre(GROUPS - 4 + u, u)
                modulate(GROUPS - 4 + u, u, u0_done, GROUPS - 3 + u)
                square(GROUPS - 4 + u, u)

            def clip_u(j, par, pair):
                pool.wait_ge(ru_ready, pair + 1)
                pool.wait_ge(uT_ps, nn(j - 1))
                G.tensor_tensor(UP[par][:, :, :], tiles(cols(U1, j, GW)), per_tile(RU, j), ALU.mult).then_inc(up_ready, 1)

            def scale_k(j, par):
                pool.wait_ge(hr_ready, j + 1)
                f = HS[:, TILES * H:2 * TILES * H].unsqueeze(2).broadcast_to([P, TILES * H, HD])
                G.tensor_tensor(heads(par, 1), heads(par, 1), f, ALU.mult).then_inc(fk_ready, 1)

            def scale_v(j, par):
                pool.wait_ge(hr_ready, j + 1)
                pool.wait_ge(v_out, 64 * j)
                f = HS[:, 2 * TILES * H:NH].unsqueeze(2).broadcast_to([P, TILES * H, HD])
                G.tensor_tensor(Vaug[:, :, :, 0:HD].rearrange("p k h d -> p (k h) d"), heads(par, 2), f, ALU.mult).then_inc(v_ready, 1)

            def low_parts(j, par, which=(0, 1)):
                for i in which:
                    pool.wait_ge(q1_done, 2 * j + i + 1)
                    if i:
                        pool.wait_ge(fk_ready, j + 1)
                    G.tensor_tensor(QK12[par][i][:, :, 1 + i, :], heads(par, i), QK12[par][i][:, :, 0, :], ALU.subtract).then_inc(low_done, 1)

            def project(j, par, pair=None, which=(0, 1)):
                scale_k(j, par)
                scale_v(j, par)
                if pair is not None:
                    clip_u(j + 2, par, pair)
                low_parts(j, par, which)

            for u in range(2):
                clip_u(u, u, 0)
            for u in range(2):
                modulate(GROUPS - 2 + u, u, u0_last, u + 1)
            project(0, 0, 1)
            project(1, 1, 1)
            with pool.Fori(1, GROUPS // 2 - 1) as i:
                for u in range(2):
                    project(2 * i + u, u, i + 1)
            project(GROUPS - 2, 0)
            project(GROUPS - 1, 1, which=(0,))

            def gated(j, par):
                pool.wait_ge(p_done, j + 1)
                G.tensor_tensor(tiles(cols(GA, j, GW)), PA[par][:, :, :], rows4(ada[:, 2 * D:3 * D]), ALU.mult).then_inc(ga_ready, 1)

            by_pairs(pool, gated)

            pool.wait_ge(ab_ready, 1)

            def update(j, done):
                G.tensor_tensor(tiles(cols(GA, j, GW)), tiles(cols(GA, j, GW)), per_tile(BE, j), ALU.mult).then_inc(done, 1)

            by_pairs(pool, lambda j, par: update(j, tmp_ready))

            def modulate3(j, par):
                pool.wait_ge(u0_done3, j + 1)
                G.tensor_tensor(tiles(cols(U3, j, GW)), tiles(cols(U3, j, GW)), rows4(ada[:, 4 * D:5 * D]), ALU.mult).then_inc(um_done3, 1)

            by_pairs(pool, modulate3)

            def gated2(j, par):
                pool.wait_ge(p2_done, j + 1)
                G.tensor_tensor(tiles(cols(GA, j, GW)), PA[par][:, :, :], rows4(ada[:, 5 * D:6 * D]), ALU.mult).then_inc(ga2_ready, 1)
                pool.wait_ge(ga2_ready, j + 1)
                pool.wait_ge(r32_done, nn(j - 1))
                G.tensor_tensor(SQ3[par][:, 2, :, :], tiles(cols(GA, j, GW)), tiles(cols(X2, j, GW)), ALU.mult).then_inc(xg2_ready, 1)

            def clip_u3(j, par):
                pool.wait_ge(uT_ps3, nn(j - 1))
                G.tensor_tensor(UP[par][:, :, :], tiles(cols(U3, j, GW)), per_tile(RU, j), ALU.mult).then_inc(up_ready3, 1)

            def hidden(j, par):
                clip_u3(j + 2, par)
                if not (isinstance(j, int) and j == 0):
                    gated2(j - 1, 1 - par)

            pool.wait_ge(ru_ready3, 1)
            clip_u3(0, 0)
            clip_u3(1, 1)
            hidden(0, 0)
            hidden(1, 1)
            with pool.Fori(1, GROUPS // 2 - 1) as i:
                for u in range(2):
                    hidden(2 * i + u, u)
            for j in range(GROUPS - 3, GROUPS):
                gated2(j, j % 2)

            pool.wait_ge(ab2_ready, 1)

            by_pairs(pool, lambda j, par: update(j, tmp2_ready))

        @block.scalar
        def _(act):
            A = nc.scalar

            def group(i, par):
                for s in range(STEPS):
                    act.wait_ge(rnn_mm, STEPS * i + s + 1)
                    A.activation(hsT[:, s * N:(s + 1) * N], ps[:, par, s * N:(s + 1) * N], ACT.Tanh).then_inc(h_ready, 1)

            by_pairs(act, group)

            def square_u(j, par, store, stored, summed, squared):
                act.wait_ge(stored, j + 1)
                act.wait_ge(summed, nn(j - 1))
                A.activation(SQU[par][:, :, :], tiles(cols(store, j, GW)), ACT.Square).then_inc(squared, 1)

            def copy_uT(j, par, bank, done, readers, count, copied):
                act.wait_ge(done, j + 1)
                act.wait_ge(readers, nn(count))
                A.activation(uT[par][:, :], ps[:, bank, :], ACT.Copy).then_inc(copied, 1)

            def copy_d(j, k):
                act.wait_ge(d_ps, TILES * j + k + 1)
                A.activation(*d_places(j, k), ACT.Copy).then_inc(d_copied, 1)

            def project(j, par, last=False):
                for k in range(TILES):
                    act.wait_ge(t_done, TILES * j + k + 1)
                    if k == 0:
                        act.wait_ge(hs_ready, j)
                    A.activation(SQT[:, :, k, :], Tq[par][:, :, k, :], ACT.Square).then_inc(sqt_done, 1)
                if not last:
                    copy_uT(j + 1, 1 - par, 1 - par, uT_ps, qkv_ps, TILES * j, uT_copied)
                lag, lag2 = (not (isinstance(j, int) and j < n) for n in (1, 2))
                if lag2:
                    copy_d(j - 2, 2)
                    copy_d(j - 2, 3)
                act.wait_ge(hs_ready, j + 1)
                A.activation(HR[:, :], HS[:, :], ACT.Sqrt).then_inc(hr_sqrt, 1)
                if lag:
                    copy_d(j - 1, 0)
                    copy_d(j - 1, 1)
                act.wait_ge(f_ready, j + 1)
                act.wait_ge(d_ps, nn(TILES * (j - 1)))
                for i in range(2):
                    if i:
                        act.wait_ge(fk_ready, j + 1)
                    A.activation(QK12[par][i][:, :, 0, :], heads(par, i), ACT.Copy).then_inc(q1_done, 1)

            copy_uT(0, 0, 0, uT_ps, qkv_ps, 0, uT_copied)
            for u in range(2):
                square_u(GROUPS - 2 + u, u, U1, u_stored, uss_done, squ_done)
            project(0, 0)
            project(1, 1)
            with act.Fori(1, GROUPS // 2 - 1) as i:
                for u in range(2):
                    project(2 * i + u, u)
            project(GROUPS - 2, 0)
            project(GROUPS - 1, 1, last=True)
            copy_d(GROUPS - 2, 2)
            copy_d(GROUPS - 2, 3)
            for k in (0, 2):
                act.wait_ge(d_ps, NT - TILES + k + 1)
                A.activation(*d_places(GROUPS - 1, k), ACT.Copy).then_inc(d_copied, 1)

            def exps(n, par):
                for hf in range(2):
                    act.wait_ge(s_ps, 2 * n + hf + 1)
                    act.wait_ge(pv_ps, nn(n - 1))
                    A.activation(Pb[par][:, 2 * hf:2 * hf + 2, :, :].rearrange("p j g q -> p (j g q)"),
                                 ps[:, 2 * hf:2 * hf + 2, :].rearrange("p j c -> p (j c)"),
                                 ACT.Exp, scale=SCALE).then_inc(p_ready, 1)

            exps(0, 0)
            exps(1, 1)
            with act.Fori(1, N // 2) as i:
                for u in range(2):
                    exps(2 * i + u, u)

            def squares(j, par, p_sem, sqp, ga_sem, sqg, summed):
                act.wait_ge(p_sem, j + 1)
                act.wait_ge(summed, nn(j - 1))
                A.activation(SQ3[par][:, 0, :, :], PA[par][:, :, :], ACT.Square).then_inc(sqp, 1)
                act.wait_ge(ga_sem, j + 1)
                A.activation(SQ3[par][:, 1, :, :], tiles(cols(GA, j, GW)), ACT.Square).then_inc(sqg, 1)

            def after_attention(j, par):
                act.wait_ge(oT_ps, j + 1)
                act.wait_ge(wo_ps, nn(j - 1))
                A.activation(oT[par][:, :], ps[:, 3 * par, :], ACT.Copy).then_inc(oT_copied, 1)
                if not (isinstance(j, int) and j == 0):
                    sums(j - 1, 1 - par)

            def sums(j, par):
                act.wait_ge(p_done, j + 1)
                for k in range(TILES):
                    ins = A.activation(SQ3[par][:, 0, k, :], PA[par][:, k, :], ACT.Square, accum_out=R3[:, 0, bass.ds(TILES * j + k, 1)])
                ins.then_inc(sqp_ready, 1)
                act.wait_ge(ga_ready, j + 1)
                act.wait_ge(r3_done, nn(j - 1))
                A.activation(SQ3[par][:, 1, :, :], tiles(cols(GA, j, GW)), ACT.Square).then_inc(sqg_ready, 1)

            by_pairs(act, after_attention)
            sums(GROUPS - 1, 1)

            def tanh(n):
                act.wait_ge(na_ready, n)
                A.activation(S[:, 5, :], S[:, 4, :], ACT.Tanh).then_inc(th_ready, 1)

            tanh(1)

            def scaled(j, dst, src, numbers, done):
                for k in range(TILES):
                    at = bass.ds(j * GW + k * D, D)
                    ins = A.activation(dst[:, at], src[:, at], ACT.Copy, scale=numbers[:, bass.ds(TILES * j + k, 1)])
                ins.then_inc(done, 1)

            act.wait_ge(ab_ready, 1)
            by_pairs(act, lambda j, par: scaled(j, X2, X1, AL, ax_ready))
            act.wait_ge(ln_ready3, 1)

            by_pairs(act, lambda j, par: scaled(j, U3, X2, LA, xs_done3))
            for j in range(GROUPS):
                act.wait_ge(u_stored3, j + 1)
                A.activation(squares3(j, 1), cols(U3, j, GW), ACT.Square).then_inc(squ_done3, 1)

            def copy_vT(j, par, c):
                act.wait_ge(f1_ps, CHUNKS * j + c + 1)
                act.wait_ge(f2_ps, nn(TILES * (j - 1)))
                act.wait_ge(vsq_done, nn(CHUNKS * (j - 1)))
                A.activation(vT[par][:, c * GW:(c + 1) * GW], ps[:, 1 + c, :], ACT.Identity, bias=b1[:, c:c + 1]).then_inc(vT_copied, 1)

            def square_v(j, par, c):
                act.wait_ge(vT_copied, CHUNKS * j + c + 1)
                act.wait_ge(ss_ps, nn(j - 1))
                A.activation(vsq[par][:, c * GW:(c + 1) * GW], vT[par][:, c * GW:(c + 1) * GW], ACT.Square).then_inc(vsq_done, 1)

            def root_v(j):
                act.wait_ge(rv_max, j + 1)
                A.activation(RV[:, 1, :], RV[:, 0, :], ACT.Sqrt).then_inc(rv_sqrt, 1)

            def hidden(j, par, last=0):
                for c in range(CHUNKS):
                    square_v(j, par, c)
                    if last < 2:
                        copy_vT(j + 1, 1 - par, c)
                    if c == 0 and not (isinstance(j, int) and j == 0):
                        root_v(j - 1)
                if not last:
                    copy_uT(j + 2, par, 0, uT_ps3, f1_ps, CHUNKS * (j + 1), uT_copied3)
                if not (isinstance(j, int) and j == 0):
                    squares(j - 1, 1 - par, p2_done, sqp2_ready, ga2_ready, sqg2_ready, r32_done)

            copy_uT(0, 0, 0, uT_ps3, f1_ps, 0, uT_copied3)
            for c in range(CHUNKS):
                copy_vT(0, 0, c)
            copy_uT(1, 1, 0, uT_ps3, f1_ps, 0, uT_copied3)
            hidden(0, 0)
            hidden(1, 1)
            with act.Fori(1, GROUPS // 2 - 1) as i:
                for u in range(2):
                    hidden(2 * i + u, u)
            hidden(GROUPS - 2, 0, last=1)
            hidden(GROUPS - 1, 1, last=2)
            root_v(GROUPS - 1)
            squares(GROUPS - 1, 1, p2_done, sqp2_ready, ga2_ready, sqg2_ready, r32_done)
            tanh(2)
            act.wait_ge(ab2_ready, 1)
            by_pairs(act, lambda j, par: scaled(j, X2, X2, AL, ax2_ready))

        @block.vector
        def _(dve):
            V = nc.vector
            small = Chain(dve, chain_small)

            small.link(V.memset(mask[:, :], 0.0))
            for g in range(ROWG):
                small.link(V.memset(mask[32 * g:32 * g + 32, g:g + 1], 1.0))
            dve.wait_ge(condT_ps, 1)
            V.tensor_copy(h0T[:, :], ps[:, 2, 0:N]).then_inc(h_ready, 1)
            V.tensor_copy(cond4[:, :, :], ps[:, 2, 0:N].unsqueeze(1).broadcast_to([P, TS, N])).then_inc(cond_ready, 1)

            def copy_xT(j):
                dve.wait_ge(xT_ps, j + 1)
                dve.wait_ge(xw_ready, j)
                V.tensor_copy(xT_sb[:, :], ps[:, 4, :]).then_inc(xT_copied, 1)

            def add_ada():
                all_rows = {0: 5, 1: 6}
                dve.wait_ge(all_w, (13 + CHUNKS) * 16)
                for half, bank in all_rows.items():
                    c = 3 * D * half
                    dve.wait_ge(ada_ps, half + 1)
                    V.tensor_tensor(ada[:, c:c + 3 * D], ada[:, c:c + 3 * D], ps[:, bank, 0:3 * D], ALU.add).then_inc(ada_used, 1)
                dve.wait_ge(ada_used, 2)
                for c in (D, 4 * D):
                    V.tensor_scalar_add(ada[:, c:c + D], ada[:, c:c + D], 1.0).then_inc(ada_used, 1)
                dve.wait_ge(ada_used, 4)
                V.memset(carry[:, :], 0.0).then_inc(setup_done, 1)

            def statistics(store, j, par, chain):
                for k in range(TILES):
                    chain.add(V.bn_stats(st[par][:, k, :], store[:, bass.ds(j * GW + k * D, D)]))

            def combine(par, chain):
                chain.sync()
                V.memset(carry[:, 1:2], 0.0)
                for k in range(TILES):
                    chain.add(V.bn_aggr(mv[:, k, :], st[par][:, k, :]))

            def keep(j, chain):
                chain.link(V.tensor_copy(MV[:, bass.ds(TILES * j, TILES), :], mv[:, :, :]))

            def states(j, par):
                bn.start(j)
                dve.wait_ge(hT_ready, j + 1)
                dve.wait_ge(x_copied, j)
                V.tensor_tensor(tiles(cols(X1, j, GW)), tiles(cols(X1, j, GW)), tiles(ps[:, 2 + par, :]), ALU.add).then_inc(x1_added, 1)
                dve.wait_ge(x1_added, j + 1)
                V.memset(carry[:, 0:1], 0.0)
                statistics(X1, j, 0, bn)
                combine(0, bn)
                bn.sync()
                keep(j, bn)

            bn = Chain(dve, chain_bn)

            def sum_u(j, par, squared, summed):
                dve.wait_ge(squared, j + 1)
                V.reduce_sum(cols(USS, j, TILES), SQU[par][:, :, :], AX.X).then_inc(summed, 1)

            def clip_factors(at, w, chain, ready):
                row = lambda i: S[:, i, 0:w]
                chain.link(V.tensor_scalar(row(16), USS[:, at], EPS2, None, ALU.max))
                rsqrt(V, row(17), row(16), row(18), row(19), chain)
                V.tensor_scalar(RU[:, at], row(17), CLIP, 1.0, ALU.mult, ALU.min).then_inc(ready, 1)

            def row(i):
                return S[:, i, :]

            ln1, clip1, front1 = Chain(dve, chain_ln), Chain(dve, chain_clip), Chain(dve, chain_front)

            def clip_pair(i):
                for u in range(2):
                    sum_u(2 * i + u, u, squ_done, uss_done)
                clip1.start(i)
                dve.wait_ge(uss_done, 2 * i + 2)
                clip_factors(bass.ds(PAIRW * i, PAIRW), PAIRW, clip1, ru_ready)

            def pair(i, last=False, next_xT=True):
                states(2 * i + 1, 1)
                if not last:
                    copy_xT(2 * i + 3)
                ln1.start(i)
                ln_coefficients(V, bass.ds(PAIRW * i, PAIRW), PAIRW, XN[0], ln1, ln_ready)
                if not last:
                    if next_xT:
                        copy_xT(2 * i + 4)
                    states(2 * i + 2, 0)
                if not (isinstance(i, int) and i == 0):
                    if last:
                        front_pair()
                    clip_pair(i - 1)

            def front_pair():
                dve.wait_ge(ln_ready, GROUPS // 2)
                for par in range(2):
                    at = (GROUPS - 2 + par)
                    dve.wait_ge(u_stored, GROUPS - 3 + par)
                    front1.link(V.tensor_tensor(U0[par][:, :, :], tiles(cols(X1, at, GW)), per_tile(LA, at), ALU.mult))
                    V.tensor_tensor(U0[par][:, :, :], U0[par][:, :, :], per_tile(LB, at), ALU.subtract).then_inc(u0_last, 1)

            copy_xT(0)
            copy_xT(1)
            states(0, 0)
            copy_xT(2)
            add_ada()
            pair(0)
            with dve.Fori(1, GROUPS // 2 - 2) as i:
                pair(i)
            pair(GROUPS // 2 - 2, next_xT=False)
            pair(GROUPS // 2 - 1, last=True)

            def repeat_parts(j, par):
                dve.wait_ge(low_done, 2 * j + 2)
                q, k = QK12[par]
                V.tensor_copy(q[:, :, 2:4, :].rearrange("p h b d -> p h (b d)"), q[:, :, 0:2, :].rearrange("p h b d -> p h (b d)"))
                V.tensor_copy(k[:, :, 1, :], k[:, :, 0, :])
                V.tensor_copy(k[:, :, 3, :], k[:, :, 2, :]).then_inc(q2_done, 1)

            hd = Chain(dve, chain_heads)

            def project(j, par):
                hd.start(j)
                for k in range(TILES):
                    dve.wait_ge(qkv_ps, TILES * j + k + 1)
                    if k == 0:
                        dve.wait_ge(v_ready, nn(j - 1))
                        dve.wait_ge(low_done, nn(2 * (j - 1)))
                    V.tensor_tensor(Tq[par][:, :, k, :], ps[:, 2 + k, 0:3 * D].rearrange("p (a d) -> p a d", a=3),
                                    bqkv[:, :].rearrange("p (a d) -> p a d", a=3), ALU.add).then_inc(t_done, 1)
                dve.wait_ge(sqt_done, TILES * (j + 1))
                dve.wait_ge(v_ready, j)
                hs, tot = HS[:, 0:NH], HS[:, NH:]
                hd.link(V.reduce_sum(hs, SQT[:, :, :, :].rearrange("p a k (h d) -> p (a k h) d", d=HD), AX.X))
                hd.link(V.reduce_sum(tot, hs.rearrange("p (a h) -> p a h", h=H), AX.X))
                V.tensor_scalar(HS[:, :], HS[:, :], EPS2, None, ALU.max).then_inc(hs_ready, 1)
                if not (isinstance(j, int) and j == 0):
                    repeat_parts(j - 1, 1 - par)
                dve.wait_ge(hr_sqrt, j + 1)
                rh, rt = HR[:, 0:NH], HR[:, NH:]
                hd.add(V.tensor_scalar(rh, rh, 1.0 / CLIP, None, ALU.mult))
                hd.link(V.tensor_scalar(rt, rt, 1.0 / CLIP, 1.0, ALU.mult, ALU.max))
                hd.link(V.tensor_scalar(rt, rt, 1.0 / BETA_UP, None, ALU.mult))
                hd.link(V.tensor_tensor(rh.rearrange("p (a h) -> p a h", h=H), rh.rearrange("p (a h) -> p a h", h=H),
                                        rt.unsqueeze(2).broadcast_to([P, 3 * TILES, H]), ALU.max))
                V.reciprocal(hs, rh).then_inc(hr_ready, 1)
                dve.wait_ge(hr_ready, j + 1)
                f = hs[:, 0:TILES * H].unsqueeze(2).broadcast_to([P, TILES * H, HD])
                V.tensor_tensor(heads(par, 0), heads(par, 0), f, ALU.mult).then_inc(f_ready, 1)

            project(0, 0)
            clip_pair(GROUPS // 2 - 1)
            project(1, 1)
            with dve.Fori(1, GROUPS // 2) as i:
                for u in range(2):
                    project(2 * i + u, u)
            q, k = QK12[1]
            dve.wait_ge(q1_done, 2 * GROUPS)
            dve.wait_ge(fk_ready, GROUPS)
            V.tensor_tensor(k[:, :, 2, :], heads(1, 1), k[:, :, 0, :], ALU.subtract).then_inc(low_last, 1)
            V.tensor_copy(k[:, :, 1, :], k[:, :, 0, :])
            dve.wait_ge(low_last, 1)
            V.tensor_copy(k[:, :, 3, :], k[:, :, 2, :])
            dve.wait_ge(low_done, 2 * GROUPS - 1)
            V.tensor_copy(q[:, :, 2:4, :].rearrange("p h b d -> p h (b d)"), q[:, :, 0:2, :].rearrange("p h b d -> p h (b d)")).then_inc(q2_done, 1)
            for k in (1, 3):
                dve.wait_ge(d_ps, NT - TILES + k + 1)
                V.tensor_copy(*d_places(GROUPS - 1, k)).then_inc(d_last, 1)

            def mask_q(n, par):
                q = QK[:, bass.ds(n, 1), 0:4, :].rearrange("p o j t -> p (o j) t")
                dve.wait_ge(s_ps, nn(2 * n - 2))
                for g in range(ROWG):
                    ins = V.tensor_scalar(QD[par][:, :, g, :], q, mask[:, g:g + 1], None, ALU.mult)
                ins.then_inc(qd_ready, 1)

            def evacuate(n, par):
                dve.wait_ge(pv_ps, n + 1)
                V.tensor_copy(OTs[par][:, :, :], ps[:, 4 + 3 * par, :].rearrange("p (j q) -> p j q", j=4)).then_inc(ot_copied, 1)

            def normal(n, par, sent):
                dve.wait_ge(o4_ps, n + 1)
                o4 = ps[:, 5 + par, :].rearrange("p (h c) -> p h c", c=32)
                V.reciprocal(rec[par][:, :], o4[:, :, HD]).then_inc(rec_done, 1)
                dve.wait_ge(rec_done, n + 1)
                dve.wait_ge(o_out[par], 16 * sent)
                V.scalar_tensor_tensor(ob[par][:, :].rearrange("p (h d) -> p h d", d=HD), o4[:, :, 0:HD], 1.0 / BETA_UP,
                                       rec[par][:, :].unsqueeze(2).broadcast_to([P, H, HD]), ALU.mult, ALU.mult).then_inc(o_norm, 1)

            dve.wait_ge(d_copied, NT - 2)
            dve.wait_ge(d_last, 2)
            mask_q(0, 0)
            mask_q(1, 1)

            def batch(i, u):
                n, par = BATCHES * i + u, u % 2
                first, last = (isinstance(i, int) and i == k for k in (0, N // BATCHES - 1))
                if not (last and u >= 2):
                    mask_q(n + 2, par)
                if not (first and u < 1):
                    evacuate(n - 1, 1 - par)
                if not (first and u < 2):
                    normal(n - 2, par, uses(i, u - 2) - 1)

            by_batches(dve, batch, 1)
            evacuate(N - 1, 1)
            normal(N - 2, 0, N // 2 - 1)
            normal(N - 1, 1, N // 2 - 1)

            def sum3(j, par, sqp, sqg, xg, done):
                dve.wait_ge(sqp, j + 1)
                dve.wait_ge(sqg, j + 1)
                dve.wait_ge(xg, j + 1)
                V.reduce_sum(R3[:, :, bass.ds(TILES * j, TILES)], SQ3[par][:, :, :, :], AX.X).then_inc(done, 1)

            def mobius(xn, n, ready):
                link, add = small.link, small.add
                link(V.tensor_scalar(row(0), R3[:, 0, :], EPS2, None, ALU.max))
                rsqrt(V, row(1), row(0), row(6), row(7), small)
                link(V.tensor_scalar(row(8), row(1), CLIP, 1.0, ALU.mult, ALU.min))
                rp = row(8)
                link(V.tensor_tensor(row(7), rp, rp, ALU.mult))
                link(V.tensor_tensor(row(2), row(7), R3[:, 1, :], ALU.mult))
                sa = row(2)
                link(V.tensor_scalar(row(3), sa, EPS2, None, ALU.max))
                rsqrt(V, row(9), row(3), row(6), row(7), small)
                V.tensor_tensor(row(4), row(3), row(9), ALU.mult).then_inc(na_ready, 1)
                dve.wait_ge(th_ready, n)
                link(V.tensor_tensor(row(10), row(5), row(9), ALU.mult))
                tau = row(10)
                add(V.tensor_tensor(row(11), tau, tau, ALU.mult))
                link(V.tensor_tensor(row(12), tau, rp, ALU.mult))
                tr = row(12)
                add(V.tensor_tensor(row(13), row(11), sa, ALU.mult))
                link(V.tensor_tensor(row(14), tr, R3[:, 2, :], ALU.mult))
                y2 = row(13)
                add(V.tensor_scalar(row(15), row(14), 2.0, 1.0, ALU.mult, ALU.add))
                link(V.tensor_tensor(row(16), xn, y2, ALU.mult))
                add(V.tensor_scalar(row(17), xn, -1.0, 1.0, ALU.mult, ALU.add))
                link(V.tensor_tensor(row(6), row(16), row(15), ALU.add))
                add(V.tensor_tensor(row(18), row(15), y2, ALU.add))
                link(V.tensor_scalar(row(7), row(6), EPS, None, ALU.max))
                link(V.reciprocal(row(6), row(7)))
                add(V.tensor_tensor(AL[:, :], row(18), row(6), ALU.mult))
                link(V.tensor_tensor(row(7), row(17), row(6), ALU.mult))
                V.tensor_tensor(BE[:, :], row(7), tr, ALU.mult).then_inc(ready, 1)
                dve.wait_ge(ready, 1)

            def after_attention(j, par):
                dve.wait_ge(wo_ps, j + 1)
                dve.wait_ge(sqp_ready, nn(j - 1))
                dve.wait_ge(ga_ready, nn(j - 1))
                V.tensor_tensor(PA[par][:, :, :], tiles(ps[:, 1 + par, :]), rows4(bo[:, :]), ALU.add).then_inc(p_done, 1)
                if not (isinstance(j, int) and j == 0):
                    sum1(j - 1, 1 - par)

            def sum1(j, par):
                dve.wait_ge(ga_ready, j + 1)
                dve.wait_ge(r3_done, nn(j - 1))
                V.tensor_tensor(SQ3[par][:, 2, :, :], tiles(cols(GA, j, GW)), tiles(cols(X1, j, GW)), ALU.mult).then_inc(xg_ready, 1)
                dve.wait_ge(xg_ready, j + 1)
                dve.wait_ge(sqg_ready, j + 1)
                V.reduce_sum(R3[:, 1:3, bass.ds(TILES * j, TILES)], SQ3[par][:, 1:3, :, :], AX.X).then_inc(r3_done, 1)

            by_pairs(dve, after_attention)
            sum1(GROUPS - 1, 1)
            dve.wait_ge(r3_done, GROUPS)
            dve.wait_ge(sqp_ready, GROUPS)
            mobius(XN[0][:, :], 1, ab_ready)

            bn3 = Chain(dve, chain_bn3)

            def new_x(j, par):
                lag = not (isinstance(j, int) and j == 0)
                if lag:
                    bn3.start(j - 1, per=2 * TILES + 1, behind=TILES)
                    combine(1 - par, bn3)
                dve.wait_ge(ax_ready, j + 1)
                dve.wait_ge(tmp_ready, j + 1)
                V.tensor_tensor(cols(X2, j, GW), cols(X2, j, GW), cols(GA, j, GW), ALU.add).then_inc(x2_done, 1)
                if lag:
                    bn3.sync()
                    keep(j - 1, bn3)
                dve.wait_ge(x2_done, j + 1)
                V.memset(carry[:, 0:1], 0.0)
                statistics(X2, j, par, bn3)

            by_pairs(dve, new_x)
            combine(1, bn3)
            bn3.sync()
            keep(GROUPS - 1, bn3)
            ln_coefficients(V, bass.ds(0, NT), NT, XN[1], small, ln_ready3)
            dve.wait_ge(ln_ready3, 1)

            def centre(j):
                dve.wait_ge(xs_done3, j + 1)
                V.tensor_tensor(tiles(cols(U3, j, GW)), tiles(cols(U3, j, GW)), per_tile(LB, j), ALU.subtract).then_inc(u0_done3, 1)

            def shift(j):
                dve.wait_ge(um_done3, j + 1)
                V.tensor_tensor(tiles(cols(U3, j, GW)), tiles(cols(U3, j, GW)), rows4(ada[:, 3 * D:4 * D]), ALU.add).then_inc(u_stored3, 1)

            def normalise(j, par):
                centre(j)
                if not (isinstance(j, int) and j == 0):
                    shift(j - 1)

            by_pairs(dve, normalise)
            shift(GROUPS - 1)
            for j in range(0, GROUPS, 2):
                dve.wait_ge(squ_done3, j + 2)
                V.reduce_sum(USS[:, TILES * j:TILES * (j + 2)], squares3(j, 2).rearrange("p (k d) -> p k d", d=D), AX.X).then_inc(uss_done3, 1)
            dve.wait_ge(uss_done3, GROUPS // 2)
            clip_factors(bass.ds(0, NT), NT, small, ru_ready3)

            def add_chunks(j, par, hf):
                dve.wait_ge(vsq_done, CHUNKS * j + 2 * hf + 2)
                at = [vsq[par][:, c * GW:(c + 1) * GW] for c in range(CHUNKS)]
                V.tensor_tensor(at[2 * hf], at[2 * hf], at[2 * hf + 1], ALU.add).then_inc(sum_half, 1)
                if hf:
                    dve.wait_ge(sum_half, 2 * j + 2)
                    V.tensor_tensor(at[0], at[0], at[2], ALU.add).then_inc(sum_done, 1)

            rvc = Chain(dve, chain_rv)

            def clip_v(j):
                dve.wait_ge(rv_sqrt, j)
                dve.wait_ge(ss_ps, j + 1)
                V.tensor_scalar(RV[:, 0, :], ps[:, 5, 0:TILES], EPS2, None, ALU.max).then_inc(rv_max, 1)

            def second(j, par):
                rvc.start(j)
                dve.wait_ge(rv_sqrt, j + 1)
                rvc.link(V.tensor_scalar(RV[:, 2, :], RV[:, 1, :], 1.0 / CLIP, 1.0, ALU.mult, ALU.max))
                rvc.link(V.reciprocal(RV[:, 4, :], RV[:, 2, :]))
                dve.wait_ge(f2_ps, TILES * (j + 1))
                for k in range(TILES):
                    ins = V.scalar_tensor_tensor(PA[par][:, k, :], ps[:, 6 + par, k * D:(k + 1) * D], RV[:, 4, k:k + 1], b2[:, :],
                                                 ALU.mult, ALU.add)
                ins.then_inc(p2_done, 1)

            def sum2(j, par):
                sum3(j, par, sqp2_ready, sqg2_ready, xg2_ready, r32_done)

            def hidden(j, par):
                lag, lag2 = (not (isinstance(j, int) and j < n) for n in (1, 2))
                if lag:
                    clip_v(j - 1)
                add_chunks(j, par, 0)
                if lag:
                    second(j - 1, 1 - par)
                add_chunks(j, par, 1)
                if lag2:
                    sum2(j - 2, par)

            by_pairs(dve, hidden)
            clip_v(GROUPS - 1)
            sum2(GROUPS - 2, 0)
            second(GROUPS - 1, 1)
            sum2(GROUPS - 1, 1)
            dve.wait_ge(r32_done, GROUPS)
            mobius(XN[1][:, :], 2, ab2_ready)

            def add_x1(j):
                dve.wait_ge(ax2_ready, j + 1)
                V.tensor_tensor(cols(X2, j, GW), cols(X2, j, GW), cols(X1, j, GW), ALU.add).then_inc(x1x2_done, 1)

            def add_update(j):
                dve.wait_ge(tmp2_ready, j + 1)
                dve.wait_ge(x1x2_done, j + 1)
                V.tensor_tensor(cols(X2, j, GW), cols(X2, j, GW), cols(GA, j, GW), ALU.add).then_inc(y_done, 1)

            def final(j, par):
                add_x1(j)
                if not (isinstance(j, int) and j == 0):
                    add_update(j - 1)

            by_pairs(dve, final)
            add_update(GROUPS - 1)

        @block.tensor
        def _(pe):
            mm = nc.tensor.matmul
            turn = nc.tensor.transpose

            def x_transpose(j, par, k):
                first = isinstance(j, int) and j == 0
                if k == 0:
                    if first:
                        pe.wait_ge(x_in[0], 64)
                    else:
                        pe.wait_ge(x_copied, j)
                    pe.wait_ge(xT_copied, j)
                src = X1[:, k * D:(k + 1) * D] if first else x_st[par][:, k, :]
                ins = turn(ps[:, 4, k * P:(k + 1) * P], src, ident[:, :])
                if k == TILES - 1:
                    ins.then_inc(xT_ps, 1)

            def x_transposes(j, par):
                for k in range(TILES):
                    x_transpose(j, par, k)

            def x_product(j, par, k):
                if k == 0:
                    pe.wait_ge(xT_copied, j + 1)
                ins = mm(ps[:, par, k * P:(k + 1) * P], wx_sb[:, :], xT_sb[:, k * P:(k + 1) * P], start=False, stop=False, skip_group_check=True)
                if k == TILES - 1:
                    ins.then_inc(xw_ready, 1)

            def bias(par, k):
                mm(ps[:, par, k * P:(k + 1) * P], b_row[:, :], ones_row[:, :], start=k == 0, stop=False, skip_group_check=True)

            def rnn_step(i, s, par):
                pe.wait_ge(h_ready, STEPS * i + s + 1)
                rhs = hsT[:, (s - 1) * N:s * N] if s else (hsT[:, (STEPS - 1) * N:] if not (isinstance(i, int) and i == 0) else h0T[:, :])
                for c in range(0, D, 32):
                    ins = mm(ps[c:c + 32, par, s * N:(s + 1) * N], wh_sb[:, c:c + 32], rhs, start=False, stop=s == STEPS - 1,
                             skip_group_check=True)
                ins.then_inc(rnn_mm, 1)

            def h_transpose(i, par, k):
                if k == 0:
                    pe.wait_ge(x1_added, nn(i - 1))
                ins = turn(ps[:, 2 + par, k * P:(k + 1) * P], hsT[:, k * P:(k + 1) * P], ident[:, :])
                if k == TILES - 1:
                    ins.then_inc(hT_ready, 1)

            pe.wait_ge(pool_const, 5)
            pe.wait_ge(pool_chain, 3)
            x_transposes(0, 0)
            pe.wait_ge(rnn_w, 64)
            turn(ps[:, 2, 0:N], cond_sb[:, :], ident[0:N, 0:N]).then_inc(condT_ps, 1)
            for k in range(TILES):
                bias(0, k)
            for k in range(TILES):
                x_product(0, 0, k)

            def ada_piece(n):
                if n == 0:
                    pe.wait_ge(all_w, (13 + CHUNKS) * 16)
                    pe.wait_ge(cond_ready, 1)
                ins = mm(ps[:, 5 + n // 3, (n % 3) * D:(n % 3 + 1) * D], cond4[:, :, :].rearrange("p s n -> p (s n)"),
                         wada_sb[:, n * D:(n + 1) * D], start=True, stop=True)
                if n % 3 == 2:
                    ins.then_inc(ada_ps, 1)

            def group(i, par, last=False):
                ada_at = {0: {9: 0, 11: 1}, 1: {4: 2, 8: 3, 10: 4, 13: 5}}.get(i, {}) if isinstance(i, int) else {}
                x_at, bias_at, product_at = {1: 0, 2: 1, 3: 2, 5: 3}, {6: 0, 7: 1, 9: 2, 10: 3}, {11: 0, 13: 1, 14: 2, 15: 3}
                first = isinstance(i, int) and i == 0
                for s in range(STEPS):
                    rnn_step(i, s, par)
                    if s == 0 and not first:
                        h_transpose(i - 1, 1 - par, TILES - 1)
                    if s % TS == 0 and s:
                        h_transpose(i, par, s // TS - 1)
                    if s in x_at and not last:
                        x_transpose(i + 1, 1 - par, x_at[s])
                    if s in bias_at and not last:
                        bias(1 - par, bias_at[s])
                    if s in product_at and not last:
                        x_product(i + 1, 1 - par, product_at[s])
                    if s in ada_at:
                        ada_piece(ada_at[s])

            group(0, 0)
            group(1, 1)
            with pe.Fori(1, GROUPS // 2 - 1) as i:
                for u in range(2):
                    group(2 * i + u, u)
            group(GROUPS - 2, 0)
            group(GROUPS - 1, 1, last=True)
            pe.wait_ge(h_ready, STEPS * GROUPS + 1)
            h_transpose(GROUPS - 1, 1, TILES - 1)

            def u_transposes(j, par, bank, ready, copied, copies, done):
                pe.wait_ge(ready, j + 1)
                pe.wait_ge(copied, nn(copies))
                for k in range(TILES):
                    ins = turn(ps[:, bank, k * P:(k + 1) * P], UP[par][:, k, :], ident[:, :])
                ins.then_inc(done, 1)

            def split_transposes(j, k, parity, copied=None, count=None):
                if k == 0:
                    pe.wait_ge(q2_done, j + 1)
                if copied is None:
                    pe.wait_ge(d_copied, nn(TILES * j + k - 1))
                else:
                    pe.wait_ge(copied, count)
                dst = ps[:, 6 + k % 2, :].bitcast(F16)
                for g in range(8):
                    h0 = H * k + 4 * (g % 4)
                    src = QK12[parity][g // 4][:, h0:h0 + 4, :, :].rearrange("p h b d -> p (h b d)")
                    ins = turn(dst[:, g * P:(g + 1) * P], src, ident16[:, :])
                ins.then_inc(d_ps, 1)

            def products(j, par, at):
                pe.wait_ge(uT_copied, j + 1)
                for k in at:
                    pe.wait_ge(t_done, nn(TILES * (j - 1) + k + 1))
                    mm(ps[:, 2 + k, 0:3 * D], uT[par][:, k * P:(k + 1) * P], wqkv_sb[:, :], start=True, stop=True).then_inc(qkv_ps, 1)

            def project(j, par, last=0):
                lag, lag2 = (not (isinstance(j, int) and j < n) for n in (1, 2))
                for k in range(2):
                    if lag2:
                        split_transposes(j - 2, 2 + k, par)
                if last < 2:
                    products(j + 1, 1 - par, (0, 1))
                for k in range(2):
                    if lag:
                        split_transposes(j - 1, k, 1 - par)
                if last < 2:
                    products(j + 1, 1 - par, (2, 3))
                if not last:
                    u_transposes(j + 2, par, par, up_ready, uT_copied, j + 1, uT_ps)

            for u in range(2):
                u_transposes(u, u, u, up_ready, uT_copied, 0, uT_ps)
            pe.wait_ge(x1_added, GROUPS)
            products(0, 0, range(TILES))
            project(0, 0)
            project(1, 1)
            with pe.Fori(1, GROUPS // 2 - 1) as i:
                for u in range(2):
                    project(2 * i + u, u)
            project(GROUPS - 2, 0, last=1)
            project(GROUPS - 1, 1, last=2)
            for k in range(2):
                split_transposes(GROUPS - 2, 2 + k, 0)
            for k in range(3):
                split_transposes(GROUPS - 1, k, 1)
            split_transposes(GROUPS - 1, 3, 1, copied=d_last, count=1)
            pe.wait_ge(d_copied, NT - 2)
            pe.wait_ge(d_last, 2)
            pe.wait_ge(t_done, NT)

            def scores(n, par, hf):
                if hf == 0:
                    pe.wait_ge(qd_ready, n + 1)
                pe.wait_ge(p_ready, nn(2 * n + hf - 1))
                for j in (2 * hf, 2 * hf + 1):
                    ins = mm(ps[:, j, :], QK[:, bass.ds(n, 1), 4 + j, :].rearrange("p o t -> p (o t)"), QD[par][:, j, :, :].rearrange("p g q -> p (g q)"), start=True, stop=True)
                ins.then_inc(s_ps, 1)

            def weighted(n, par, hf, loads):
                if hf == 0:
                    pe.wait_ge(v_in[par], 16 * loads)
                    pe.wait_ge(ot_copied, nn(n - 1))
                pe.wait_ge(p_ready, 2 * n + hf + 1)
                for j in (2 * hf, 2 * hf + 1):
                    for g in range(ROWG):
                        h = 4 * j + g
                        ins = mm(ps[32 * g:32 * g + 32, 4 + 3 * par, j * T:(j + 1) * T], Vb[par][:, VW * h:VW * h + 32],
                                 Pb[par][:, j, g, :], start=True, stop=True)
                if hf == 1:
                    ins.then_inc(pv_ps, 1)

            def back(n, par):
                pe.wait_ge(ot_copied, n + 1)
                pe.wait_ge(o_norm, nn(n - 1))
                for j in range(4):
                    ins = turn(ps[:, 5 + par, j * P:(j + 1) * P], OTs[par][:, j, :], ident[:, :])
                ins.then_inc(o4_ps, 1)

            def batch(i, u):
                n, par = BATCHES * i + u, u % 2
                first = isinstance(i, int) and i == 0
                for hf in range(2):
                    scores(n, par, hf)
                    if not (first and u < 1):
                        weighted(n - 1, 1 - par, hf, uses(i, u - 1))
                if not (first and u < 2):
                    back(n - 2, par)

            by_batches(pe, batch, 1)
            for hf in range(2):
                weighted(N - 1, 1, hf, N // 2)
            back(N - 2, 0)
            back(N - 1, 1)

            def o_transposes(j, par):
                pair = j // 2
                pe.wait_ge(o_in[pair % 2], 64 * (pair // 2 + 1))
                pe.wait_ge(oT_copied, nn(j - 1))
                for k in range(TILES):
                    at = TILES * par + k
                    ins = turn(ps[:, 3 * par, k * P:(k + 1) * P], o_ld[pair % 2][:, at * D:(at + 1) * D], ident[:, :])
                ins.then_inc(oT_ps, 1)

            def o_products(j, par):
                pe.wait_ge(oT_copied, j + 1)
                pe.wait_ge(p_done, nn(j - 1))
                for k in range(TILES):
                    ins = mm(ps[:, 1 + par, k * D:(k + 1) * D], oT[par][:, k * P:(k + 1) * P], wo_sb[:, :], start=True, stop=True)
                ins.then_inc(wo_ps, 1)

            o_transposes(0, 0)
            for j in range(GROUPS):
                if j < GROUPS - 1:
                    o_transposes(j + 1, 1 - j % 2)
                o_products(j, j % 2)
            pe.wait_ge(p_done, GROUPS)

            def f1(j, par, c):
                if c == 0:
                    pe.wait_ge(uT_copied3, j + 1)
                pe.wait_ge(vT_copied, nn(CHUNKS * (j - 1) + c + 1))
                mm(ps[:, 1 + c, :], w1_sb[:, c * P:(c + 1) * P], uT[par][:, :], start=True, stop=True).then_inc(f1_ps, 1)

            def f2(j, par, k):
                if k == 0:
                    pe.wait_ge(vT_copied, CHUNKS * (j + 1))
                    pe.wait_ge(p2_done, nn(j - 1))
                for c in range(CHUNKS):
                    ins = mm(ps[:, 6 + par, k * D:(k + 1) * D], vT[par][:, c * GW + k * P:c * GW + (k + 1) * P], w2_sb[:, c, :],
                             start=c == 0, stop=c == CHUNKS - 1)
                ins.then_inc(f2_ps, 1)

            def squared_norms(j, par):
                pe.wait_ge(sum_done, j + 1)
                pe.wait_ge(rv_max, j)
                for k in range(TILES):
                    ins = mm(ps[:, 5, k:k + 1], vsq[par][:, k * P:(k + 1) * P], ones[:, :], start=True, stop=True)
                ins.then_inc(ss_ps, 1)

            def hidden(j, par, last=0):
                for c in range(CHUNKS - 1):
                    if last < 2:
                        f1(j + 1, 1 - par, c)
                f2(j, par, 0)
                if last < 2:
                    f1(j + 1, 1 - par, CHUNKS - 1)
                f2(j, par, 1)
                if not last:
                    u_transposes(j + 2, par, 0, up_ready3, uT_copied3, j + 2, uT_ps3)
                for k in range(2, TILES):
                    f2(j, par, k)
                squared_norms(j, par)

            u_transposes(0, 0, 0, up_ready3, uT_copied3, 0, uT_ps3)
            for c in range(CHUNKS):
                f1(0, 0, c)
            u_transposes(1, 1, 0, up_ready3, uT_copied3, 1, uT_ps3)
            hidden(0, 0)
            hidden(1, 1)
            with pe.Fori(1, GROUPS // 2 - 1) as i:
                for u in range(2):
                    hidden(2 * i + u, u)
            hidden(GROUPS - 2, 0, last=1)
            hidden(GROUPS - 1, 1, last=2)
_INS = ['x', 'cond_1024', 'L0_cond_Wx', 'L0_cond_Wh', 'L0_cond_b', 'L1_cond_w_q', 'L1_cond_b_q', 'L1_cond_w_k',
        'L1_cond_b_k', 'L1_cond_w_v', 'L1_cond_b_v', 'L1_cond_w_o', 'L1_cond_b_o', 'L1_cond_w_f1', 'L1_cond_b_f1',
        'L1_cond_w_f2', 'L1_cond_b_f2', 'L1_cond_w_ada', 'L1_cond_b_ada']


def kernel(**inputs):
    import numpy as _np
    import concourse.bacc as _bacc
    from concourse import mybir as _mybir
    from concourse.bass_utils import run_bass_kernel_spmd as _run

    nc = _bacc.Bacc("TRN2", target_bir_lowering=False, num_devices=1)
    arrays, args = {}, []
    for name in _INS:
        a = _np.ascontiguousarray(inputs[name])
        arrays[f"in_{name}_dram"] = a
        args.append(nc.dram_tensor(f"in_{name}_dram", a.shape, _mybir.dt.from_np(a.dtype), kind="ExternalInput").ap())
    args.append(nc.dram_tensor("out_0_dram", (N, T, D), F32, kind="ExternalOutput").ap())
    build(nc, *args)
    r = _run(nc, [arrays], core_ids=[0])
    return r.results[0]["out_0_dram"]
```
